# Optimizing a Trainium2 kernel written in Bass

```python
import numpy as np
import jax
import jax.numpy as jnp

def _softmax(x, axis=-1):
    return jax.nn.softmax(x, axis=axis)

def _gelu(x):
    return jax.nn.gelu(x, approximate=True)

def _silu(x):
    return jax.nn.silu(x)

def _sigmoid(x):
    return jax.nn.sigmoid(x)

def _layernorm(x, axis=-1, eps=1e-05):
    m = jnp.mean(x, axis=axis, keepdims=True)
    v = jnp.var(x, axis=axis, keepdims=True)
    return (x - m) / jnp.sqrt(v + eps)

def _scatter_add(tgt, idx, src, axis=0):
    return tgt.at[idx].add(src)

def _segment_sum(src, seg, n):
    return jax.ops.segment_sum(src, seg, n)
kernel_name = 'mk_xattn_ffn_d4_seqx_r8_519a21'

def setup_inputs(seed: int=0):
    np.random.seed(seed)
    _w = jnp.asarray

    def _rec_inputs():
        import jax
        import jax.numpy as jnp
        _rk = jax.random.key(seed)
        x = -0.0005207 + 1.001 * jax.random.normal(jax.random.fold_in(_rk, 1), (32, 64, 128), jnp.float32)
        _lenS = 64 - jax.random.randint(jax.random.fold_in(_rk, 7), (32,), 0, max(1, 64 // 4) + 1, jnp.int32)
        _lenS2 = 64 - jax.random.randint(jax.random.fold_in(_rk, 8), (32,), 0, max(1, 64 // 4) + 1, jnp.int32)
        _ctx_1024P = jax.random.normal(jax.random.fold_in(_rk, 11), (32, 16, 128), jnp.float32)
        _ctx_1024c = jax.random.dirichlet(jax.random.fold_in(_rk, 511), 0.3 * jnp.ones((16,), jnp.float32), (32, 64))
        _ctx_1024t = jnp.einsum('bsk,bkd->bsd', _ctx_1024c, _ctx_1024P)
        _ctx_1024t = _ctx_1024t * jax.lax.rsqrt(jnp.mean(jnp.square(_ctx_1024t)) + 1e-12) * 0.953939
        ctx_1024 = -0.000514642 + 1.00011 * (_ctx_1024t + 0.3 * jax.random.normal(jax.random.fold_in(_rk, 611), (32, 64, 128), jnp.float32))
        itok_SxS2_0_2016 = jax.random.randint(jax.random.fold_in(_rk, 12), (64, 64), 0, 2017, jnp.int32)
        return (x, ctx_1024, itok_SxS2_0_2016)
    x, ctx_1024, itok_SxS2_0_2016 = _rec_inputs()

    def _L0_xattn_setup():
        import jax, jax.numpy as jnp
        import numpy as np
        EMBED_DIM = 128
        NUM_HEADS = 16
        HEAD_DIM = EMBED_DIM // NUM_HEADS
        WINDOW = 64

        def apply_rope(x):
            B, H, S, d = x.shape
            half = d // 2
            pos = jnp.arange(S, dtype=x.dtype)
            freqs = 1.0 / 10000.0 ** (jnp.arange(half, dtype=x.dtype) / half)
            ang = pos[:, None] * freqs[None, :]
            cos, sin = (jnp.cos(ang), jnp.sin(ang))
            x1, x2 = (x[..., :half], x[..., half:])
            return jnp.concatenate([x1 * cos - x2 * sin, x1 * sin + x2 * cos], axis=-1)

        def _forward(query, key, value, q_w, q_b, k_w, k_b, v_w, v_b, o_w, o_b):
            B, S_q, D = query.shape
            S_k = key.shape[1]
            H, d, W = (NUM_HEADS, HEAD_DIM, WINDOW)
            q = (query @ q_w.T + q_b).reshape(B, S_q, H, d).transpose(0, 2, 1, 3)
            k = (key @ k_w.T + k_b).reshape(B, S_k, H, d).transpose(0, 2, 1, 3)
            v = (value @ v_w.T + v_b).reshape(B, S_k, H, d).transpose(0, 2, 1, 3)
            q = apply_rope(q) * d ** (-0.5)
            k = apply_rope(k)
            q_pos = jnp.arange(S_q)[:, None]
            offsets = jnp.arange(-W, 1)[None, :]
            idx = q_pos + offsets
            local_mask = (idx < 0) | (idx >= S_k)
            gidx = jnp.clip(idx, 0, S_k - 1)
            k_win = k[:, :, gidx, :]
            v_win = v[:, :, gidx, :]
            scores = jnp.einsum('bhqd,bhqwd->bhqw', q, k_win)
            mask = local_mask[None, None, :, :]
            scores = jnp.where(mask, -jnp.inf, scores)
            m = jnp.max(scores, axis=-1, keepdims=True)
            m = jnp.where(jnp.isfinite(m), m, 0.0)
            e = jnp.exp(scores - m)
            denom = jnp.sum(e, axis=-1, keepdims=True)
            probs = jnp.where(denom > 0, e / jnp.where(denom > 0, denom, 1.0), 0.0)
            ctx = jnp.einsum('bhqw,bhqwd->bhqd', probs, v_win)
            ctx = ctx.transpose(0, 2, 1, 3).reshape(B, S_q, D)
            return ctx @ o_w.T + o_b
        key = jax.random.key(seed)
        ks = jax.random.split(key, 12)
        B, S, D = (1, 256, EMBED_DIM)
        scale = 1.0 / np.sqrt(D)
        inp = {'query': jax.random.normal(ks[0], (B, S, D), jnp.float32), 'key': jax.random.normal(ks[1], (B, S, D), jnp.float32), 'value': jax.random.normal(ks[2], (B, S, D), jnp.float32), 'q_w': jax.random.normal(ks[3], (D, D), jnp.float32) * scale, 'q_b': jax.random.normal(ks[4], (D,), jnp.float32) * 0.01, 'k_w': jax.random.normal(ks[5], (D, D), jnp.float32) * scale, 'k_b': jax.random.normal(ks[6], (D,), jnp.float32) * 0.01, 'v_w': jax.random.normal(ks[7], (D, D), jnp.float32) * scale, 'v_b': jax.random.normal(ks[8], (D,), jnp.float32) * 0.01, 'o_w': jax.random.normal(ks[9], (D, D), jnp.float32) * scale, 'o_b': jax.random.normal(ks[10], (D,), jnp.float32) * 0.01}
        return inp
    _L0_xattn_all = _L0_xattn_setup()
    _L0_xattn_in = {k: v for k, v in _L0_xattn_all.items() if k in ('q_w', 'q_b', 'k_w', 'k_b', 'v_w', 'v_b', 'o_w', 'o_b')}
    del _L0_xattn_all

    def _L0_ffn_setup():
        import jax, jax.numpy as jnp
        import numpy as np
        N_EXPERTS = 8
        CAP_FACTOR = 1.25
        BATCH, SEQ, DMODEL, DFF = (4, 256, 128, 512)
        key = jax.random.key(seed)
        k0, k1, k2, k3 = jax.random.split(key, 4)
        x = jax.random.normal(k0, (BATCH, SEQ, DMODEL), dtype=jnp.float32)
        Wr = jax.random.normal(k1, (DMODEL, N_EXPERTS), dtype=jnp.float32) * 0.02
        W1 = jax.random.normal(k2, (N_EXPERTS, DMODEL, DFF), dtype=jnp.float32) * 0.02
        W2 = jax.random.normal(k3, (N_EXPERTS, DFF, DMODEL), dtype=jnp.float32) * 0.02
        return {'x': x, 'Wr': Wr, 'W1': W1, 'W2': W2}
    _L0_ffn_all = _L0_ffn_setup()
    _L0_ffn_in = {k: v for k, v in _L0_ffn_all.items() if k in ('Wr', 'W1', 'W2')}
    del _L0_ffn_all

    def _L1_xattn_setup():
        import jax, jax.numpy as jnp
        import numpy as np
        D_MODEL = 128
        NUM_HEADS = 16
        D_K = D_MODEL // NUM_HEADS

        def _split_heads(x):
            B, S, _ = x.shape
            return x.reshape(B, S, NUM_HEADS, D_K).transpose(0, 2, 1, 3)
        key = jax.random.key(seed)
        ks = jax.random.split(key, 11)
        B, S, D = (2, 256, D_MODEL)
        scale = 1.0 / np.sqrt(D)
        inp = {'queries': jax.random.normal(ks[0], (B, S, D), jnp.float32), 'keys': jax.random.normal(ks[1], (B, S, D), jnp.float32), 'values': jax.random.normal(ks[2], (B, S, D), jnp.float32), 'w_q': jax.random.normal(ks[3], (D, D), jnp.float32) * scale, 'b_q': jnp.zeros((D,), jnp.float32), 'w_k': jax.random.normal(ks[4], (D, D), jnp.float32) * scale, 'b_k': jnp.zeros((D,), jnp.float32), 'w_v': jax.random.normal(ks[5], (D, D), jnp.float32) * scale, 'b_v': jnp.zeros((D,), jnp.float32), 'w_o': jax.random.normal(ks[6], (D, D), jnp.float32) * scale, 'b_o': jnp.zeros((D,), jnp.float32)}
        return inp
    _L1_xattn_all = _L1_xattn_setup()
    _L1_xattn_in = {k: v for k, v in _L1_xattn_all.items() if k in ('w_q', 'b_q', 'w_k', 'b_k', 'w_v', 'b_v', 'w_o', 'b_o')}
    del _L1_xattn_all

    def _L1_ffn_setup():
        import math
        import jax, jax.numpy as jnp
        import numpy as np
        D_MODEL = 128
        D_FF = 512
        E = 8
        K = 2
        CF = 1.25
        CLAMP = 10000.0
        key = jax.random.key(seed)
        k0, k1, k2, k3 = jax.random.split(key, 4)
        B, S = (4, 256)
        x = jax.random.normal(k0, (B, S, D_MODEL), dtype=jnp.float32)
        ln_gamma = jnp.ones((D_MODEL,), jnp.float32)
        ln_beta = jnp.zeros((D_MODEL,), jnp.float32)
        rb = 0.02 * math.sqrt(3.0)
        Wr = jax.random.uniform(k1, (E, D_MODEL), jnp.float32, -rb, rb)
        b12 = math.sqrt(6.0 / (D_MODEL + 2 * D_FF))
        W12 = jax.random.uniform(k2, (E, 2 * D_FF, D_MODEL), jnp.float32, -b12, b12)
        b3 = math.sqrt(6.0 / (D_FF + D_MODEL))
        W3 = jax.random.uniform(k3, (E, D_MODEL, D_FF), jnp.float32, -b3, b3)
        return {'x': x, 'ln_gamma': ln_gamma, 'ln_beta': ln_beta, 'Wr': Wr, 'W12': W12, 'W3': W3}
    _L1_ffn_all = _L1_ffn_setup()
    _L1_ffn_in = {k: v for k, v in _L1_ffn_all.items() if k in ('ln_gamma', 'ln_beta', 'Wr', 'W12', 'W3')}
    del _L1_ffn_all

    def _L2_xattn_setup():
        import jax, jax.numpy as jnp
        import numpy as np
        B, S, DIM, NH = (32, 64, 128, 8)
        DH = DIM // NH
        EPS = 1e-06
        LN_EPS = 1e-05

        def _make_hops(n):
            hops = np.zeros((n, n), dtype=np.int64)
            cur = 1
            for i in range(n):
                for j in range(i + 1, n):
                    hops[i, j] = cur
                    hops[j, i] = cur
                    cur += 1
            return (hops, cur)

        def _mlstm_forward(q, k, v, igate_w, igate_b, fgate_w, fgate_b, rpe, ln_w, ln_b, hops):
            Bq, Sq, _ = q.shape
            pos_emb = rpe[hops]
            gate_in = jnp.concatenate([q, k, v], axis=-1)
            ig = gate_in @ igate_w.T + igate_b
            fg = gate_in @ fgate_w.T + fgate_b
            ig = jnp.transpose(ig, (0, 2, 1))
            fg = jnp.transpose(fg, (0, 2, 1))
            qh = q.reshape(Bq, Sq, NH, DH).transpose(0, 2, 1, 3)
            kh = k.reshape(Bq, Sq, NH, DH).transpose(0, 2, 1, 3)
            vh = v.reshape(Bq, Sq, NH, DH).transpose(0, 2, 1, 3)
            log_f = jax.nn.log_sigmoid(fg)
            csum = jnp.cumsum(log_f, axis=-1)
            csum = jnp.concatenate([jnp.zeros((Bq, NH, 1), csum.dtype), csum], axis=-1)
            lfm = csum[:, :, :, None] - csum[:, :, None, :]
            ltr = jnp.tril(jnp.ones((Sq, Sq), dtype=bool))
            log_fg_matrix = jnp.where(ltr, lfm[:, :, 1:, 1:], -jnp.inf)
            log_D = log_fg_matrix + ig[:, :, None, :]
            max_log_D = jnp.max(log_D, axis=-1, keepdims=True)
            D = jnp.exp(log_D - max_log_D)
            k_scaled = kh / np.sqrt(DH).astype(np.float32)
            pe = pos_emb.reshape(Sq, Sq, NH, DH)
            k_hop = jnp.einsum('bhvc,vmhc->bhvm', qh, pe)
            qk = jnp.einsum('bhsd,bhtd->bhst', qh, k_scaled)
            C = (qk + k_hop) * D
            normalizer = jnp.maximum(jnp.abs(jnp.sum(C, axis=-1, keepdims=True)), jnp.exp(-max_log_D))
            Cn = C / (normalizer + EPS)
            h = Cn @ vh
            mu = jnp.mean(h, axis=-1, keepdims=True)
            var = jnp.mean(jnp.square(h - mu), axis=-1, keepdims=True)
            hn = (h - mu) / jnp.sqrt(var + LN_EPS)
            w = (1.0 + ln_w).reshape(NH, DH)
            b = ln_b.reshape(NH, DH)
            hn = hn * w[None, :, None, :] + b[None, :, None, :]
            return hn.transpose(0, 2, 1, 3).reshape(Bq, Sq, DIM)
        key = jax.random.key(seed)
        ks = jax.random.split(key, 8)
        hops_np, curnum = _make_hops(S)
        return {'q': jax.random.normal(ks[0], (B, S, DIM), dtype=jnp.float32), 'k': jax.random.normal(ks[1], (B, S, DIM), dtype=jnp.float32), 'v': jax.random.normal(ks[2], (B, S, DIM), dtype=jnp.float32), 'igate_w': jax.random.normal(ks[3], (NH, 3 * DIM), dtype=jnp.float32) * 0.02, 'igate_b': jax.random.normal(ks[4], (NH,), dtype=jnp.float32) * 0.1, 'fgate_w': jax.random.normal(ks[5], (NH, 3 * DIM), dtype=jnp.float32) * 0.02, 'fgate_b': jnp.linspace(3.0, 6.0, NH, dtype=jnp.float32), 'rpe': jax.random.normal(ks[6], (curnum, DIM), dtype=jnp.float32) * 0.02, 'ln_w': jax.random.normal(ks[7], (DIM,), dtype=jnp.float32) * 0.1, 'ln_b': jnp.zeros((DIM,), dtype=jnp.float32), 'hops': jnp.asarray(hops_np)}
    _L2_xattn_all = _L2_xattn_setup()
    _L2_xattn_in = {k: v for k, v in _L2_xattn_all.items() if k in ('igate_w', 'igate_b', 'fgate_w', 'fgate_b', 'rpe', 'ln_w', 'ln_b')}
    del _L2_xattn_all

    def _L2_ffn_setup():
        import jax, jax.numpy as jnp
        import numpy as np
        B, S, D = (4, 256, 128)
        E, H, TOP_K = (8, 256, 2)
        key = jax.random.key(seed)
        k_x, k_g, k_w1, k_w2, k_w3 = jax.random.split(key, 5)
        s_d = 1.0 / np.sqrt(D)
        s_h = 1.0 / np.sqrt(H)
        return {'x': jax.random.normal(k_x, (B, S, D), dtype=jnp.float32), 'w_gate': jax.random.normal(k_g, (D, E), dtype=jnp.float32) * s_d, 'w1': jax.random.normal(k_w1, (E, D, H), dtype=jnp.float32) * s_d, 'w3': jax.random.normal(k_w3, (E, D, H), dtype=jnp.float32) * s_d, 'w2': jax.random.normal(k_w2, (E, H, D), dtype=jnp.float32) * s_h}
    _L2_ffn_all = _L2_ffn_setup()
    _L2_ffn_in = {k: v for k, v in _L2_ffn_all.items() if k in ('w_gate', 'w1', 'w3', 'w2')}
    del _L2_ffn_all

    def _L3_xattn_setup():
        import jax, jax.numpy as jnp
        import numpy as np
        B, S, D, H = (4, 256, 128, 16)
        DH = D // H
        key = jax.random.key(seed)
        ks = jax.random.split(key, 11)
        s = 0.02
        return {'query': jax.random.normal(ks[0], (B, S, D), jnp.float32), 'key': jax.random.normal(ks[1], (B, S, D), jnp.float32), 'value': jax.random.normal(ks[2], (B, S, D), jnp.float32), 'Wq': jax.random.normal(ks[3], (D, D), jnp.float32) * s, 'bq': jnp.zeros((D,), jnp.float32), 'Wk': jax.random.normal(ks[4], (D, D), jnp.float32) * s, 'bk': jnp.zeros((D,), jnp.float32), 'Wv': jax.random.normal(ks[5], (D, D), jnp.float32) * s, 'bv': jnp.zeros((D,), jnp.float32), 'Wo': jax.random.normal(ks[6], (D, D), jnp.float32) * s, 'bo': jnp.zeros((D,), jnp.float32)}
    _L3_xattn_all = _L3_xattn_setup()
    _L3_xattn_in = {k: v for k, v in _L3_xattn_all.items() if k in ('Wq', 'bq', 'Wk', 'bk', 'Wv', 'bv', 'Wo', 'bo')}
    del _L3_xattn_all

    def _L3_ffn_setup():
        import jax, jax.numpy as jnp
        import numpy as np
        E = 16
        G = 4
        EPG = E // G
        K = 4
        TOPK_GROUP = 2
        PER_GROUP_K = K // TOPK_GROUP

        def _route(xf, router_w, correction_bias):
            S = xf.shape[0]
            logits = xf @ router_w.T
            scores = jax.nn.sigmoid(logits)
            sb = scores + correction_bias
            grp_top = jax.lax.top_k(sb.reshape(S, G, EPG), PER_GROUP_K)[0]
            group_scores = grp_top.sum(axis=-1)
            _, group_idx = jax.lax.top_k(group_scores, TOPK_GROUP)
            group_mask = jnp.zeros((S, G), sb.dtype).at[jnp.arange(S)[:, None], group_idx].set(1.0)
            score_mask = jnp.broadcast_to(group_mask[:, :, None], (S, G, EPG)).reshape(S, E)
            masked = jnp.where(score_mask > 0, sb, -jnp.inf)
            _, topk_idx = jax.lax.top_k(masked, K)
            w = jnp.take_along_axis(scores, topk_idx, axis=1)
            w = w / (w.sum(axis=-1, keepdims=True) + 1e-20)
            return (topk_idx, w, scores)
        key = jax.random.key(seed)
        ks = jax.random.split(key, 9)
        B, T, C, H, HS = (2, 128, 128, 32, 256)
        std = 0.02
        return {'x': jax.random.normal(ks[0], (B, T, C), jnp.float32), 'router_w': jax.random.normal(ks[1], (E, C), jnp.float32) * std, 'correction_bias': jnp.zeros((E,), jnp.float32), 'gate_w': jax.random.normal(ks[2], (E, C, H), jnp.float32) * std, 'up_w': jax.random.normal(ks[3], (E, C, H), jnp.float32) * std, 'down_w': jax.random.normal(ks[4], (E, H, C), jnp.float32) * std, 'shared_gate_w': jax.random.normal(ks[5], (HS, C), jnp.float32) * std, 'shared_up_w': jax.random.normal(ks[6], (HS, C), jnp.float32) * std, 'shared_down_w': jax.random.normal(ks[7], (C, HS), jnp.float32) * std}
    _L3_ffn_all = _L3_ffn_setup()
    _L3_ffn_in = {k: v for k, v in _L3_ffn_all.items() if k in ('router_w', 'correction_bias', 'gate_w', 'up_w', 'down_w', 'shared_gate_w', 'shared_up_w', 'shared_down_w')}
    del _L3_ffn_all
    return {'x': x, 'ctx_1024': ctx_1024, 'itok_SxS2_0_2016': itok_SxS2_0_2016, 'L0_xattn_q_w': _L0_xattn_in['q_w'], 'L0_xattn_q_b': _L0_xattn_in['q_b'], 'L0_xattn_k_w': _L0_xattn_in['k_w'], 'L0_xattn_k_b': _L0_xattn_in['k_b'], 'L0_xattn_v_w': _L0_xattn_in['v_w'], 'L0_xattn_v_b': _L0_xattn_in['v_b'], 'L0_xattn_o_w': _L0_xattn_in['o_w'], 'L0_xattn_o_b': _L0_xattn_in['o_b'], 'L0_ffn_Wr': _L0_ffn_in['Wr'], 'L0_ffn_W1': _L0_ffn_in['W1'], 'L0_ffn_W2': _L0_ffn_in['W2'], 'L1_xattn_w_q': _L1_xattn_in['w_q'], 'L1_xattn_b_q': _L1_xattn_in['b_q'], 'L1_xattn_w_k': _L1_xattn_in['w_k'], 'L1_xattn_b_k': _L1_xattn_in['b_k'], 'L1_xattn_w_v': _L1_xattn_in['w_v'], 'L1_xattn_b_v': _L1_xattn_in['b_v'], 'L1_xattn_w_o': _L1_xattn_in['w_o'], 'L1_xattn_b_o': _L1_xattn_in['b_o'], 'L1_ffn_ln_gamma': _L1_ffn_in['ln_gamma'], 'L1_ffn_ln_beta': _L1_ffn_in['ln_beta'], 'L1_ffn_Wr': _L1_ffn_in['Wr'], 'L1_ffn_W12': _L1_ffn_in['W12'], 'L1_ffn_W3': _L1_ffn_in['W3'], 'L2_xattn_igate_w': _L2_xattn_in['igate_w'], 'L2_xattn_igate_b': _L2_xattn_in['igate_b'], 'L2_xattn_fgate_w': _L2_xattn_in['fgate_w'], 'L2_xattn_fgate_b': _L2_xattn_in['fgate_b'], 'L2_xattn_rpe': _L2_xattn_in['rpe'], 'L2_xattn_ln_w': _L2_xattn_in['ln_w'], 'L2_xattn_ln_b': _L2_xattn_in['ln_b'], 'L2_ffn_w_gate': _L2_ffn_in['w_gate'], 'L2_ffn_w1': _L2_ffn_in['w1'], 'L2_ffn_w3': _L2_ffn_in['w3'], 'L2_ffn_w2': _L2_ffn_in['w2'], 'L3_xattn_Wq': _L3_xattn_in['Wq'], 'L3_xattn_bq': _L3_xattn_in['bq'], 'L3_xattn_Wk': _L3_xattn_in['Wk'], 'L3_xattn_bk': _L3_xattn_in['bk'], 'L3_xattn_Wv': _L3_xattn_in['Wv'], 'L3_xattn_bv': _L3_xattn_in['bv'], 'L3_xattn_Wo': _L3_xattn_in['Wo'], 'L3_xattn_bo': _L3_xattn_in['bo'], 'L3_ffn_router_w': _L3_ffn_in['router_w'], 'L3_ffn_correction_bias': _L3_ffn_in['correction_bias'], 'L3_ffn_gate_w': _L3_ffn_in['gate_w'], 'L3_ffn_up_w': _L3_ffn_in['up_w'], 'L3_ffn_down_w': _L3_ffn_in['down_w'], 'L3_ffn_shared_gate_w': _L3_ffn_in['shared_gate_w'], 'L3_ffn_shared_up_w': _L3_ffn_in['shared_up_w'], 'L3_ffn_shared_down_w': _L3_ffn_in['shared_down_w']}

def reference(x, ctx_1024, itok_SxS2_0_2016, L0_xattn_q_w, L0_xattn_q_b, L0_xattn_k_w, L0_xattn_k_b, L0_xattn_v_w, L0_xattn_v_b, L0_xattn_o_w, L0_xattn_o_b, L0_ffn_Wr, L0_ffn_W1, L0_ffn_W2, L1_xattn_w_q, L1_xattn_b_q, L1_xattn_w_k, L1_xattn_b_k, L1_xattn_w_v, L1_xattn_b_v, L1_xattn_w_o, L1_xattn_b_o, L1_ffn_ln_gamma, L1_ffn_ln_beta, L1_ffn_Wr, L1_ffn_W12, L1_ffn_W3, L2_xattn_igate_w, L2_xattn_igate_b, L2_xattn_fgate_w, L2_xattn_fgate_b, L2_xattn_rpe, L2_xattn_ln_w, L2_xattn_ln_b, L2_ffn_w_gate, L2_ffn_w1, L2_ffn_w3, L2_ffn_w2, L3_xattn_Wq, L3_xattn_bq, L3_xattn_Wk, L3_xattn_bk, L3_xattn_Wv, L3_xattn_bv, L3_xattn_Wo, L3_xattn_bo, L3_ffn_router_w, L3_ffn_correction_bias, L3_ffn_gate_w, L3_ffn_up_w, L3_ffn_down_w, L3_ffn_shared_gate_w, L3_ffn_shared_up_w, L3_ffn_shared_down_w):
    import jax
    import jax.numpy as jnp

    def _L0_xattn_ref(query, key, value, q_w, q_b, k_w, k_b, v_w, v_b, o_w, o_b):
        import jax, jax.numpy as jnp
        import numpy as np
        EMBED_DIM = 128
        NUM_HEADS = 16
        HEAD_DIM = EMBED_DIM // NUM_HEADS
        WINDOW = 64

        def apply_rope(x):
            B, H, S, d = x.shape
            half = d // 2
            pos = jnp.arange(S, dtype=x.dtype)
            freqs = 1.0 / 10000.0 ** (jnp.arange(half, dtype=x.dtype) / half)
            ang = pos[:, None] * freqs[None, :]
            cos, sin = (jnp.cos(ang), jnp.sin(ang))
            x1, x2 = (x[..., :half], x[..., half:])
            return jnp.concatenate([x1 * cos - x2 * sin, x1 * sin + x2 * cos], axis=-1)

        def _forward(query, key, value, q_w, q_b, k_w, k_b, v_w, v_b, o_w, o_b):
            B, S_q, D = query.shape
            S_k = key.shape[1]
            H, d, W = (NUM_HEADS, HEAD_DIM, WINDOW)
            q = (query @ q_w.T + q_b).reshape(B, S_q, H, d).transpose(0, 2, 1, 3)
            k = (key @ k_w.T + k_b).reshape(B, S_k, H, d).transpose(0, 2, 1, 3)
            v = (value @ v_w.T + v_b).reshape(B, S_k, H, d).transpose(0, 2, 1, 3)
            q = apply_rope(q) * d ** (-0.5)
            k = apply_rope(k)
            q_pos = jnp.arange(S_q)[:, None]
            offsets = jnp.arange(-W, 1)[None, :]
            idx = q_pos + offsets
            local_mask = (idx < 0) | (idx >= S_k)
            gidx = jnp.clip(idx, 0, S_k - 1)
            k_win = k[:, :, gidx, :]
            v_win = v[:, :, gidx, :]
            scores = jnp.einsum('bhqd,bhqwd->bhqw', q, k_win)
            mask = local_mask[None, None, :, :]
            scores = jnp.where(mask, -jnp.inf, scores)
            m = jnp.max(scores, axis=-1, keepdims=True)
            m = jnp.where(jnp.isfinite(m), m, 0.0)
            e = jnp.exp(scores - m)
            denom = jnp.sum(e, axis=-1, keepdims=True)
            probs = jnp.where(denom > 0, e / jnp.where(denom > 0, denom, 1.0), 0.0)
            ctx = jnp.einsum('bhqw,bhqwd->bhqd', probs, v_win)
            ctx = ctx.transpose(0, 2, 1, 3).reshape(B, S_q, D)
            return ctx @ o_w.T + o_b
        return _forward(query, key, value, q_w, q_b, k_w, k_b, v_w, v_b, o_w, o_b)

    def _L0_ffn_ref(x, Wr, W1, W2):
        import jax, jax.numpy as jnp
        import numpy as np
        N_EXPERTS = 8
        CAP_FACTOR = 1.25
        BATCH, SEQ, DMODEL, DFF = (4, 256, 128, 512)
        B, S, D = x.shape
        E = W1.shape[0]
        cap = int(CAP_FACTOR * B * S / E)
        t = x.reshape(-1, D)
        probs = jax.nn.softmax(t @ Wr, axis=-1)
        idx = jnp.argmax(probs, axis=-1)
        pmax = jnp.max(probs, axis=-1)
        onehot = jax.nn.one_hot(idx, E, dtype=jnp.int32)
        pos = jnp.sum(jnp.cumsum(onehot, axis=0) * onehot, axis=-1) - 1
        kept = pos < cap
        flat = idx * cap + jnp.minimum(pos, cap - 1)
        disp = jnp.zeros((E * cap, D), t.dtype).at[flat].add(t * kept[:, None].astype(t.dtype))
        ein = disp.reshape(E, cap, D)
        h = jax.nn.relu(jnp.einsum('ecd,edf->ecf', ein, W1))
        eout = jnp.einsum('ecf,efd->ecd', h, W2).reshape(E * cap, D)
        comb = jnp.where(kept[:, None], eout[flat], t)
        factor = jnp.where(kept, pmax, jnp.ones_like(pmax))
        out = (comb * factor[:, None]).reshape(B, S, D)
        return out

    def _L1_xattn_ref(queries, keys, values, w_q, b_q, w_k, b_k, w_v, b_v, w_o, b_o):
        import jax, jax.numpy as jnp
        import numpy as np
        D_MODEL = 128
        NUM_HEADS = 16
        D_K = D_MODEL // NUM_HEADS

        def _split_heads(x):
            B, S, _ = x.shape
            return x.reshape(B, S, NUM_HEADS, D_K).transpose(0, 2, 1, 3)
        q = _split_heads(queries @ w_q.T + b_q)
        k = _split_heads(keys @ w_k.T + b_k)
        v = _split_heads(values @ w_v.T + b_v)
        scores = jnp.einsum('bhqd,bhkd->bhqk', q, k) / jnp.sqrt(jnp.asarray(D_K, q.dtype))
        weights = jax.nn.softmax(scores, axis=-1)
        attn = jnp.einsum('bhqk,bhkd->bhqd', weights, v)
        B, H, S, dk = attn.shape
        merged = attn.transpose(0, 2, 1, 3).reshape(B, S, H * dk)
        return merged @ w_o.T + b_o

    def _L1_ffn_ref(x, ln_gamma, ln_beta, Wr, W12, W3):
        import math
        import jax, jax.numpy as jnp
        import numpy as np
        D_MODEL = 128
        D_FF = 512
        E = 8
        K = 2
        CF = 1.25
        CLAMP = 10000.0
        B, S, D = x.shape
        T = B * S
        xf = x.reshape(T, D)
        mu = xf.mean(-1, keepdims=True)
        var = ((xf - mu) ** 2).mean(-1, keepdims=True)
        xn = (xf - mu) / jnp.sqrt(var + 1e-05) * ln_gamma + ln_beta
        logits = jnp.clip(xn @ Wr.T, -CLAMP, CLAMP)
        m = logits.max(-1, keepdims=True)
        ex = jnp.exp(logits - m)
        probs = ex / (ex.sum(-1, keepdims=True) + 1e-12)
        top_p, top_i = jax.lax.top_k(probs, K)
        Sslots = T * K
        experts = top_i.reshape(-1)
        weights = top_p.reshape(-1)
        tokens = jnp.repeat(jnp.arange(T, dtype=jnp.int32), K)
        order = jnp.argsort(experts, stable=True)
        e_s = experts[order]
        w_s = weights[order]
        t_s = tokens[order]
        counts = jnp.bincount(e_s, length=E)
        offsets = jnp.concatenate([jnp.zeros((1,), counts.dtype), jnp.cumsum(counts)])
        rank = jnp.arange(Sslots, dtype=counts.dtype) - offsets[e_s]
        cap = max(1, math.ceil(math.ceil(T * K * CF) / E))
        kept = rank < cap
        pos = jnp.where(kept, rank, cap)
        buf = jnp.zeros((E, cap, D), x.dtype).at[e_s, pos].set(xn[t_s], mode='drop')
        gu = jnp.einsum('ecd,efd->ecf', buf, W12)
        g, u = (gu[..., :D_FF], gu[..., D_FF:])
        h = jax.nn.silu(g) * u
        y = jnp.einsum('ecf,edf->ecd', h, W3)
        y_slot = y[e_s, jnp.minimum(pos, cap - 1)] * (w_s * kept.astype(x.dtype))[:, None]
        out = jnp.zeros((T, D), x.dtype).at[t_s].add(y_slot)
        return out.reshape(B, S, D)

    def _L2_xattn_ref(q, k, v, igate_w, igate_b, fgate_w, fgate_b, rpe, ln_w, ln_b, hops):
        import jax, jax.numpy as jnp
        import numpy as np
        B, S, DIM, NH = (32, 64, 128, 8)
        DH = DIM // NH
        EPS = 1e-06
        LN_EPS = 1e-05

        def _make_hops(n):
            hops = np.zeros((n, n), dtype=np.int64)
            cur = 1
            for i in range(n):
                for j in range(i + 1, n):
                    hops[i, j] = cur
                    hops[j, i] = cur
                    cur += 1
            return (hops, cur)

        def _mlstm_forward(q, k, v, igate_w, igate_b, fgate_w, fgate_b, rpe, ln_w, ln_b, hops):
            Bq, Sq, _ = q.shape
            pos_emb = rpe[hops]
            gate_in = jnp.concatenate([q, k, v], axis=-1)
            ig = gate_in @ igate_w.T + igate_b
            fg = gate_in @ fgate_w.T + fgate_b
            ig = jnp.transpose(ig, (0, 2, 1))
            fg = jnp.transpose(fg, (0, 2, 1))
            qh = q.reshape(Bq, Sq, NH, DH).transpose(0, 2, 1, 3)
            kh = k.reshape(Bq, Sq, NH, DH).transpose(0, 2, 1, 3)
            vh = v.reshape(Bq, Sq, NH, DH).transpose(0, 2, 1, 3)
            log_f = jax.nn.log_sigmoid(fg)
            csum = jnp.cumsum(log_f, axis=-1)
            csum = jnp.concatenate([jnp.zeros((Bq, NH, 1), csum.dtype), csum], axis=-1)
            lfm = csum[:, :, :, None] - csum[:, :, None, :]
            ltr = jnp.tril(jnp.ones((Sq, Sq), dtype=bool))
            log_fg_matrix = jnp.where(ltr, lfm[:, :, 1:, 1:], -jnp.inf)
            log_D = log_fg_matrix + ig[:, :, None, :]
            max_log_D = jnp.max(log_D, axis=-1, keepdims=True)
            D = jnp.exp(log_D - max_log_D)
            k_scaled = kh / np.sqrt(DH).astype(np.float32)
            pe = pos_emb.reshape(Sq, Sq, NH, DH)
            k_hop = jnp.einsum('bhvc,vmhc->bhvm', qh, pe)
            qk = jnp.einsum('bhsd,bhtd->bhst', qh, k_scaled)
            C = (qk + k_hop) * D
            normalizer = jnp.maximum(jnp.abs(jnp.sum(C, axis=-1, keepdims=True)), jnp.exp(-max_log_D))
            Cn = C / (normalizer + EPS)
            h = Cn @ vh
            mu = jnp.mean(h, axis=-1, keepdims=True)
            var = jnp.mean(jnp.square(h - mu), axis=-1, keepdims=True)
            hn = (h - mu) / jnp.sqrt(var + LN_EPS)
            w = (1.0 + ln_w).reshape(NH, DH)
            b = ln_b.reshape(NH, DH)
            hn = hn * w[None, :, None, :] + b[None, :, None, :]
            return hn.transpose(0, 2, 1, 3).reshape(Bq, Sq, DIM)
        return _mlstm_forward(q, k, v, igate_w, igate_b, fgate_w, fgate_b, rpe, ln_w, ln_b, hops)

    def _L2_ffn_ref(x, w_gate, w1, w3, w2):
        import jax, jax.numpy as jnp
        import numpy as np
        B, S, D = (4, 256, 128)
        E, H, TOP_K = (8, 256, 2)
        bsz, seq_len, embed_dim = x.shape
        xt = x.reshape(-1, embed_dim)
        T = xt.shape[0]
        logits = xt @ w_gate
        top_logits, sel = jax.lax.top_k(logits, TOP_K)
        probs = jax.nn.softmax(top_logits, axis=-1).astype(x.dtype)
        h = jax.nn.silu(jnp.einsum('td,edh->eth', xt, w1)) * jnp.einsum('td,edh->eth', xt, w3)
        y = jnp.einsum('eth,ehd->etd', h, w2)
        t_idx = jnp.arange(T)
        yk = y[sel.T, t_idx[None, :], :]
        out = jnp.einsum('ktd,tk->td', yk, probs)
        return out.reshape(bsz, seq_len, embed_dim)

    def _L3_xattn_ref(query, key, value, Wq, bq, Wk, bk, Wv, bv, Wo, bo):
        import jax, jax.numpy as jnp
        import numpy as np
        B, S, D, H = (4, 256, 128, 16)
        DH = D // H
        b, s, _ = query.shape
        q = query @ Wq + bq
        k = key @ Wk + bk
        v = value @ Wv + bv
        q = q.reshape(b, s, H, DH).transpose(0, 2, 1, 3)
        k = k.reshape(b, s, H, DH).transpose(0, 2, 1, 3)
        v = v.reshape(b, s, H, DH).transpose(0, 2, 1, 3)
        scale = jnp.sqrt(jnp.asarray(DH, jnp.float32))
        attn = jnp.einsum('bhqd,bhkd->bhqk', q, k) / scale
        attn = jax.nn.softmax(attn, axis=-1)
        out = jnp.einsum('bhqk,bhkd->bhqd', attn, v)
        out = out.transpose(0, 2, 1, 3).reshape(b, s, D)
        return out @ Wo + bo

    def _L3_ffn_ref(x, router_w, correction_bias, gate_w, up_w, down_w, shared_gate_w, shared_up_w, shared_down_w):
        import jax, jax.numpy as jnp
        import numpy as np
        E = 16
        G = 4
        EPG = E // G
        K = 4
        TOPK_GROUP = 2
        PER_GROUP_K = K // TOPK_GROUP

        def _route(xf, router_w, correction_bias):
            S = xf.shape[0]
            logits = xf @ router_w.T
            scores = jax.nn.sigmoid(logits)
            sb = scores + correction_bias
            grp_top = jax.lax.top_k(sb.reshape(S, G, EPG), PER_GROUP_K)[0]
            group_scores = grp_top.sum(axis=-1)
            _, group_idx = jax.lax.top_k(group_scores, TOPK_GROUP)
            group_mask = jnp.zeros((S, G), sb.dtype).at[jnp.arange(S)[:, None], group_idx].set(1.0)
            score_mask = jnp.broadcast_to(group_mask[:, :, None], (S, G, EPG)).reshape(S, E)
            masked = jnp.where(score_mask > 0, sb, -jnp.inf)
            _, topk_idx = jax.lax.top_k(masked, K)
            w = jnp.take_along_axis(scores, topk_idx, axis=1)
            w = w / (w.sum(axis=-1, keepdims=True) + 1e-20)
            return (topk_idx, w, scores)
        B, T, C = x.shape
        S = B * T
        xf = x.reshape(S, C)
        sg = xf @ shared_gate_w.T
        su = xf @ shared_up_w.T
        shared_out = jax.nn.silu(sg) * su @ shared_down_w.T
        topk_idx, w, _scores = _route(xf, router_w, correction_bias)
        combine = jnp.zeros((S, E), xf.dtype).at[jnp.arange(S)[:, None], topk_idx].add(w)
        g = jnp.einsum('sc,ech->esh', xf, gate_w)
        u = jnp.einsum('sc,ech->esh', xf, up_w)
        h = jax.nn.silu(g) * u
        hw = h * combine.T[:, :, None]
        routed = jnp.einsum('esh,ehc->sc', hw, down_w)
        return (shared_out + routed).reshape(B, T, C)
    x = x + _L0_xattn_ref(_layernorm(x, axis=-1), ctx_1024, ctx_1024, L0_xattn_q_w, L0_xattn_q_b, L0_xattn_k_w, L0_xattn_k_b, L0_xattn_v_w, L0_xattn_v_b, L0_xattn_o_w, L0_xattn_o_b)
    x = x + _L0_ffn_ref(_layernorm(x, axis=-1), L0_ffn_Wr, L0_ffn_W1, L0_ffn_W2)
    x = x + _L1_xattn_ref(_layernorm(x, axis=-1), ctx_1024, ctx_1024, L1_xattn_w_q, L1_xattn_b_q, L1_xattn_w_k, L1_xattn_b_k, L1_xattn_w_v, L1_xattn_b_v, L1_xattn_w_o, L1_xattn_b_o)
    x = x + _L1_ffn_ref(_layernorm(x, axis=-1), L1_ffn_ln_gamma, L1_ffn_ln_beta, L1_ffn_Wr, L1_ffn_W12, L1_ffn_W3)
    x = x + _L2_xattn_ref(_layernorm(x, axis=-1), ctx_1024, ctx_1024, L2_xattn_igate_w, L2_xattn_igate_b, L2_xattn_fgate_w, L2_xattn_fgate_b, L2_xattn_rpe, L2_xattn_ln_w, L2_xattn_ln_b, itok_SxS2_0_2016)
    x = x + _L2_ffn_ref(_layernorm(x, axis=-1), L2_ffn_w_gate, L2_ffn_w1, L2_ffn_w3, L2_ffn_w2)
    x = x + _L3_xattn_ref(_layernorm(x, axis=-1), ctx_1024, ctx_1024, L3_xattn_Wq, L3_xattn_bq, L3_xattn_Wk, L3_xattn_bk, L3_xattn_Wv, L3_xattn_bv, L3_xattn_Wo, L3_xattn_bo)
    x = x + _L3_ffn_ref(_layernorm(x, axis=-1), L3_ffn_router_w, L3_ffn_correction_bias, L3_ffn_gate_w, L3_ffn_up_w, L3_ffn_down_w, L3_ffn_shared_gate_w, L3_ffn_shared_up_w, L3_ffn_shared_down_w)
    return x

_drawn_inputs = setup_inputs


def setup_inputs(seed=0):
    import zlib

    import numpy as np

    out = dict(_drawn_inputs(seed))
    spreads = {'L1_xattn_b_q': (0.0, 0.1),
     'L1_xattn_b_k': (0.0, 2.0),
     'L1_xattn_b_v': (0.0, 0.1),
     'L1_xattn_b_o': (0.0, 0.1),
     'L1_ffn_ln_gamma': (1.0, 0.577),
     'L1_ffn_ln_beta': (0.0, 0.489),
     'L2_xattn_ln_b': (0.0, 0.1),
     'L3_xattn_bq': (0.0, 0.8),
     'L3_xattn_bk': (0.0, 2.0),
     'L3_xattn_bv': (0.0, 0.8),
     'L3_xattn_bo': (0.0, 0.1),
     'L3_ffn_correction_bias': (0.0, 0.8)}
    factors = {'L0_xattn_q_b': 7.375,
     'L0_xattn_k_b': 8.0,
     'L0_ffn_W1': 3.689,
     'L0_ffn_W2': 3.32,
     'L2_xattn_igate_b': 64.0,
     'L2_xattn_fgate_w': 3.634,
     'L3_xattn_Wq': 8.0,
     'L3_xattn_Wk': 8.0,
     'L3_xattn_Wv': 4.465,
     'L3_xattn_Wo': 3.526,
     'L3_ffn_router_w': 8.0,
     'L3_ffn_gate_w': 8.0,
     'L3_ffn_up_w': 8.0,
     'L3_ffn_down_w': 8.0,
     'L3_ffn_shared_gate_w': 8.0,
     'L3_ffn_shared_up_w': 8.0,
     'L3_ffn_shared_down_w': 8.0}
    for name, (base, spread) in spreads.items():
        noise = np.random.default_rng([zlib.crc32(name.encode()), seed]).standard_normal(out[name].shape)
        drawn = base * np.exp(spread * noise) if base else spread * noise
        out[name] = jnp.asarray(drawn.astype(out[name].dtype))
    for name, factor in factors.items():
        out[name] = (out[name] * factor).astype(out[name].dtype)
    return out
```

```python
from contextlib import ExitStack, contextmanager

import numpy as np
import concourse.bass as bass
from concourse import mybir

F32 = mybir.dt.float32
BF16 = mybir.dt.bfloat16
ALU = mybir.AluOpType
ACT = mybir.ActivationFunctionType
AX = mybir.AxisListType

P = 128
D = 128
S = 64
NT = 16
H = 16
DH = D // H
G = 2
HG = H // G
NEG = -1.0e30

CONST_COLS = {}


def host_constants():
    p = np.arange(P)
    parts = []

    def add(name, a):
        a = np.asarray(a, np.float32).reshape(P, -1)
        start = sum(x.shape[1] for x in parts)
        CONST_COLS[name] = (start, start + a.shape[1])
        parts.append(a)

    add("ident", np.eye(P))
    add("ones", np.ones((P, P)))
    add("tri", p[:, None] <= p[None, :])
    seq = p // S
    add("tri_seq", (p[:, None] <= p[None, :]) & (seq[:, None] == seq[None, :]))
    add("causal", np.where(np.arange(S)[None, :] <= (p % S)[:, None], 0.0, NEG))
    add("head_mask", ((p % S) // DH)[:, None] == np.arange(HG)[None, :])
    add("pair_mask", (p // S)[:, None] == np.arange(2)[None, :])
    half = DH // 2
    freqs = (1.0 / np.float32(10000.0) ** (np.arange(half, dtype=np.float32) / np.float32(half))).astype(np.float32)
    dim = (p % DH)
    ang = (np.arange(S, dtype=np.float32)[None, :] * freqs[dim % half][:, None]).astype(np.float32)
    cos, sin = np.cos(ang), np.sin(ang) * np.where(dim < half, -1.0, 1.0)[:, None]
    add("rope", np.stack([cos, cos, sin, sin, cos, cos, sin, sin], 1))
    add("down8", np.broadcast_to(8.0 - np.arange(8), (P, 8)))
    add("down16", np.broadcast_to(16.0 - np.arange(16), (P, 16)))
    add("down4", np.broadcast_to(4.0 - np.arange(4), (P, 4)))
    add("mask16", (p // 16)[:, None] == np.arange(8)[None, :])
    add("later", np.where((p % S)[:, None] <= np.arange(S)[None, :], 0.0, -NEG))
    r = np.zeros((P, 4, P))
    for q in range(4):
        for e in range(4):
            r[4 * q + e, q, 32 * e:32 * e + 32] = 1
    add("spread", r)
    return np.concatenate(parts, 1)


CONSTS = host_constants()


def alloc(nc, stack, sems=None):
    def sb(name, shape, dt=F32):
        return stack.enter_context(nc.sbuf_tensor(name, shape, dt))

    def ps(name, shape, dt=F32):
        return stack.enter_context(nc.psum_tensor(name, shape, dt))

    def sem(name):
        if sems is None:
            return stack.enter_context(nc.semaphore(name))
        sems.append(nc.alloc_semaphore(name))
        return sems[-1]
    return sb, ps, sem


@contextmanager
def stage(nc):
    sems = []
    with ExitStack() as stack:
        yield stack, sems
    nc.clear_and_free_semaphores(sems)
    nc.all_engine_barrier()


def pipeline(eng, body, first, last):
    head = 6 if last > NT + 2 else 4
    tail = NT if (NT - head) % 2 == 0 else NT - 1
    for i in range(first, head):
        body(i, i % 2, i)
    with eng.Fori(head, tail - 1, 2) as i:
        for u in range(2):
            body(i + u, u, None)
    for i in range(tail, last):
        body(i, i % 2, i)


def norm_stats(nc, stack, sems, tag, x):
    sb, ps, sem = alloc(nc, stack, sems)
    stats = sb(f"{tag}_stats", [P, NT, 6])
    mv = sb(f"{tag}_mv", [P, NT, 2])
    std = sb(f"{tag}_std", [P, NT])
    rstd = sb(f"{tag}_rstd", [P, NT])
    stats_ready, mv_ready = sem(f"{tag}_stats_ready"), sem(f"{tag}_mv_ready")
    std_ready, rstd_ready = sem(f"{tag}_std_ready"), sem(f"{tag}_rstd_ready")

    def on_vector(dve):
        for t in range(NT):
            nc.vector.bn_stats(stats[:, t, :], x[:, t, :]).then_inc(stats_ready, 1)
        for t in range(NT):
            dve.wait_ge(stats_ready, t + 1)
            nc.vector.bn_aggr(mv[:, t, :], stats[:, t, :]).then_inc(mv_ready, 1)
        dve.wait_ge(mv_ready, NT)
        nc.vector.tensor_scalar(std[:], mv[:, :, 1], 1e-5, None, ALU.add).then_inc(mv_ready, 1)
        dve.wait_ge(std_ready, 1)
        nc.vector.reciprocal(rstd[:], std[:]).then_inc(rstd_ready, 1)
        dve.wait_ge(rstd_ready, 1)

    def on_scalar(act):
        act.wait_ge(mv_ready, NT + 1)
        nc.scalar.activation(std[:], std[:], ACT.Sqrt).then_inc(std_ready, 1)

    return mv, rstd, on_vector, on_scalar


def attention(nc, tag, g, weights, cols, vrow, orow, rope):
    with stage(nc) as (stack, sems):
        sb, ps, sem = alloc(nc, stack, sems)
        x, ctxT, c, ident = g["x"], g["ctxT"], g["c"], g["c"]("ident")
        ones_row = c("ones")[0:1, :]
        wq, wqr, wk, wkr, wv, wo = weights
        nproj = 8 if rope else 4
        mv, rstd, stats_on_vector, stats_on_scalar = norm_stats(nc, stack, sems, tag, x)
        scale = float(DH) ** -0.5

        xn = sb(f"{tag}_xn", [P, 2, D])
        xnT = sb(f"{tag}_xnT", [P, 2, P])
        ctx2 = sb(f"{tag}_ctx2", [P, 2, 2, 2, S])
        qk = sb(f"{tag}_qk", [P, 8, S]) if rope else None
        qkr = sb(f"{tag}_qkr", [P, 8, S]) if rope else None
        qb = sb(f"{tag}_qb", [P, 2, G, P])
        kT = sb(f"{tag}_kT", [P, 2, G, S])
        km = sb(f"{tag}_km", [P, 2, G, HG, S])
        vb = sb(f"{tag}_vb", [P, 2, H // 2, 2, 2, DH + 1])
        mx = sb(f"{tag}_mx", [P, 2, H])
        pr = sb(f"{tag}_pr", [P, 2, G, HG, S])
        prT = sb(f"{tag}_prT", [P, 2, H // 2, P])
        rec = sb(f"{tag}_rec", [P, 2, H // 2, 2])
        o = sb(f"{tag}_o", [P, 2, D])
        oT = sb(f"{tag}_oT", [P, 2, P])

        ps_s = ps(f"{tag}_ps_s", [P, G, 512])
        ps_t = ps(f"{tag}_ps_t", [P, G, 512])
        ps_qk = ps(f"{tag}_ps_qk", [P, 8, S])
        ps_v = ps(f"{tag}_ps_v", [P, 512])
        ps_o = ps(f"{tag}_ps_o", [P, 512])
        ps_y = ps(f"{tag}_ps_y", [P, 512])
        V, XT = ps_v[:, 0:2 * D], ps_v[:, 384:512]
        O, OT = ps_o[:, 0:288], ps_o[:, 384:512]

        names = ("cleared", "ctx_ready", "xn_ready", "xT_ready", "xnT_ready", "qk_ready", "v_ready", "biased", "turned",
                 "q_ready", "k_ready", "vb_ready", "km_ready", "s_ready", "max_ready", "sub_ready", "exp_ready",
                 "pT_ready", "prT_ready", "o_ready", "rec_ready", "on_ready", "oT_ps_ready", "oT_ready",
                 "y_ready", "x_ready")
        s = {n: sem(f"{tag}_{n}") for n in names}

        with nc.Block() as block:
            @block.vector
            def _(dve):
                nc.vector.memset(qb[:], 0.0).then_inc(s["cleared"], 1)
                for u in range(2):
                    for b in range(2):
                        nc.vector.tensor_copy(vb[:, u, :, b, :, DH],
                                              c("pair_mask").unsqueeze(1).broadcast_to([P, H // 2, 2])
                                              ).then_inc(s["cleared"], 1)
                stats_on_vector(dve)
                dve.wait_ge(s["cleared"], 5)

                def normalise(t, u, edge):
                    if edge is None or t >= 2:
                        dve.wait_ge(s["xT_ready"], t - 1)
                    m = mv[:, bass.ds(t, 1), 0:1].rearrange("p a b -> p (a b)")
                    nc.vector.tensor_scalar(xn[:, u, :], x[:, bass.ds(t, 1), :].rearrange("p a d -> p (a d)"),
                                            m, rstd[:, bass.ds(t, 1)], ALU.subtract, ALU.mult
                                            ).then_inc(s["xn_ready"], 1)

                def spread_qk(t, u, edge):
                    dve.wait_ge(s["qk_ready"], t + 1)
                    if edge is None or t >= 2:
                        dve.wait_ge(s["s_ready"], 2 * t - 2)
                        dve.wait_ge(s["km_ready"], 2 * t - 2)
                    if rope:
                        nc.vector.tensor_tensor(qk[:], ps_qk[:], cols.unsqueeze(2).broadcast_to([P, 8, S]),
                                                ALU.add).then_inc(s["biased"], 1)
                        dve.wait_ge(s["biased"], t + 1)
                        nc.vector.tensor_tensor(qkr[:], qk[:], c("rope").rearrange("p (a s) -> p a s", a=8),
                                                ALU.mult).then_inc(s["turned"], 1)
                        dve.wait_ge(s["turned"], t + 1)
                        a, b, ka, kb = (qkr[:, 2 * i:2 * i + 2, :] for i in range(4))
                    else:
                        a, ka = ps_qk[:, 0:2, :], ps_qk[:, 2:4, :]
                        b = cols[:, 0:2].unsqueeze(2).broadcast_to([P, 2, S])
                        kb = cols[:, 2:4].unsqueeze(2).broadcast_to([P, 2, S])
                    nc.vector.tensor_tensor(kT[:, u], ka, kb, ALU.add).then_inc(s["k_ready"], 1)
                    for n in range(2):
                        r = slice(S * n, S * n + S)
                        nc.vector.tensor_tensor(qb[r, u, :, r], a[r], b[r], ALU.add).then_inc(s["q_ready"], 1)

                def spread_v(t, u, edge):
                    dve.wait_ge(s["v_ready"], t + 1)
                    if edge is None or t >= 2:
                        dve.wait_ge(s["o_ready"], t - 1)
                    for b in range(2):
                        nc.vector.tensor_tensor(
                            vb[:, u, :, b, :, 0:DH],
                            V[:, b * D:b * D + D].rearrange("p (a h d) -> p a h d", h=2, d=DH),
                            c("pair_mask").unsqueeze(1).unsqueeze(3).broadcast_to([P, H // 2, 2, DH]),
                            ALU.mult).then_inc(s["vb_ready"], 1)

                def softmax_shift(t, u, edge):
                    for k in range(G):
                        dve.wait_ge(s["s_ready"], 2 * t + k + 1)
                        sc = ps_s[:, k, :].rearrange("p (h k) -> p h k", k=S)
                        m = mx[:, u, HG * k:HG * k + HG]
                        nc.vector.tensor_reduce(m, sc, AX.X, ALU.max).then_inc(s["max_ready"], 1)
                        dve.wait_ge(s["max_ready"], 2 * t + k + 1)
                        if edge is None or t >= 2:
                            dve.wait_ge(s["pT_ready"], 2 * t + k - 3)
                        nc.vector.tensor_tensor(pr[:, u, k], sc, m.unsqueeze(2).broadcast_to([P, HG, S]),
                                                ALU.subtract).then_inc(s["sub_ready"], 1)

                def normalise_o(t, u, edge):
                    dve.wait_ge(s["o_ready"], t + 1)
                    if edge is None or t >= 2:
                        dve.wait_ge(s["oT_ps_ready"], t - 1)
                    for b in range(2):
                        r = slice(S * b, S * b + S)
                        ob = O[r].rearrange("p (a b h d) -> p a b h d", a=8, b=2, h=2)[:, :, b]
                        nc.vector.reciprocal(rec[r, u], ob[:, :, :, DH]).then_inc(s["rec_ready"], 1)
                    for b in range(2):
                        r = slice(S * b, S * b + S)
                        ob = O[r].rearrange("p (a b h d) -> p a b h d", a=8, b=2, h=2)[:, :, b]
                        dve.wait_ge(s["rec_ready"], 2 * t + b + 1)
                        nc.vector.tensor_tensor(
                            o[r, u, :].rearrange("p (a h d) -> p a h d", h=2, d=DH), ob[:, :, :, 0:DH],
                            rec[r, u].unsqueeze(3).broadcast_to([S, H // 2, 2, DH]),
                            ALU.mult).then_inc(s["on_ready"], 1)

                def residual(t, u, edge):
                    dve.wait_ge(s["y_ready"], t + 1)
                    xt = x[:, bass.ds(t, 1), :].rearrange("p a d -> p (a d)")
                    nc.vector.tensor_tensor(xt, ps_y[:, 0:D], xt, ALU.add).then_inc(s["x_ready"], 1)

                def body(i, u, edge):
                    if edge is None or i < NT:
                        normalise(i, u, edge)
                    if edge is None or 1 <= i < NT + 1:
                        spread_qk(i - 1, 1 - u, edge)
                        spread_v(i - 1, 1 - u, edge)
                        softmax_shift(i - 1, 1 - u, edge)
                    if edge is None or 2 <= i < NT + 2:
                        normalise_o(i - 2, u, edge)
                    if edge is None or 3 <= i:
                        residual(i - 3, 1 - u, edge)
                pipeline(dve, body, 0, NT + 3)

            @block.gpsimd
            def _(pool):
                def body(t, u, edge):
                    if edge is None or t >= 2:
                        pool.wait_ge(s["v_ready"], t - 1)
                    nc.gpsimd.tensor_copy(ctx2[:, u], ctxT[:, bass.ds(t * P, P)].rearrange("p (b k) -> p b k", b=2)
                                          .unsqueeze(2).broadcast_to([P, 2, 2, S])).then_inc(s["ctx_ready"], 1)
                    pool.wait_ge(s["k_ready"], t + 1)
                    if edge is None or t >= 2:
                        pool.wait_ge(s["s_ready"], 2 * t - 2)
                    for k in range(G):
                        nc.gpsimd.tensor_tensor(km[:, u, k], kT[:, u, k].unsqueeze(1).broadcast_to([P, HG, S]),
                                                c("head_mask").unsqueeze(2).broadcast_to([P, HG, S]), ALU.mult
                                                ).then_inc(s["km_ready"], 1)
                pipeline(pool, body, 0, NT)

            @block.scalar
            def _(act):
                stats_on_scalar(act)

                def body(i, u, edge):
                    if edge is None or i < NT:
                        act.wait_ge(s["xT_ready"], i + 1)
                        if edge is None or i >= 2:
                            act.wait_ge(s["qk_ready"], i - 1)
                        nc.scalar.copy(xnT[:, u, :], XT).then_inc(s["xnT_ready"], 1)
                    if edge is None or 3 <= i:
                        t, v = i - 3, 1 - u
                        act.wait_ge(s["oT_ps_ready"], t + 1)
                        if edge is None or t >= 2:
                            act.wait_ge(s["y_ready"], t - 1)
                        nc.scalar.copy(oT[:, v, :], OT).then_inc(s["oT_ready"], 1)
                    if edge is None or 2 <= i < NT + 2:
                        t = i - 2
                        for k in range(G):
                            act.wait_ge(s["pT_ready"], 2 * t + k + 1)
                            if edge is None or t >= 2:
                                act.wait_ge(s["o_ready"], t - 1)
                            nc.scalar.copy(prT[:, u, 4 * k:4 * k + 4, :],
                                           ps_t[:, k, :].rearrange("p (a q) -> p a q", a=4)
                                           ).then_inc(s["prT_ready"], 1)
                    if edge is None or 1 <= i < NT + 1:
                        t, v = i - 1, 1 - u
                        for k in range(G):
                            act.wait_ge(s["sub_ready"], 2 * t + k + 1)
                            nc.scalar.activation(pr[:, v, k], pr[:, v, k], ACT.Exp, scale=scale
                                                 ).then_inc(s["exp_ready"], 1)
                pipeline(act, body, 0, NT + 3)

            @block.tensor
            def _(pe):
                pe.wait_ge(s["cleared"], 5)

                def out_transpose(t, u, edge):
                    pe.wait_ge(s["on_ready"], 2 * t + 2)
                    if edge is None or t >= 1:
                        pe.wait_ge(s["oT_ready"], t)
                    nc.tensor.transpose(OT, o[:, u, :], ident).then_inc(s["oT_ps_ready"], 1)

                def x_transpose(t, u, edge):
                    pe.wait_ge(s["xn_ready"], t + 1)
                    if edge is None or t >= 1:
                        pe.wait_ge(s["xnT_ready"], t)
                    if edge is None or t >= 2:
                        pe.wait_ge(s["vb_ready"], 2 * t - 2)
                    nc.tensor.transpose(XT, xn[:, u, :], ident).then_inc(s["xT_ready"], 1)

                def project(t, u, edge):
                    pe.wait_ge(s["xnT_ready"], t + 1)
                    pe.wait_ge(s["ctx_ready"], t + 1)
                    if edge is None or t >= 1:
                        pe.wait_ge(s["q_ready"], 2 * t)
                        pe.wait_ge(s["k_ready"], t)
                    n = 0
                    for w, src in ((wq, 0), (wqr, 0), (wk, 1), (wkr, 1)):
                        if w is None:
                            continue
                        for k in range(G):
                            for b in range(2):
                                rhs = ctx2[:, u, b, 0] if src else xnT[:, u, S * b:S * b + S]
                                mm = nc.tensor.matmul(ps_qk[S * b:S * b + S, n, :], w[:, S * k:S * k + S], rhs,
                                                      start=True, stop=True)
                            n += 1
                    mm.then_inc(s["qk_ready"], 1)

                def values(t, u, edge):
                    pe.wait_ge(s["xnT_ready"], min(t + 2, NT) if edge is not None else t + 2)
                    for b in range(2):
                        dst = V[:, b * D:b * D + D]
                        nc.tensor.matmul(dst, ctx2[:, u, b].rearrange("p a k -> p (a k)"), wv, start=True, stop=False)
                        mm = nc.tensor.matmul(dst, ones_row, vrow, start=False, stop=True)
                    mm.then_inc(s["v_ready"], 1)

                def prob_transpose(t, u, edge):
                    for k in range(G):
                        pe.wait_ge(s["exp_ready"], 2 * t + k + 1)
                        if edge is None or t >= 1:
                            pe.wait_ge(s["prT_ready"], 2 * t + k - 1)
                        flat = pr[:, u, k].rearrange("p h k -> p (h k)")
                        for a in range(4):
                            mm = nc.tensor.transpose(ps_t[:, k, P * a:P * a + P], flat[:, P * a:P * a + P], ident)
                        mm.then_inc(s["pT_ready"], 1)

                def out_project(t, u, edge):
                    pe.wait_ge(s["oT_ready"], t + 1)
                    if edge is None or t >= 1:
                        pe.wait_ge(s["x_ready"], t)
                    nc.tensor.matmul(ps_y[:, 0:D], oT[:, u, :], wo, start=True, stop=False)
                    nc.tensor.matmul(ps_y[:, 0:D], ones_row, orow, start=False, stop=True
                                     ).then_inc(s["y_ready"], 1)

                def scores(t, u, edge):
                    pe.wait_ge(s["q_ready"], 2 * t + 2)
                    pe.wait_ge(s["km_ready"], 2 * t + 2)
                    for k in range(G):
                        if edge is None or t >= 1:
                            pe.wait_ge(s["sub_ready"], 2 * t + k - 1)
                        if rope:
                            nc.tensor.matmul(ps_s[:, k, :].rearrange("p (h k) -> p h k", k=S), g["ident_bf"],
                                             g["causal_bf"].unsqueeze(1).broadcast_to([P, HG, S]),
                                             start=True, stop=False)
                        nc.tensor.matmul(ps_s[:, k, :].rearrange("p (h k) -> p h k", k=S), qb[:, u, k, :],
                                         km[:, u, k], start=not rope, stop=True).then_inc(s["s_ready"], 1)

                def weigh(t, u, edge):
                    pe.wait_ge(s["prT_ready"], 2 * t + 2)
                    pe.wait_ge(s["vb_ready"], 2 * t + 2)
                    if edge is None or t >= 1:
                        pe.wait_ge(s["on_ready"], 2 * t)
                        pe.wait_ge(s["oT_ready"], t)
                    for a in range(H // 2):
                        mm = nc.tensor.matmul(O[:, 36 * a:36 * a + 36], prT[:, u, a, :],
                                              vb[:, u, a].rearrange("p b h d -> p (b h d)"), start=True, stop=True)
                    mm.then_inc(s["o_ready"], 1)

                def body(i, u, edge):
                    if edge is None or 3 <= i:
                        out_transpose(i - 3, 1 - u, edge)
                    if edge is None or i < NT:
                        x_transpose(i, u, edge)
                    if edge is None or 1 <= i < NT + 1:
                        project(i - 1, 1 - u, edge)
                        values(i - 1, 1 - u, edge)
                    if edge is None or 2 <= i < NT + 2:
                        prob_transpose(i - 2, u, edge)
                    if edge is None or 3 <= i:
                        out_project(i - 3, 1 - u, edge)
                    if edge is None or 1 <= i < NT + 1:
                        scores(i - 1, 1 - u, edge)
                    if edge is None or 2 <= i < NT + 2:
                        weigh(i - 2, u, edge)
                pipeline(pe, body, 0, NT + 3)


class Steps:

    def __init__(self, eng, sem):
        self.eng, self.sem, self.n = eng, sem, 0

    def then(self, instruction):
        self.n += 1
        instruction.then_inc(self.sem, 1)
        self.eng.wait_ge(self.sem, self.n)


def experts(nc, tag, g, kind, n_exp, nf, n_route, w_router, w_gate, w_up, w_down, weights_loaded, cols=None, capacity=None, spare=None):
    with stage(nc) as (stack, sems):
        sb, ps, sem = alloc(nc, stack, sems)
        x, c, ident = g["x"], g["c"], g["c"]("ident")
        E, E8 = n_route, NT * n_route
        again = kind == "capacity2"
        silu = kind != "capacity1"
        grouped = kind == "grouped"
        mv, rstd, stats_on_vector, stats_on_scalar = norm_stats(nc, stack, sems, tag, x)
        xn = sb(f"{tag}_xn", [P, NT, D])
        if again:
            mv2, rstd2, stats2_on_vector, stats2_on_scalar = norm_stats(nc, stack, sems, tag + "_again", xn)
        xT = sb(f"{tag}_xT", [P, NT * P])
        hT = sb(f"{tag}_hT", [P, 2, nf, 512])
        sg = sb(f"{tag}_sg", [P, 2, 512])
        lg = sb(f"{tag}_lg", [P, NT, E])
        gate = sb(f"{tag}_gate", [P, NT, E])
        W = [sb(f"{tag}_work{i}", [P, NT, E]) for i in range(6)]
        M = [sb(f"{tag}_max{i}", [P, NT]) for i in range(5)]
        grp = [sb(f"{tag}_grp{i}", [P, NT, 4]) for i in range(4)] if grouped else None
        gateT = spare[0:E, 0:NT * P] if grouped else None

        ps_g = ps(f"{tag}_ps_g", [P, 2, 512])
        ps_u = ps(f"{tag}_ps_u", [P, 2, 512])
        ps_y = ps(f"{tag}_ps_y", [P, 2, 512])
        ps_t = ps(f"{tag}_ps_t", [P, 512])
        ps_r = ps(f"{tag}_ps_r", [P, 512])

        names = ("xn_ready", "xT_ps_ready", "xT_ready", "logits_ready", "step", "exp_in", "exp_out", "sel_ready",
                 "ranks_ready", "gate_ready", "gateT_ps_ready", "gateT_ready", "dropped_ready",
                 "g_ready", "u_ready", "act_ready", "h_ready", "y_ready", "x_ready", "c_ready", "prod_ready")
        s = {n: sem(f"{tag}_{n}") for n in names}

        with nc.Block() as block:
            @block.vector
            def _(dve):
                step = Steps(dve, s["step"])
                stats_on_vector(dve)
                for t in range(NT):
                    nc.vector.tensor_scalar(xn[:, t, :], x[:, t, :], mv[:, t, 0:1], rstd[:, t:t + 1],
                                            ALU.subtract, ALU.mult).then_inc(s["xn_ready"], 1)
                if again:
                    dve.wait_ge(s["xn_ready"], NT)
                    stats2_on_vector(dve)
                    for t in range(NT):
                        nc.vector.tensor_scalar(xn[:, t, :], xn[:, t, :], mv2[:, t, 0:1], rstd2[:, t:t + 1],
                                                ALU.subtract, ALU.mult).then_inc(s["xn_ready"], 1)
                dve.wait_ge(s["logits_ready"], 1)
                logits = ps_r[:, 0:E8].rearrange("p (t e) -> p t e", e=E)
                full = [P, NT, E]

                def over(m, like=full):
                    return m.unsqueeze(2).broadcast_to(like)

                def tt(out, a, b, op):
                    step.then(nc.vector.tensor_tensor(out, a, b, op))

                def ts(out, a, s1, s2, op0, op1=ALU.bypass):
                    step.then(nc.vector.tensor_scalar(out, a, s1, s2, op0, op1))

                def red(out, a, op=ALU.max):
                    step.then(nc.vector.tensor_reduce(out, a, AX.X, op))

                def first_of_max(values, m, first, tmp, down, shape=full):
                    red(m, values)
                    tt(first, values, over(m, shape), ALU.is_equal)
                    tt(first, first, down, ALU.mult)
                    red(tmp, first)
                    tt(first, first, over(tmp, shape), ALU.is_equal)

                down = c(f"down{E}").unsqueeze(1).broadcast_to(full)
                if again:
                    ts(lg[:], logits, 10000.0, -10000.0, ALU.min, ALU.max)
                else:
                    step.then(nc.vector.tensor_copy(lg[:], logits))

                def ask_exp(n):
                    nc.vector.tensor_copy(W[5][:], W[4][:]).then_inc(s["exp_in"], 1)
                    dve.wait_ge(s["exp_out"], n)

                if kind in ("capacity1", "capacity2"):
                    red(M[0][:], lg[:])
                    tt(W[4][:], lg[:], over(M[0][:]), ALU.subtract)
                    ask_exp(1)
                    red(M[1][:], W[5][:], ALU.add)
                    if kind == "capacity2":
                        ts(M[1][:], M[1][:], 1e-12, None, ALU.add)
                    step.then(nc.vector.reciprocal(M[1][:], M[1][:]))
                    src = lg if kind == "capacity1" else W[5]
                    first_of_max(src[:], M[2][:], W[0][:], M[3][:], down)
                    if kind == "capacity2":
                        ts(W[1][:], W[0][:], -2.0, None, ALU.mult)
                        tt(W[1][:], W[1][:], W[5][:], ALU.add)
                        first_of_max(W[1][:], M[2][:], W[2][:], M[3][:], down)
                        tt(W[0][:], W[0][:], W[2][:], ALU.add)
                    nc.vector.tensor_copy(W[1][:], W[0][:]).then_inc(s["sel_ready"], 1)
                    dve.wait_ge(s["ranks_ready"], 1)
                    prefix = ps_r[:, E8:2 * E8].rearrange("p (t e) -> p t e", e=E)
                    totals = ps_r[:, 2 * E8:3 * E8].rearrange("p (t e) -> p e t", e=E)
                    tot = W[2][:].rearrange("p t e -> p (t e)").rearrange("p (e t) -> p e t", t=NT)
                    inc = W[3][:].rearrange("p t e -> p (t e)")
                    keep = W[4][:].rearrange("p t e -> p (t e)").rearrange("p (e t) -> p e t", t=NT)
                    step.then(nc.vector.tensor_copy(tot, totals))
                    step.then(nc.vector.memset(keep, 1.0))
                    step.then(nc.vector.memset(keep[:, :, 0:1], 0.0))
                    step.then(nc.vector.tensor_tensor_scan(
                        inc, W[4][:].rearrange("p t e -> p (t e)"), W[2][:].rearrange("p t e -> p (t e)"), 0.0,
                        ALU.mult, ALU.add))
                    tt(inc.rearrange("p (e t) -> p e t", t=NT), inc.rearrange("p (e t) -> p e t", t=NT), tot,
                       ALU.subtract)
                    tt(W[4][:], prefix, inc.rearrange("p (e t) -> p t e", t=NT), ALU.add)
                    ts(W[4][:], W[4][:], float(capacity), None, ALU.is_le)
                    tt(W[0][:], W[0][:], W[4][:], ALU.mult)
                    if kind == "capacity1":
                        red(M[2][:], W[0][:], ALU.add)
                        ts(M[2][:], M[2][:], -1.0, 1.0, ALU.mult, ALU.add)
                        tt(gate[:], W[0][:], over(M[1][:]), ALU.mult)
                        for t in range(NT):
                            nc.vector.scalar_tensor_tensor(out=x[:, t, :], in0=xn[:, t, :], scalar=M[2][:, t:t + 1],
                                                           in1=x[:, t, :], op0=ALU.mult, op1=ALU.add
                                                           ).then_inc(s["dropped_ready"], 1)
                        dve.wait_ge(s["dropped_ready"], NT)
                    else:
                        tt(W[1][:], W[5][:], over(M[1][:]), ALU.mult)
                        tt(gate[:], W[0][:], W[1][:], ALU.mult)
                elif kind == "top2":
                    first_of_max(lg[:], M[0][:], W[0][:], M[3][:], down)
                    ts(W[1][:], W[0][:], 2.0 * NEG, None, ALU.mult)
                    tt(W[1][:], W[1][:], lg[:], ALU.add)
                    first_of_max(W[1][:], M[1][:], W[2][:], M[3][:], down)
                    tt(M[1][:], M[1][:], M[0][:], ALU.subtract)
                    step.then(nc.vector.tensor_copy(W[4][:], over(M[1][:])))
                    ask_exp(1)
                    ts(M[2][:], W[5][:, :, 0], 1.0, None, ALU.add)
                    step.then(nc.vector.reciprocal(M[2][:], M[2][:]))
                    tt(M[3][:], M[2][:], W[5][:, :, 0], ALU.mult)
                    tt(W[0][:], W[0][:], over(M[2][:]), ALU.mult)
                    tt(W[2][:], W[2][:], over(M[3][:]), ALU.mult)
                    tt(gate[:], W[0][:], W[2][:], ALU.add)
                else:
                    ts(W[4][:], lg[:], -1.0, None, ALU.mult)
                    ask_exp(1)
                    ts(W[5][:], W[5][:], 1.0, None, ALU.add)
                    step.then(nc.vector.reciprocal(W[0][:], W[5][:]))
                    bias = cols["bias"].unsqueeze(1).broadcast_to(full)
                    tt(W[1][:], W[0][:], bias, ALU.add)
                    four = [P, NT * 4, 4]

                    def by4(a):
                        return a.rearrange("p t (g e) -> p (t g) e", e=4)
                    down4 = c("down4").unsqueeze(1)
                    sb4, f4, r4 = by4(W[1][:]), by4(W[2][:]), by4(W[3][:])
                    m1 = W[4][:, :, 0:4]
                    g1 = grp[0][:]
                    g2 = grp[1][:]
                    g3 = grp[2][:]
                    g4 = grp[3][:]
                    flat = lambda a: a.rearrange("p t g -> p (t g)")
                    first_of_max(sb4, flat(g1), f4, flat(g2), down4.broadcast_to(four), four)
                    ts(f4, f4, NEG, None, ALU.mult)
                    tt(r4, f4, sb4, ALU.add)
                    red(flat(g2), r4)
                    tt(g1, g1, g2, ALU.add)
                    small = [P, NT, 4]
                    d4 = down4.broadcast_to(small)
                    first_of_max(g1, M[0][:], g2, M[1][:], d4, small)
                    ts(g3, g2, NEG, None, ALU.mult)
                    tt(g3, g3, g1, ALU.add)
                    first_of_max(g3, M[0][:], g4, M[1][:], d4, small)
                    tt(g2, g2, g4, ALU.add)
                    ts(g2, g2, -NEG, NEG, ALU.mult, ALU.add)
                    tt(r4, sb4, flat(g2).unsqueeze(2).broadcast_to(four), ALU.add)
                    step.then(nc.vector.memset(gate[:], 0.0))
                    for k in range(4):
                        first_of_max(W[3][:], M[0][:], W[2][:], M[1][:], down)
                        tt(gate[:], gate[:], W[2][:], ALU.add)
                        ts(W[2][:], W[2][:], 4.0 * NEG, None, ALU.mult)
                        tt(W[3][:], W[3][:], W[2][:], ALU.add)
                    tt(gate[:], gate[:], W[0][:], ALU.mult)
                    red(M[0][:], gate[:], ALU.add)
                    ts(M[0][:], M[0][:], 1e-20, None, ALU.add)
                    step.then(nc.vector.reciprocal(M[0][:], M[0][:]))
                    tt(gate[:], gate[:], over(M[0][:]), ALU.mult)
                    nc.vector.tensor_copy(W[1][:], gate[:]).then_inc(s["gate_ready"], 1)

                def hidden(b, e):
                    n = b * n_exp + e
                    for f in range(nf):
                        m = n * nf + f
                        if not silu and f % 2 == 0:
                            continue
                        dve.wait_ge(s["act_ready"] if silu else s["g_ready"], m + 1)
                        if f < 2 and not (isinstance(n, int) and n < 2):
                            dve.wait_ge(s["y_ready"], n - 1)
                        if silu:
                            dve.wait_ge(s["u_ready"], m + 1)
                            ins = nc.vector.tensor_tensor(hT[:, e % 2 if n_exp > 1 else 0, f, :], sg[:, f % 2, :],
                                                          ps_u[:, f % 2, :], ALU.mult)
                            ins.then_inc(s["h_ready"], 1)
                        elif f % 2:
                            nc.vector.tensor_scalar(hT[:, e % 2, f, :], ps_g[:, f % 2, :], 0.0, None, ALU.max
                                                    ).then_inc(s["h_ready"], 1)

                def combine(b, e):
                    n = b * n_exp + e
                    dve.wait_ge(s["y_ready"], n + 1)
                    for k in range(4):
                        if not (isinstance(n, int) and n == 0):
                            dve.wait_ge(s["x_ready"], 4 * n + k - 3)
                        xt = x[:, bass.ds(4 * b + k, 1), :].rearrange("p a d -> p (a d)")
                        y = ps_y[:, e % 2, P * k:P * k + P]
                        gk = gate[:, bass.ds(4 * b + k, 1), e:e + 1].rearrange("p a b -> p (a b)")
                        nc.vector.scalar_tensor_tensor(out=xt, in0=y, scalar=gk, in1=xt, op0=ALU.mult, op1=ALU.add
                                                       ).then_inc(s["x_ready"], 1)

                def add_block(b):
                    dve.wait_ge(s["y_ready"], b + 1)
                    nc.vector.tensor_tensor(x[:, 4 * b:4 * b + 4, :],
                                            ps_y[:, b % 2, :].rearrange("p (t d) -> p t d", d=D),
                                            x[:, 4 * b:4 * b + 4, :], ALU.add).then_inc(s["x_ready"], 4)

                if not grouped:
                    blocks_of_experts(dve, n_exp, hidden, combine)
                else:
                    for b in range(4):
                        for f in range(nf):
                            m = b * nf + f
                            dve.wait_ge(s["act_ready"], m + 1)
                            if f == 0 and b >= 2:
                                dve.wait_ge(s["y_ready"], b - 1)
                            dve.wait_ge(s["u_ready"], m + 1)
                            h = hT[:, b % 2, f, :]
                            ins = nc.vector.tensor_tensor(h, sg[:, f % 2, :], ps_u[:, f % 2, :], ALU.mult)
                            if f < 4:
                                ins.then_inc(s["prod_ready"], 1)
                                dve.wait_ge(s["prod_ready"], 1 + 4 * b + f)
                                dve.wait_ge(s["c_ready"], 4 * b + f + 1)
                                ins = nc.vector.tensor_tensor(h, h, (ps_t if f % 2 else ps_r)[:, 0:512], ALU.mult)
                            ins.then_inc(s["h_ready"], 1)
                        if b:
                            add_block(b - 1)
                    add_block(3)

            @block.scalar
            def _(act):
                stats_on_scalar(act)
                if again:
                    stats2_on_scalar(act)
                for q in range(4):
                    act.wait_ge(s["xT_ps_ready"], q + 1)
                    if again:
                        nc.scalar.activation(xT[:, 512 * q:512 * q + 512], ps_t[:], ACT.Identity,
                                             bias=cols["beta"], scale=cols["gamma"]).then_inc(s["xT_ready"], 1)
                    else:
                        nc.scalar.copy(xT[:, 512 * q:512 * q + 512], ps_t[:]).then_inc(s["xT_ready"], 1)
                act.wait_ge(s["exp_in"], 1)
                nc.scalar.activation(W[5][:], W[5][:], ACT.Exp).then_inc(s["exp_out"], 1)
                if grouped:
                    for q in range(4):
                        act.wait_ge(s["gateT_ps_ready"], q + 1)
                        nc.scalar.copy(gateT[:, 512 * q:512 * q + 512], ps_t[0:E, :]).then_inc(s["gateT_ready"], 1)

                def hidden(b, e):
                    n = b * n_exp + e
                    for f in range(nf):
                        m = n * nf + f
                        if not silu and f % 2:
                            continue
                        act.wait_ge(s["g_ready"], m + 1)
                        if silu:
                            if not (isinstance(m, int) and m < 2):
                                act.wait_ge(s["h_ready"], m - 1)
                            nc.scalar.activation(sg[:, f % 2, :], ps_g[:, f % 2, :], ACT.Silu
                                                 ).then_inc(s["act_ready"], 1)
                        else:
                            if not (isinstance(n, int) and n < 2):
                                act.wait_ge(s["y_ready"], n - 1)
                            nc.scalar.activation(hT[:, e % 2, f, :], ps_g[:, f % 2, :], ACT.Relu
                                                 ).then_inc(s["act_ready"], 1)

                if grouped:
                    for b in range(4):
                        hidden(b, 0)
                else:
                    blocks_of_experts(act, n_exp, hidden, None)

            @block.tensor
            def _(pe):
                pe.wait_ge(weights_loaded, 16)
                for q in range(4):
                    if q >= 1:
                        pe.wait_ge(s["xT_ready"], q)
                    for k in range(4):
                        t = 4 * q + k
                        pe.wait_ge(s["xn_ready"], t + 1 + (NT if again else 0))
                        mm = nc.tensor.transpose(ps_t[:, P * k:P * k + P], xn[:, t, :], ident)
                    mm.then_inc(s["xT_ps_ready"], 1)
                for t in range(NT):
                    pe.wait_ge(s["xT_ready"], t // 4 + 1)
                    mm = nc.tensor.matmul(ps_r[:, E * t:E * t + E], xT[:, P * t:P * t + P], w_router,
                                          start=True, stop=True)
                mm.then_inc(s["logits_ready"], 1)
                if kind in ("capacity1", "capacity2"):
                    pe.wait_ge(s["sel_ready"], 1)
                    sel = W[1][:].rearrange("p t e -> p (t e)")
                    nc.tensor.matmul(ps_r[:, E8:2 * E8], c("tri"), sel, start=True, stop=True)
                    nc.tensor.matmul(ps_r[:, 2 * E8:3 * E8], c("ones"), sel, start=True, stop=True
                                     ).then_inc(s["ranks_ready"], 1)
                if grouped:
                    pe.wait_ge(s["gate_ready"], 1)
                    for q in range(4):
                        if q:
                            pe.wait_ge(s["gateT_ready"], q)
                        for k in range(4):
                            mm = nc.tensor.transpose(ps_t[0:E, P * k:P * k + P], W[1][:, 4 * q + k, :], ident)
                        mm.then_inc(s["gateT_ps_ready"], 1)
                    pe.wait_ge(s["gateT_ready"], 4)

                def up(b, e):
                    n = b * n_exp + e
                    tokens = xT[:, bass.ds(b * 512, 512)]
                    for f in range(nf):
                        m = n * nf + f
                        if not (isinstance(m, int) and m < 2):
                            if silu:
                                pe.wait_ge(s["act_ready"], m - 1)
                            elif f % 2:
                                pe.wait_ge(s["h_ready"], 2 * n + (f - 1) // 2)
                            else:
                                pe.wait_ge(s["act_ready"], 2 * n + f // 2)
                        nc.tensor.matmul(ps_g[:, f % 2, :], w_gate(e, f), tokens, start=True, stop=True
                                         ).then_inc(s["g_ready"], 1)
                        if silu:
                            if not (isinstance(m, int) and m < 2):
                                pe.wait_ge(s["h_ready"], m - 1)
                            nc.tensor.matmul(ps_u[:, f % 2, :], w_up(e, f), tokens, start=True, stop=True
                                             ).then_inc(s["u_ready"], 1)
                        if grouped and f < 4:
                            if b or f >= 2:
                                pe.wait_ge(s["h_ready"], b * nf + f - 1 if f >= 2 else b * nf - 4 + f + 1)
                            nc.tensor.matmul((ps_t if f % 2 else ps_r)[:, 0:512], c("spread")[0:E, P * f:P * f + P],
                                             gateT[:, 512 * b:512 * b + 512], start=True, stop=True
                                             ).then_inc(s["c_ready"], 1)

                def down(b, e):
                    n = b * n_exp + e
                    if silu:
                        pe.wait_ge(s["h_ready"], nf * (n + 1))
                    else:
                        pe.wait_ge(s["h_ready"], nf // 2 * (n + 1))
                        pe.wait_ge(s["act_ready"], nf // 2 * (n + 1))
                    if not (isinstance(n, int) and n < 2):
                        pe.wait_ge(s["x_ready"], 4 * (n - 1))
                    par = (b if n_exp == 1 else e) % 2
                    for k in range(4):
                        for f in range(nf):
                            mm = nc.tensor.matmul(ps_y[:, par, P * k:P * k + P], hT[:, par, f, P * k:P * k + P],
                                                  w_down(e, f), start=f == 0, stop=f == nf - 1)
                    mm.then_inc(s["y_ready"], 1)

                if grouped:
                    for b in range(4):
                        up(b, 0)
                        if b:
                            down(b - 1, 0)
                    down(3, 0)
                else:
                    blocks_of_experts(pe, n_exp, up, down)


def blocks_of_experts(eng, n_exp, ahead, behind):
    def turn(b, first):
        for e in range(n_exp):
            ahead(b, e)
            if behind is not None and not (first and e == 0):
                behind(*((b, e - 1) if e else (b - 1, n_exp - 1)))
    turn(0, True)
    with eng.Fori(1, 4, 1) as b:
        turn(b, False)
    if behind is not None:
        behind(3, n_exp - 1)


def mlstm(nc, g, a, weights_free_arena, gate_w, gate_row, ln_w, ln_b):
    NH, C = 8, 16
    with stage(nc) as (stack, sems):
        sb, ps, sem = alloc(nc, stack, sems)
        x, ctxT, c, ident = g["x"], g["ctxT"], g["c"], g["c"]("ident")
        arena = weights_free_arena
        mv, rstd, stats_on_vector, stats_on_scalar = norm_stats(nc, stack, sems, "l2a", x)
        qz = arena[:, 0:16384].rearrange("p (b h s) -> p b h s", b=2 * NT, h=NH)
        work = arena[:, 16384:20480].rearrange("p (k u n) -> p k u n", k=4, u=2)
        mb, dt, sc, cw = (work[:, k] for k in range(4))
        small = work[:, 3].rearrange("p u (k n) -> p (u k) n", k=4)
        khop = sb("l2a_khop", [P, NT, NH, S])
        xn = sb("l2a_xn", [P, 2, D])
        xT = sb("l2a_xT", [P, 2, P])
        hops = sb("l2a_hops", [P, 32], mybir.dt.int32)
        RING = 4
        pe_rows = sb("l2a_pe_rows", [P, RING, D])
        pe_T = sb("l2a_pe_T", [P, 2, 4 * S])
        gw_ctx = sb("l2a_gw_ctx", [P, 16])
        cum = sb("l2a_cum", [P, P])
        key_gate = sb("l2a_key_gate", [P, NT, NH])
        maxT = sb("l2a_maxT", [P, P])
        floor_ = sb("l2a_floor", [P, NT, NH])
        ctx_t = sb("l2a_ctx_t", [P, 2, D])
        vb = sb("l2a_vb", [P, 2, NH, C + 1])
        absum = sb("l2a_absum", [P, 2, NH])
        n8 = sb("l2a_n8", [P, 6, NH])
        hd = sb("l2a_hd", [P, 2, D])
        cen = sb("l2a_cen", [P, 2, D])
        sq = sb("l2a_sq", [P, D])
        half = sb("l2a_half", [P, NH])

        ps_a = ps("l2a_ps_a", [P, 2, 512])
        ps_k = ps("l2a_ps_k", [P, 2, 512])
        ps_g = ps("l2a_ps_g", [P, 512])
        ps_c = ps("l2a_ps_c", [P, 512])
        ps_x = ps("l2a_ps_x", [P, 2, 512])

        names = ("w_ready", "xn_ready", "xT_ps_ready", "q_ready", "xT_ready", "step", "act_in", "act_out",
                 "logf_ready", "cum_ready", "a_ready", "aT_ready", "maxT_ready", "max_ps_ready", "max_stored",
                 "hops_ready", "peT_ps_ready", "peT_ready", "khop_ps_ready", "khop_ready",
                 "vb_ready", "s_ready", "m1_ready", "m2_ready", "exp_ready", "sc_ready", "cw_ready", "o_ready",
                 "abs_ready", "chain", "cen_ready", "var_ready", "rs_ready", "pchain", "x_ready", "gates_done", "ones", "gate_mm", "x_head")
        s = {n: sem(f"l2a_{n}") for n in names}
        rows_in = [sem(f"l2a_rows_in{k}") for k in range(RING)]
        tile_in = [sem(f"l2a_tile_in{k}") for k in range(2)]
        scratch = nc.dram_tensor("max_scratch", (2, NT, NH, S), F32).ap()

        with nc.Block() as block:
            @block.sync
            def _(sp):
                sp.dma_start(hops[:], a["hops"]).then_inc(s["hops_ready"], 16)
                sp.wait_ge(s["maxT_ready"], 2)
                sp.dma_start(scratch.rearrange("b t h s -> (t h) b s"),
                             maxT[:].rearrange("p (b s) -> p b s", b=2)).then_inc(s["max_stored"], 16)
                sp.wait_ge(s["max_stored"], 16)

                def body(t, u, edge):
                    if edge is None or t >= 2:
                        sp.wait_ge(s["m1_ready"], t - 1)
                        sp.wait_ge(s["vb_ready"], t - 1)
                    for b in range(2):
                        src = scratch[b, bass.ds(t, 1)].rearrange("a h s -> a (h s)").broadcast_to([S, NH * S])
                        sp.dma_start(mb[S * b:S * b + S, u, :], src).then_inc(tile_in[u], 16)
                    sp.dma_start(ctx_t[:, u, :], a["ctx"][:, bass.ds(t, 1), :].rearrange("p a d -> p (a d)")
                                 ).then_inc(tile_in[u], 16)
                pipeline(sp, body, 0, NT)

            @block.gpsimd
            def _(pool):
                nc.gpsimd.memset(half[:], -0.5).then_inc(s["ones"], 1)
                nc.gpsimd.memset(vb[:, :, :, C:C + 1], 1.0).then_inc(s["ones"], 1)
                pool.wait_ge(s["ones"], 2)
                pool.wait_ge(s["hops_ready"], 16)
                for j in range(32):
                    if j >= RING:
                        pool.wait_ge(s["peT_ps_ready"], j // 2 - 1)
                    nc.gpsimd.indirect_dma_start(
                        out=pe_rows[:, j % RING, :], out_offset=None, in_=a["rpe"],
                        in_offset=bass.IndirectOffsetOnAxis(ap=hops[:, j:j + 1], axis=0)
                        ).then_inc(rows_in[j % RING], 16)

                def mask_max(t, u, edge):
                    pool.wait_ge(tile_in[u], 24 * (t - u) + 48)
                    if edge is None or t >= 2:
                        pool.wait_ge(s["o_ready"], t - 1)
                        pool.wait_ge(s["cw_ready"], t - 1)
                    nc.gpsimd.tensor_tensor(dt[:, u].rearrange("p (h s) -> p h s", h=NH),
                                            mb[:, u].rearrange("p (h s) -> p h s", h=NH),
                                            c("later").unsqueeze(1).broadcast_to([P, NH, S]), ALU.add
                                            ).then_inc(s["m1_ready"], 1)
                    nc.gpsimd.tensor_copy(vb[:, u, :, 0:C], ctx_t[:, u, :].rearrange("p (h c) -> p h c", h=NH)
                                          ).then_inc(s["vb_ready"], 1)

                def weights(t, u, edge):
                    pool.wait_ge(s["exp_ready"], t + 1)
                    pool.wait_ge(s["sc_ready"], t + 1)
                    if edge is None or t >= 2:
                        pool.wait_ge(s["o_ready"], t - 1)
                    else:
                        pool.wait_ge(s["gates_done"], 1)
                    nc.gpsimd.tensor_tensor(cw[:, u], sc[:, u], dt[:, u], ALU.mult).then_inc(s["cw_ready"], 1)

                def finish(t, u, edge):
                    pool.wait_ge(s["var_ready"], t + 1)
                    nc.gpsimd.tensor_tensor(n8[:, 4 + u, :], n8[:, 2 + u, :], half[:], ALU.pow
                                            ).then_inc(s["rs_ready"], 1)
                    pool.wait_ge(s["rs_ready"], t + 1)
                    y = cen[:, u, :]
                    y3 = y.rearrange("p (h c) -> p h c", h=NH)
                    nc.gpsimd.tensor_tensor(y3, y3, n8[:, 4 + u, :].unsqueeze(2).broadcast_to([P, NH, C]), ALU.mult
                                            ).then_inc(s["pchain"], 1)
                    pool.wait_ge(s["pchain"], 3 * t + 1)
                    nc.gpsimd.tensor_tensor(y, y, ln_w, ALU.mult).then_inc(s["pchain"], 1)
                    pool.wait_ge(s["pchain"], 3 * t + 2)
                    nc.gpsimd.tensor_tensor(y, y, ln_b, ALU.add).then_inc(s["pchain"], 1)
                    pool.wait_ge(s["pchain"], 3 * t + 3)
                    xt = x[:, bass.ds(t, 1), :].rearrange("p a d -> p (a d)")
                    nc.gpsimd.tensor_tensor(xt, xt, y, ALU.add).then_inc(s["x_ready"], 1)

                def body(i, u, edge):
                    if edge is None or i < NT:
                        mask_max(i, u, edge)
                    if edge is None or 1 <= i < NT + 1:
                        weights(i - 1, 1 - u, edge)
                    if edge is None or 3 <= i:
                        finish(i - 3, 1 - u, edge)
                pipeline(pool, body, 0, NT + 3)

            @block.vector
            def _(dve):
                step = Steps(dve, s["step"])
                nc.vector.tensor_tensor(gw_ctx[:], gate_w[:, 1, :], gate_w[:, 2, :], ALU.add).then_inc(s["w_ready"], 1)
                stats_on_vector(dve)
                for t in range(NT + 1):
                    if t < NT:
                        if t >= 2:
                            dve.wait_ge(s["xT_ps_ready"], t - 1)
                        nc.vector.tensor_scalar(xn[:, t % 2, :], x[:, t, :], mv[:, t, 0:1], rstd[:, t:t + 1],
                                                ALU.subtract, ALU.mult).then_inc(s["xn_ready"], 1)
                    if t >= 1:
                        k = t - 1
                        dve.wait_ge(s["xT_ready"], k + 1)
                        for b in range(2):
                            nc.vector.tensor_tensor(
                                qz[:, 2 * k + b], ps_x[:, k % 2, S * b:S * b + S].unsqueeze(1).broadcast_to([P, NH, S]),
                                c("mask16").unsqueeze(2).broadcast_to([P, NH, S]), ALU.mult).then_inc(s["q_ready"], 1)
                dve.wait_ge(s["gate_mm"], NT)
                gates = ps_g[:, 0:256].rearrange("p (t e) -> p t e", e=16)
                ig, fg, nab, ex, lf = (small[:, k].rearrange("p (t h) -> p t h", h=NH) for k in range(5))
                row = gate_row.unsqueeze(1)
                step.then(nc.vector.tensor_tensor(ig, gates[:, :, 0:8], row[:, :, 0:8].broadcast_to([P, NT, NH]), ALU.add))
                step.then(nc.vector.tensor_tensor(fg, gates[:, :, 8:16], row[:, :, 8:16].broadcast_to([P, NT, NH]),
                                                  ALU.add))
                nc.vector.scalar_tensor_tensor(out=nab, in0=fg, scalar=-1.0, in1=fg, op0=ALU.mult, op1=ALU.min
                                               ).then_inc(s["act_in"], 1)
                dve.wait_ge(s["act_out"], 2)
                nc.vector.scalar_tensor_tensor(out=lf, in0=fg, scalar=0.0, in1=ex, op0=ALU.min, op1=ALU.subtract
                                               ).then_inc(s["logf_ready"], 1)
                dve.wait_ge(s["cum_ready"], 1)
                step.then(nc.vector.tensor_copy(cum[:], ps_c[:, 0:P]))
                nc.vector.tensor_tensor(key_gate[:], ig, cum[:].rearrange("p (t h) -> p t h", h=NH), ALU.subtract
                                        ).then_inc(s["a_ready"], 1)
                dve.wait_ge(s["aT_ready"], 1)
                for b in range(2):
                    nc.vector.tensor_tensor_scan(maxT[:, S * b:S * b + S], c("ones")[:, 0:S],
                                                 ps_c[:, P + S * b:P + S * b + S], -3.0e38, ALU.mult, ALU.max
                                                 ).then_inc(s["maxT_ready"], 1)
                dve.wait_ge(s["max_ps_ready"], 1)
                nc.vector.tensor_tensor(floor_[:], ps_c[:, 2 * P:3 * P].rearrange("p (t h) -> p t h", h=NH),
                                        cum[:].rearrange("p (t h) -> p t h", h=NH), ALU.add).then_inc(s["act_in"], 1)
                dve.wait_ge(s["act_out"], 3)
                step.then(nc.vector.tensor_scalar(floor_[:], floor_[:], 1e-6, None, ALU.add))
                nc.vector.tensor_copy(absum[:], floor_[:, 0:2, :]).then_inc(s["gates_done"], 1)

                def scores(t, u, edge):
                    dve.wait_ge(s["m1_ready"], t + 1)
                    d3 = dt[:, u].rearrange("p (h s) -> p h s", h=NH)
                    ag = key_gate[:, bass.ds(t, 1), :].rearrange("p a h -> p (a h)")
                    nc.vector.tensor_tensor(d3, d3, ag.unsqueeze(2).broadcast_to([P, NH, S]), ALU.subtract
                                            ).then_inc(s["m2_ready"], 1)
                    dve.wait_ge(s["s_ready"], t + 1)
                    if edge is not None and t == 0:
                        dve.wait_ge(s["khop_ready"], 16)
                    if edge is None or t >= 2:
                        dve.wait_ge(s["cw_ready"], t - 1)
                    kh = khop[:, bass.ds(t, 1)].rearrange("p a h s -> p (a h s)")
                    nc.vector.scalar_tensor_tensor(out=sc[:, u], in0=ps_a[:, u, :], scalar=0.25, in1=kh,
                                                   op0=ALU.mult, op1=ALU.add).then_inc(s["sc_ready"], 1)

                def head_norm(t, u, edge):
                    n = [0]

                    def then(ins):
                        n[0] += 1
                        ins.then_inc(s["chain"], 1)
                        dve.wait_ge(s["chain"], 5 * t + n[0])
                    dve.wait_ge(s["o_ready"], t + 1)
                    dve.wait_ge(s["abs_ready"], t + 1)
                    O = ps_k[:, u, 0:NH * (C + 1)].rearrange("p (h c) -> p h c", h=NH)
                    norm, var = n8[:, u, :], n8[:, 2 + u, :]
                    h3, c3 = (w[:, u, :].rearrange("p (h c) -> p h c", h=NH) for w in (hd, cen))
                    fl = floor_[:, bass.ds(t, 1), :].rearrange("p a h -> p (a h)")
                    then(nc.vector.scalar_tensor_tensor(out=norm, in0=absum[:, u, :], scalar=1e-6, in1=fl,
                                                        op0=ALU.add, op1=ALU.max))
                    then(nc.vector.reciprocal(norm, norm))
                    nc.vector.tensor_tensor(h3, O[:, :, 0:C], norm.unsqueeze(2).broadcast_to([P, NH, C]), ALU.mult
                                            ).then_inc(s["x_head"], 1)
                    dve.wait_ge(s["x_head"], t + 1)
                    then(nc.vector.tensor_reduce(norm, h3, AX.X, ALU.add))
                    if edge is None or t >= 2:
                        dve.wait_ge(s["x_ready"], t - 1)
                    nc.vector.scalar_tensor_tensor(out=c3, in0=norm.unsqueeze(2).broadcast_to([P, NH, C]),
                                                   scalar=-1.0 / C, in1=h3, op0=ALU.mult, op1=ALU.add
                                                   ).then_inc(s["cen_ready"], 1)
                    dve.wait_ge(s["cen_ready"], t + 1)
                    then(nc.vector.tensor_tensor(sq[:], cen[:, u, :], cen[:, u, :], ALU.mult))
                    then(nc.vector.tensor_reduce(var, sq[:].rearrange("p (h c) -> p h c", h=NH), AX.X, ALU.add))
                    nc.vector.tensor_scalar(var, var, 1.0 / C, 1e-5, ALU.mult, ALU.add).then_inc(s["var_ready"], 1)

                def body(i, u, edge):
                    if edge is None or i < NT:
                        scores(i, u, edge)
                    if edge is None or 2 <= i < NT + 2:
                        head_norm(i - 2, u, edge)
                pipeline(dve, body, 0, NT + 2)

            @block.scalar
            def _(act):
                stats_on_scalar(act)
                for t in range(NT):
                    act.wait_ge(s["xT_ps_ready"], t + 1)
                    if t >= 2:
                        act.wait_ge(s["gate_mm"], t - 1)
                    nc.scalar.copy(xT[:, t % 2, :], ps_x[:, t % 2, 0:P]).then_inc(s["xT_ready"], 1)
                nab, ex = small[:, 2], small[:, 3]
                act.wait_ge(s["act_in"], 1)
                nc.scalar.activation(ex, nab, ACT.Exp).then_inc(s["act_out"], 1)
                act.wait_ge(s["act_out"], 1)
                nc.scalar.activation(ex, ex, ACT.Ln, bias=1.0).then_inc(s["act_out"], 1)
                act.wait_ge(s["act_in"], 2)
                nc.scalar.activation(floor_[:], floor_[:], ACT.Exp, scale=-1.0).then_inc(s["act_out"], 1)
                for j in range(16):
                    act.wait_ge(s["peT_ps_ready"], j + 1)
                    if j >= 2:
                        act.wait_ge(s["khop_ps_ready"], j - 1)
                    nc.scalar.copy(pe_T[:, j % 2, :], ps_a[:, j % 2, 0:4 * S]).then_inc(s["peT_ready"], 1)
                    act.wait_ge(s["khop_ps_ready"], j + 1)
                    nc.scalar.copy(khop[:].rearrange("p t h v -> p v (t h)")[:, 4 * j:4 * j + 4, :],
                                   ps_k[:, j % 2, :].rearrange("p (v n) -> p v n", v=4)
                                   ).then_inc(s["khop_ready"], 1)

                def body(i, u, edge):
                    if edge is None or i < NT:
                        act.wait_ge(s["m2_ready"], i + 1)
                        nc.scalar.activation(dt[:, u], dt[:, u], ACT.Exp, scale=-1.0).then_inc(s["exp_ready"], 1)
                    if edge is None or 2 <= i < NT + 2:
                        act.wait_ge(s["o_ready"], i - 1)
                        if edge is None or i >= 4:
                            act.wait_ge(s["x_head"], i - 3)
                        else:
                            act.wait_ge(s["gates_done"], 1)
                        O = ps_k[:, u, 0:NH * (C + 1)].rearrange("p (h c) -> p h c", h=NH)
                        nc.scalar.activation(absum[:, u, :], O[:, :, C], ACT.Abs).then_inc(s["abs_ready"], 1)
                pipeline(act, body, 0, NT + 2)

            @block.tensor
            def _(pe):
                pe.wait_ge(s["w_ready"], 1)

                def gate_mm(t):
                    pe.wait_ge(s["xT_ready"], t + 1)
                    dst = ps_g[:, 16 * t:16 * t + 16]
                    nc.tensor.matmul(dst, xT[:, t % 2, :], gate_w[:, 0, :], start=True, stop=False)
                    nc.tensor.matmul(dst, ctxT[:, P * t:P * t + P], gw_ctx[:], start=False, stop=True
                                     ).then_inc(s["gate_mm"], 1)
                for t in range(NT):
                    pe.wait_ge(s["xn_ready"], t + 1)
                    if t >= 2:
                        pe.wait_ge(s["q_ready"], 2 * (t - 1))
                    nc.tensor.transpose(ps_x[:, t % 2, 0:P], xn[:, t % 2, :], ident).then_inc(s["xT_ps_ready"], 1)
                    if t >= 1:
                        gate_mm(t - 1)
                gate_mm(NT - 1)
                pe.wait_ge(s["logf_ready"], 1)
                nc.tensor.matmul(ps_c[:, 0:P], c("tri_seq"), small[:, 4], start=True, stop=True
                                 ).then_inc(s["cum_ready"], 1)
                pe.wait_ge(s["a_ready"], 1)
                nc.tensor.transpose(ps_c[:, P:2 * P], key_gate[:].rearrange("p t h -> p (t h)"), ident
                                    ).then_inc(s["aT_ready"], 1)
                pe.wait_ge(s["maxT_ready"], 2)
                nc.tensor.transpose(ps_c[:, 2 * P:3 * P], maxT[:], ident).then_inc(s["max_ps_ready"], 1)

                pe.wait_ge(s["q_ready"], 2 * NT)
                for j in range(17):
                    if j < 16:
                        if j >= 2:
                            pe.wait_ge(s["peT_ready"], j - 1)
                        for k in range(2):
                            r = 2 * j + k
                            pe.wait_ge(rows_in[r % RING], 16 * (r // RING + 1))
                            mm = nc.tensor.transpose(ps_a[:, j % 2, P * k:P * k + P], pe_rows[:, r % RING, :], ident)
                        mm.then_inc(s["peT_ps_ready"], 1)
                    if j >= 1:
                        i = j - 1
                        pe.wait_ge(s["peT_ready"], i + 1)
                        if i >= 2:
                            pe.wait_ge(s["khop_ready"], i - 1)
                        for v in range(4):
                            for b in range(2):
                                q = qz[:, b:2 * NT:2, :, 4 * i + v]
                                mm = nc.tensor.matmul(
                                    ps_k[S * b:S * b + S, i % 2, P * v:P * v + P].rearrange("p (t h) -> p t h", h=NH),
                                    pe_T[:, i % 2, S * v:S * v + S], q, start=True, stop=True)
                        mm.then_inc(s["khop_ps_ready"], 1)

                pe.wait_ge(s["ones"], 2)
                for t in range(NT + 1):
                    if t < NT:
                        if t >= 2:
                            pe.wait_ge(s["sc_ready"], t - 1)
                        else:
                            pe.wait_ge(s["peT_ready"], 16)
                        for b in range(2):
                            mm = nc.tensor.matmul(ps_a[S * b:S * b + S, t % 2, :].rearrange("p (h s) -> p h s", h=NH),
                                                  ctxT[:, P * t + S * b:P * t + S * b + S], qz[:, 2 * t + b],
                                                  start=True, stop=True)
                        mm.then_inc(s["s_ready"], 1)
                    if t >= 1:
                        k = t - 1
                        pe.wait_ge(s["cw_ready"], k + 1)
                        pe.wait_ge(s["vb_ready"], k + 1)
                        if k >= 2:
                            pe.wait_ge(s["x_head"], k - 1)
                        else:
                            pe.wait_ge(s["khop_ready"], 16)
                        for b in range(2):
                            r = slice(S * b, S * b + S)
                            for h in range(NH):
                                mm = nc.tensor.matmul(ps_k[r, k % 2, (C + 1) * h:(C + 1) * (h + 1)],
                                                      cw[r, k % 2, S * h:S * h + S], vb[r, k % 2, h, :],
                                                      start=True, stop=True)
                        mm.then_inc(s["o_ready"], 1)


ATT = ["L0_q", "L0_q_turned", "L0_k", "L0_k_turned", "L0_v", "L0_o", "L1_q", "L1_k", "L1_v", "L1_o",
       "L3_q", "L3_k", "L3_v", "L3_o"]
ROWS = ["L0_v", "L0_o", "L1_v", "L1_o", "L3_v", "L3_o"]
STOP = 8
L0_W, L1_W, L2_W, L3_W = 8192, 12288, 6144, 2304


def build(nc, a, out):
    with ExitStack() as stack:
        sb, ps, sem = alloc(nc, stack)
        g = {}
        x = g["x"] = sb("x", [P, NT, D])
        ctxT = g["ctxT"] = sb("ctxT", [P, NT * P])
        consts = sb("consts", [P, CONSTS.shape[1]])
        att_w = sb("att_w", [P, len(ATT), D])
        att_col = sb("att_col", [P, 16])
        rows = sb("rows", [1, len(ROWS), D])
        ident_bf = sb("ident_bf", [P, P], BF16)
        causal_bf = sb("causal_bf", [P, S], BF16)
        g["ident_bf"], g["causal_bf"] = ident_bf[:], causal_bf[:]
        loaded = sem("loaded")
        casts = sem("casts")
        stored = sem("stored")

        def c(name):
            lo, hi = CONST_COLS[name]
            return consts[:, lo:hi]
        g["c"] = c
        arena = sb("arena", [P, L0_W + L1_W])
        late_w = sb("late_w", [P, L2_W + L3_W])
        routers = sb("routers", [P, 8 + 8 + 8 + 16])
        gate_w = sb("gate_w", [P, 3, 16])
        gate_row = sb("gate_row", [P, 17, 16])
        expert_col = sb("expert_col", [P, 2 + 16])
        ffn_loaded = {n: sem(f"ffn_loaded_{n}") for n in ("L0", "L1", "L2", "L3")}

        with nc.Block() as block:
            @block.sync
            def _(sp):
                for dst, src in ((consts, "consts"), (x, "x"), (ctxT, "ctxT"), (att_w, "att_w"),
                                 (att_col, "att_col"), (rows, "rows")):
                    sp.dma_start(dst[:], a[src]).then_inc(loaded, 16)
                sp.dma_start(routers[:], a["routers"]).then_inc(loaded, 16)
                sp.dma_start(expert_col[:], a["expert_col"]).then_inc(loaded, 16)
                sp.dma_start(gate_w[:], a["gate_w"]).then_inc(loaded, 16)
                sp.dma_start(gate_row[:], a["gate_row"]).then_inc(loaded, 16)
                sp.wait_ge(loaded, 16 * 10)
                for n, dst in (("L0", arena[:, 0:L0_W]), ("L1", arena[:, L0_W:L0_W + L1_W]),
                               ("L2", late_w[:, 0:L2_W]), ("L3", late_w[:, L2_W:L2_W + L3_W])):
                    sp.dma_start(dst, a[f"{n}_experts"]).then_inc(ffn_loaded[n], 16)

            @block.vector
            def _(dve):
                dve.wait_ge(loaded, 16 * 10)
                nc.vector.tensor_scalar(gate_row[:, 1:9, :], gate_row[:, 1:9, :], 1.0, None, ALU.add
                                        ).then_inc(casts, 1)
                nc.vector.tensor_copy(ident_bf[:], c("ident")).then_inc(casts, 1)
                nc.vector.tensor_copy(causal_bf[:], c("causal")).then_inc(casts, 1)
                dve.wait_ge(casts, 3)

        w = {n: att_w[:, i, :] for i, n in enumerate(ATT)}
        r = {n: rows[:, i, :] for i, n in enumerate(ROWS)}
        attention(nc, "l0a", g, (w["L0_q"], w["L0_q_turned"], w["L0_k"], w["L0_k_turned"], w["L0_v"], w["L0_o"]),
                  att_col[:, 0:8], r["L0_v"], r["L0_o"], rope=True)

        l0w, l1w = arena[:, 0:L0_W], arena[:, L0_W:L0_W + L1_W]
        l2w, l3w = late_w[:, 0:L2_W], late_w[:, L2_W:L2_W + L3_W]

        if STOP >= 2:
            experts(nc, "l0f", g, "capacity1", 8, 4, 8, routers[:, 0:8],
                    lambda e, f: l0w[:, e * 512 + f * P:e * 512 + f * P + P], None,
                    lambda e, f: l0w[:, 4096 + (e * 4 + f) * P:4096 + (e * 4 + f) * P + P],
                    ffn_loaded["L0"], capacity=int(1.25 * NT * P / 8))
        if STOP >= 3:
            attention(nc, "l1a", g, (w["L1_q"], None, w["L1_k"], None, w["L1_v"], w["L1_o"]),
                      att_col[:, 8:12], r["L1_v"], r["L1_o"], rope=False)
        if STOP >= 4:
            experts(nc, "l1f", g, "capacity2", 8, 4, 8, routers[:, 8:16],
                    lambda e, f: l1w[:, e * 1024 + f * P:e * 1024 + f * P + P],
                    lambda e, f: l1w[:, e * 1024 + 512 + f * P:e * 1024 + 512 + f * P + P],
                    lambda e, f: l1w[:, 8192 + (e * 4 + f) * P:8192 + (e * 4 + f) * P + P],
                    ffn_loaded["L1"], cols={"gamma": expert_col[:, 0:1], "beta": expert_col[:, 1:2]},
                    capacity=-(-int(np.ceil(NT * P * 2 * 1.25)) // 8))
        if STOP >= 5:
            mlstm(nc, g, a, arena, gate_w, gate_row[:, 0, :], gate_row[:, 1:9, :].rearrange("p a b -> p (a b)"),
                  gate_row[:, 9:17, :].rearrange("p a b -> p (a b)"))
        if STOP >= 6:
            experts(nc, "l2f", g, "top2", 8, 2, 8, routers[:, 16:24],
                    lambda e, f: l2w[:, e * 256 + f * P:e * 256 + f * P + P],
                    lambda e, f: l2w[:, 2048 + e * 256 + f * P:2048 + e * 256 + f * P + P],
                    lambda e, f: l2w[:, 4096 + (e * 2 + f) * P:4096 + (e * 2 + f) * P + P],
                    ffn_loaded["L2"])
        if STOP >= 7:
            attention(nc, "l3a", g, (w["L3_q"], None, w["L3_k"], None, w["L3_v"], w["L3_o"]),
                      att_col[:, 12:16], r["L3_v"], r["L3_o"], rope=False)
        if STOP >= 8:
            experts(nc, "l3f", g, "grouped", 1, 6, 16, routers[:, 24:40],
                    lambda e, f: l3w[:, f * P:f * P + P],
                    lambda e, f: l3w[:, 768 + f * P:768 + f * P + P],
                    lambda e, f: l3w[:, 1536 + f * P:1536 + f * P + P],
                    ffn_loaded["L3"], cols={"bias": expert_col[:, 2:18]}, spare=arena)

        with nc.Block() as block:
            @block.sync
            def _(sp):
                sp.dma_start(out, x[:]).then_inc(stored, 16)
                sp.wait_ge(stored, 16)


def kernel(**inputs):
    import concourse.bacc as bacc
    from concourse.bass_utils import run_bass_kernel_spmd

    def two_halves(v):
        return np.concatenate([v.reshape(G, S).T] * 2, 0)

    v = {k: np.asarray(w) for k, w in inputs.items()}
    turn = (np.arange(D) // DH) * DH + (np.arange(D) + DH // 2) % DH
    att = {"L0_q": v["L0_xattn_q_w"].T, "L0_q_turned": v["L0_xattn_q_w"][turn].T,
           "L0_k": v["L0_xattn_k_w"].T, "L0_k_turned": v["L0_xattn_k_w"][turn].T,
           "L0_v": v["L0_xattn_v_w"].T, "L0_o": v["L0_xattn_o_w"].T,
           "L1_q": v["L1_xattn_w_q"].T, "L1_k": v["L1_xattn_w_k"].T, "L1_v": v["L1_xattn_w_v"].T,
           "L1_o": v["L1_xattn_w_o"].T, "L3_q": v["L3_xattn_Wq"], "L3_k": v["L3_xattn_Wk"],
           "L3_v": v["L3_xattn_Wv"], "L3_o": v["L3_xattn_Wo"]}
    arrays = {
        "consts": CONSTS,
        "x": v["x"].reshape(NT, P, D).transpose(1, 0, 2),
        "ctxT": v["ctx_1024"].reshape(NT * P, D).T,
        "att_w": np.stack([att[n] for n in ATT], 1),
        "att_col": np.concatenate([two_halves(w) for w in (
            v["L0_xattn_q_b"], v["L0_xattn_q_b"][turn], v["L0_xattn_k_b"], v["L0_xattn_k_b"][turn],
            v["L1_xattn_b_q"], v["L1_xattn_b_k"], v["L3_xattn_bq"], v["L3_xattn_bk"])], 1),
        "rows": np.stack([v["L0_xattn_v_b"], v["L0_xattn_o_b"], v["L1_xattn_b_v"], v["L1_xattn_b_o"],
                          v["L3_xattn_bv"], v["L3_xattn_bo"]])[None],
    }

    def wide(w):
        return w.transpose(1, 0, 2).reshape(w.shape[1], -1)

    def tall(w):
        e, f, d = w.shape
        return w.reshape(e, f // P, P, d).transpose(2, 0, 1, 3).reshape(P, -1)

    arrays["L0_experts"] = np.concatenate([wide(v["L0_ffn_W1"]), tall(v["L0_ffn_W2"])], 1)
    arrays["L1_experts"] = np.concatenate([wide(v["L1_ffn_W12"].transpose(0, 2, 1)),
                                           tall(v["L1_ffn_W3"].transpose(0, 2, 1))], 1)
    arrays["L2_experts"] = np.concatenate([wide(v["L2_ffn_w1"]), wide(v["L2_ffn_w3"]), tall(v["L2_ffn_w2"])], 1)
    arrays["L3_experts"] = np.concatenate([
        wide(v["L3_ffn_gate_w"]), v["L3_ffn_shared_gate_w"].T, wide(v["L3_ffn_up_w"]), v["L3_ffn_shared_up_w"].T,
        tall(v["L3_ffn_down_w"].reshape(1, 512, D)), tall(v["L3_ffn_shared_down_w"].T[None])], 1)
    arrays["routers"] = np.concatenate([v["L0_ffn_Wr"], v["L1_ffn_Wr"].T, v["L2_ffn_w_gate"],
                                        v["L3_ffn_router_w"].T], 1)
    arrays["ctx"] = v["ctx_1024"].reshape(NT, P, D).transpose(1, 0, 2)
    arrays["rpe"] = v["L2_xattn_rpe"]
    arrays["hops"] = v["itok_SxS2_0_2016"].reshape(32, P).T
    arrays["gate_w"] = np.concatenate([v["L2_xattn_igate_w"], v["L2_xattn_fgate_w"]]).reshape(16, 3, P).transpose(2, 1, 0)
    arrays["gate_row"] = np.broadcast_to(np.concatenate([
        v["L2_xattn_igate_b"], v["L2_xattn_fgate_b"], v["L2_xattn_ln_w"], v["L2_xattn_ln_b"]]
        ).reshape(17, 16), (P, 17, 16))
    arrays["expert_col"] = np.concatenate([
        v["L1_ffn_ln_gamma"][:, None], v["L1_ffn_ln_beta"][:, None],
        np.broadcast_to(v["L3_ffn_correction_bias"], (P, 16))], 1)
    nc = bacc.Bacc("TRN2", target_bir_lowering=False, num_devices=1)
    dram = {}
    for name, arr in list(arrays.items()):
        arrays[f"in_{name}"] = arr = np.ascontiguousarray(arrays.pop(name))
        dram[name] = nc.dram_tensor(f"in_{name}", arr.shape, mybir.dt.from_np(arr.dtype), kind="ExternalInput").ap()
    out = nc.dram_tensor("out", (P, NT, D), F32, kind="ExternalOutput").ap()
    build(nc, dram, out)
    result = run_bass_kernel_spmd(nc, [arrays], core_ids=[0]).results[0]["out"]
    return np.ascontiguousarray(result.transpose(1, 0, 2)).reshape(2 * NT, S, D)
```

```python
from contextlib import ExitStack, contextmanager

import numpy as np
import concourse.bass as bass
from concourse import mybir

F32 = mybir.dt.float32
BF16 = mybir.dt.bfloat16
F32R = mybir.dt.float32r
ALU = mybir.AluOpType
ACT = mybir.ActivationFunctionType
AX = mybir.AxisListType

P = 128
D = 128
S = 64
NT = 16
H = 16
DH = D // H
G = 2
HG = H // G
NEG = -1.0e30
L0_CAP = int(1.25 * NT * P / 8)
L1_CAP = -(-int(np.ceil(NT * P * 2 * 1.25)) // 8)

CONST_COLS = {}


def host_constants():
    p = np.arange(P)
    parts = []

    def add(name, a):
        a = np.asarray(a, np.float32).reshape(P, -1)
        start = sum(x.shape[1] for x in parts)
        CONST_COLS[name] = (start, start + a.shape[1])
        parts.append(a)

    add("ident", np.eye(P))
    add("ones", np.ones((P, P)))
    add("tri", p[:, None] <= p[None, :])
    seq = p // S
    add("tri_seq", (p[:, None] <= p[None, :]) & (seq[:, None] == seq[None, :]))
    add("causal", np.where(np.arange(S)[None, :] <= (p % S)[:, None], 0.0, NEG))
    add("head_mask", ((p % S) // DH)[:, None] == np.arange(HG)[None, :])
    add("pair_mask", (p // S)[:, None] == np.arange(2)[None, :])
    half = DH // 2
    freqs = (1.0 / np.float32(10000.0) ** (np.arange(half, dtype=np.float32) / np.float32(half))).astype(np.float32)
    dim = (p % DH)
    ang = (np.arange(S, dtype=np.float32)[None, :] * freqs[dim % half][:, None]).astype(np.float32)
    cos, sin = np.cos(ang), np.sin(ang) * np.where(dim < half, -1.0, 1.0)[:, None]
    add("rope", np.stack([cos, cos, sin, sin, cos, cos, sin, sin], 1))
    add("down8", np.broadcast_to(8.0 - np.arange(8), (P, 8)))
    add("down16", np.broadcast_to(16.0 - np.arange(16), (P, 16)))
    add("down4", np.broadcast_to(4.0 - np.arange(4), (P, 4)))
    for cap in (L0_CAP, L1_CAP):
        add(f"first_slot{cap}", np.broadcast_to(np.arange(8.0) * cap - 1.0, (P, 8)))
    add("mask16", (p // 16)[:, None] == np.arange(8)[None, :])
    add("later", np.where((p % S)[:, None] <= np.arange(S)[None, :], 0.0, -NEG))
    r = np.zeros((P, 4, P))
    for q in range(4):
        for e in range(4):
            r[4 * q + e, q, 32 * e:32 * e + 32] = 1
    add("spread", r)
    return np.concatenate(parts, 1)


CONSTS = host_constants()


def alloc(nc, stack, sems=None):
    def sb(name, shape, dt=F32):
        return stack.enter_context(nc.sbuf_tensor(name, shape, dt))

    def ps(name, shape, dt=F32):
        return stack.enter_context(nc.psum_tensor(name, shape, dt))

    def sem(name):
        if sems is None:
            return stack.enter_context(nc.semaphore(name))
        sems.append(nc.alloc_semaphore(name))
        return sems[-1]
    return sb, ps, sem


@contextmanager
def stage(nc):
    sems = []
    with ExitStack() as stack:
        yield stack, sems
    nc.clear_and_free_semaphores(sems)
    nc.all_engine_barrier()


def pipeline(eng, body, first, last, peel=4):
    head = 6 if last > NT + 2 else peel
    tail = NT if (NT - head) % 2 == 0 else NT - 1
    for i in range(first, head):
        body(i, i % 2, i)
    with eng.Fori(head, tail - 1, 2) as i:
        for u in range(2):
            body(i + u, u, None)
    for i in range(tail, last):
        body(i, i % 2, i)


def norm_stats(nc, stack, sems, tag, x):
    sb, ps, sem = alloc(nc, stack, sems)
    stats = sb(f"{tag}_stats", [P, NT, 6])
    mv = sb(f"{tag}_mv", [P, NT, 2])
    std = sb(f"{tag}_std", [P, NT])
    rstd = sb(f"{tag}_rstd", [P, NT])
    stats_ready, mv_ready = sem(f"{tag}_stats_ready"), sem(f"{tag}_mv_ready")
    std_ready, rstd_ready = sem(f"{tag}_std_ready"), sem(f"{tag}_rstd_ready")

    def on_vector(dve):
        for t in range(NT):
            nc.vector.bn_stats(stats[:, t, :], x[:, t, :]).then_inc(stats_ready, 1)
        for t in range(NT):
            dve.wait_ge(stats_ready, t + 1)
            nc.vector.bn_aggr(mv[:, t, :], stats[:, t, :]).then_inc(mv_ready, 1)
        dve.wait_ge(mv_ready, NT)
        nc.vector.tensor_scalar(std[:], mv[:, :, 1], 1e-5, None, ALU.add).then_inc(mv_ready, 1)
        dve.wait_ge(std_ready, 1)
        nc.vector.reciprocal(rstd[:], std[:]).then_inc(rstd_ready, 1)
        dve.wait_ge(rstd_ready, 1)

    def on_scalar(act):
        act.wait_ge(mv_ready, NT + 1)
        nc.scalar.activation(std[:], std[:], ACT.Sqrt).then_inc(std_ready, 1)

    return mv, rstd, on_vector, on_scalar


def attention(nc, tag, g, weights, cols, vcol, orow, rope):
    with stage(nc) as (stack, sems):
        sb, ps, sem = alloc(nc, stack, sems)
        x, ctxT, c, ident = g["x"], g["ctxT"], g["c"], g["c"]("ident")
        ones_row = c("ones")[0:1, :]
        wq, wqr, wk, wkr, wv, wo = weights
        mv, rstd, stats_on_vector, stats_on_scalar = norm_stats(nc, stack, sems, tag, x)
        scale = float(DH) ** -0.5

        xn = sb(f"{tag}_xn", [P, 2, D])
        xnT = sb(f"{tag}_xnT", [P, 2, P])
        ctx2 = sb(f"{tag}_ctx2", [P, 2, 2, 2, S])
        qk = sb(f"{tag}_qk", [P, 2, 8, S]) if rope else None
        qkr = sb(f"{tag}_qkr", [P, 2, 8, S]) if rope else None
        qb = sb(f"{tag}_qb", [P, 2, G, P])
        kT = sb(f"{tag}_kT", [P, 2, G, S])
        km = sb(f"{tag}_km", [P, 2, G, HG, S])
        vb = sb(f"{tag}_vb", [P, 2, H // 2, 2, 2, DH + 1])
        mx = sb(f"{tag}_mx", [P, 2, H])
        pr = sb(f"{tag}_pr", [P, 2, G, HG, S])
        prT = sb(f"{tag}_prT", [P, 2, H // 2, P])
        rec = sb(f"{tag}_rec", [P, 2, H // 2, 2])
        o = sb(f"{tag}_o", [P, 2, D])
        oT = sb(f"{tag}_oT", [P, 2, P])
        vcols = sb(f"{tag}_vcols", [P, P])
        ybias = sb(f"{tag}_ybias", [P, D])

        ps_s = ps(f"{tag}_ps_s", [P, G, 512])
        ps_t = ps(f"{tag}_ps_t", [P, G, 512])
        ps_qk = ps(f"{tag}_ps_qk", [P, 8, S])
        ps_mix = ps(f"{tag}_ps_mix", [P, 512])
        ps_o = ps(f"{tag}_ps_o", [P, 512])
        ps_y = ps(f"{tag}_ps_y", [P, 512])
        V, XT, OT, O = ps_mix[:, 0:2 * D], ps_mix[:, 256:384], ps_mix[:, 384:512], ps_o[:, 0:288]

        names = ("cleared", "ctx_ready", "xn_ready", "xT_ready", "qk_ready", "biased", "turned",
                 "q_ready", "k_ready", "km_ready", "s_ready", "max_ready", "sub_ready", "exp_ready",
                 "pT_ready", "prT_ready", "mix_ready", "mix_taken", "o_ready", "rec_ready", "on_ready",
                 "y_ready", "x_ready", "ybias_ps_ready", "ybias_ready", "x_biased")
        s = {n: sem(f"{tag}_{n}") for n in names}

        def live(edge, t):
            return edge is None or 0 <= t < NT

        with nc.Block() as block:
            @block.vector
            def _(dve):
                nc.vector.tensor_copy(vcols[:], vcol.broadcast_to([P, P])).then_inc(s["cleared"], 1)
                nc.vector.memset(qb[:], 0.0).then_inc(s["cleared"], 1)
                for u in range(2):
                    for b in range(2):
                        nc.vector.tensor_copy(vb[:, u, :, b, :, DH],
                                              c("pair_mask").unsqueeze(1).broadcast_to([P, H // 2, 2])
                                              ).then_inc(s["cleared"], 1)
                stats_on_vector(dve)
                dve.wait_ge(s["ybias_ps_ready"], 1)
                nc.vector.tensor_copy(ybias[:], ps_y[:, 0:D]).then_inc(s["ybias_ready"], 1)
                dve.wait_ge(s["cleared"], 6)

                def normalise(t, u, edge):
                    if edge is None or t >= 2:
                        dve.wait_ge(s["mix_ready"], t - 1)
                    m = mv[:, bass.ds(t, 1), 0:1].rearrange("p a b -> p (a b)")
                    nc.vector.tensor_scalar(xn[:, u, :], x[:, bass.ds(t, 1), :].rearrange("p a d -> p (a d)"),
                                            m, rstd[:, bass.ds(t, 1)], ALU.subtract, ALU.mult
                                            ).then_inc(s["xn_ready"], 1)

                def bias_qk(t, u, edge):
                    dve.wait_ge(s["qk_ready"], t + 1)
                    nc.vector.tensor_tensor(qk[:, u], ps_qk[:], cols.unsqueeze(2).broadcast_to([P, 8, S]),
                                            ALU.add).then_inc(s["biased"], 1)

                def spread_qk(t, u, edge):
                    if edge is None or t >= 2:
                        dve.wait_ge(s["s_ready"], 2 * t - 2)
                        dve.wait_ge(s["km_ready"], 2 * t - 2)
                    if rope:
                        dve.wait_ge(s["turned"], t + 1)
                        a, b, ka, kb = (qkr[:, u, 2 * i:2 * i + 2, :] for i in range(4))
                    else:
                        dve.wait_ge(s["qk_ready"], t + 1)
                        a, ka = ps_qk[:, 0:2, :], ps_qk[:, 2:4, :]
                        b = cols[:, 0:2].unsqueeze(2).broadcast_to([P, 2, S])
                        kb = cols[:, 2:4].unsqueeze(2).broadcast_to([P, 2, S])
                    nc.vector.tensor_tensor(kT[:, u], ka, kb, ALU.add).then_inc(s["k_ready"], 1)
                    for n in range(2):
                        r = slice(S * n, S * n + S)
                        nc.vector.tensor_tensor(qb[r, u, :, r], a[r], b[r], ALU.add).then_inc(s["q_ready"], 1)

                def softmax_shift(t, u, edge, k):
                    dve.wait_ge(s["s_ready"], 2 * t + k + 1)
                    sc = ps_s[:, k, :].rearrange("p (h k) -> p h k", k=S)
                    m = mx[:, u, HG * k:HG * k + HG]
                    nc.vector.tensor_reduce(m, sc, AX.X, ALU.max).then_inc(s["max_ready"], 1)
                    dve.wait_ge(s["max_ready"], 2 * t + k + 1)
                    if edge is None or t >= 2:
                        dve.wait_ge(s["pT_ready"], 2 * t + k - 3)
                    nc.vector.tensor_tensor(pr[:, u, k], sc, m.unsqueeze(2).broadcast_to([P, HG, S]),
                                            ALU.subtract).then_inc(s["sub_ready"], 1)

                def normalise_o(t, u, edge):
                    dve.wait_ge(s["o_ready"], t + 1)
                    for b in range(2):
                        r = slice(S * b, S * b + S)
                        ob = O[r].rearrange("p (a b h d) -> p a b h d", a=8, b=2, h=2)[:, :, b]
                        nc.vector.reciprocal(rec[r, u], ob[:, :, :, DH]).then_inc(s["rec_ready"], 1)
                    for b in range(2):
                        r = slice(S * b, S * b + S)
                        ob = O[r].rearrange("p (a b h d) -> p a b h d", a=8, b=2, h=2)[:, :, b]
                        dve.wait_ge(s["rec_ready"], 2 * t + b + 1)
                        nc.vector.tensor_tensor(
                            o[r, u, :].rearrange("p (a h d) -> p a h d", h=2, d=DH), ob[:, :, :, 0:DH],
                            rec[r, u].unsqueeze(3).broadcast_to([S, H // 2, 2, DH]),
                            ALU.mult).then_inc(s["on_ready"], 1)

                def residual(t, u, edge):
                    dve.wait_ge(s["y_ready"], t + 1)
                    dve.wait_ge(s["x_biased"], t + 1)
                    xt = x[:, bass.ds(t, 1), :].rearrange("p a d -> p (a d)")
                    nc.vector.tensor_tensor(xt, ps_y[:, 0:D], xt, ALU.add).then_inc(s["x_ready"], 1)

                def body(i, u, edge):
                    if rope and live(edge, i - 1):
                        bias_qk(i - 1, 1 - u, edge)
                    if live(edge, i):
                        normalise(i, u, edge)
                    if not rope and live(edge, i - 1):
                        spread_qk(i - 1, 1 - u, edge)
                    if live(edge, i - 2):
                        softmax_shift(i - 2, u, edge, 0)
                    if rope and live(edge, i - 1):
                        spread_qk(i - 1, 1 - u, edge)
                    if live(edge, i - 2):
                        softmax_shift(i - 2, u, edge, 1)
                    if live(edge, i - 3):
                        normalise_o(i - 3, 1 - u, edge)
                    if live(edge, i - 4):
                        residual(i - 4, u, edge)
                pipeline(dve, body, 0, NT + 4)

            @block.gpsimd
            def _(pool):
                pool.wait_ge(s["ybias_ready"], 1)

                def body(i, u, edge):
                    if live(edge, i - 1):
                        t, v = i - 1, 1 - u
                        if rope:
                            pool.wait_ge(s["biased"], t + 1)
                            nc.gpsimd.tensor_tensor(qkr[:, v], qk[:, v], c("rope").rearrange("p (a s) -> p a s", a=8),
                                                    ALU.mult).then_inc(s["turned"], 1)
                        pool.wait_ge(s["k_ready"], t + 1)
                        if edge is None or t >= 2:
                            pool.wait_ge(s["s_ready"], 2 * t - 2)
                        for k in range(G):
                            nc.gpsimd.tensor_tensor(km[:, v, k], kT[:, v, k].unsqueeze(1).broadcast_to([P, HG, S]),
                                                    c("head_mask").unsqueeze(2).broadcast_to([P, HG, S]), ALU.mult
                                                    ).then_inc(s["km_ready"], 1)
                    if live(edge, i):
                        pool.wait_ge(s["xn_ready"], i + 1)
                        xt = x[:, bass.ds(i, 1), :].rearrange("p a d -> p (a d)")
                        nc.gpsimd.tensor_tensor(xt, xt, ybias[:], ALU.add).then_inc(s["x_biased"], 1)
                pipeline(pool, body, 0, NT + 1, peel=6)

            @block.scalar
            def _(act):
                stats_on_scalar(act)

                def body(i, u, edge):
                    if live(edge, i - 3):
                        t, v = i - 3, 1 - u
                        for k in range(G):
                            act.wait_ge(s["pT_ready"], 2 * t + k + 1)
                            if edge is None or t >= 2:
                                act.wait_ge(s["o_ready"], t - 1)
                            nc.scalar.copy(prT[:, v, 4 * k:4 * k + 4, :],
                                           ps_t[:, k, :].rearrange("p (a q) -> p a q", a=4)
                                           ).then_inc(s["prT_ready"], 1)
                    if live(edge, i - 2):
                        exponential(i - 2, u, 0)
                    act.wait_ge(s["mix_ready"], i + 1)
                    n = 0
                    if live(edge, i - 4):
                        if edge is None or i >= 6:
                            act.wait_ge(s["y_ready"], i - 5)
                        nc.scalar.copy(oT[:, u, :], OT).then_inc(s["mix_taken"], 1)
                        n += 1
                    if live(edge, i):
                        if edge is None or i >= 2:
                            act.wait_ge(s["qk_ready"], i - 1)
                        nc.scalar.copy(xnT[:, u, :], XT).then_inc(s["mix_taken"], 1)
                        n += 1
                    if live(edge, i - 2):
                        if edge is None or i >= 4:
                            act.wait_ge(s["o_ready"], i - 3)
                        for h in range(2):
                            nc.scalar.activation(vb[:, u, :, :, h, 0:DH].rearrange("p a b d -> p b a d"),
                                                 V.rearrange("p (b a h d) -> p b a h d", b=2, h=2, d=DH)[:, :, :, h],
                                                 ACT.Copy, scale=c("pair_mask")[:, h:h + 1]
                                                 ).then_inc(s["mix_taken"], 1)
                            n += 1
                    if n < 4:
                        act.sem_inc(s["mix_taken"], 4 - n)
                    if live(edge, i):
                        nc.scalar.copy(ctx2[:, u], ctxT[:, bass.ds(i * P, P)].rearrange("p (b k) -> p b k", b=2)
                                       .unsqueeze(2).broadcast_to([P, 2, 2, S])).then_inc(s["ctx_ready"], 1)
                    if live(edge, i - 2):
                        exponential(i - 2, u, 1)

                def exponential(t, u, k):
                    act.wait_ge(s["sub_ready"], 2 * t + k + 1)
                    nc.scalar.activation(pr[:, u, k], pr[:, u, k], ACT.Exp, scale=scale).then_inc(s["exp_ready"], 1)
                pipeline(act, body, 0, NT + 4)

            @block.tensor
            def _(pe):
                pe.wait_ge(s["cleared"], 6)
                nc.tensor.matmul(ps_y[:, 0:D], vcols[:], wo, start=True, stop=False)
                nc.tensor.matmul(ps_y[:, 0:D], ones_row, orow, start=False, stop=True
                                 ).then_inc(s["ybias_ps_ready"], 1)

                def project(t, u, edge):
                    pe.wait_ge(s["mix_taken"], 4 * t + 4)
                    pe.wait_ge(s["ctx_ready"], t + 1)
                    if edge is None or t >= 1:
                        if rope:
                            pe.wait_ge(s["biased"], t)
                        else:
                            pe.wait_ge(s["q_ready"], 2 * t)
                            pe.wait_ge(s["k_ready"], t)
                    n = 0
                    for w, is_key in ((wq, False), (wqr, False), (wk, True), (wkr, True)):
                        if w is None:
                            continue
                        for k in range(G):
                            for b in range(2):
                                rhs = ctx2[:, u, b, 0] if is_key else xnT[:, u, S * b:S * b + S]
                                mm = nc.tensor.matmul(ps_qk[S * b:S * b + S, n, :], w[:, S * k:S * k + S], rhs,
                                                      start=True, stop=True)
                            n += 1
                    mm.then_inc(s["qk_ready"], 1)

                def scores(t, u, edge, k):
                    pe.wait_ge(s["q_ready"], 2 * t + 2)
                    pe.wait_ge(s["km_ready"], 2 * t + k + 1)
                    if edge is None or t >= 1:
                        pe.wait_ge(s["sub_ready"], 2 * t + k - 1)
                    if rope:
                        nc.tensor.matmul(ps_s[:, k, :].rearrange("p (h k) -> p h k", k=S), g["ident_bf"],
                                         g["causal_bf"].unsqueeze(1).broadcast_to([P, HG, S]),
                                         start=True, stop=False)
                    nc.tensor.matmul(ps_s[:, k, :].rearrange("p (h k) -> p h k", k=S), qb[:, u, k, :],
                                     km[:, u, k], start=not rope, stop=True).then_inc(s["s_ready"], 1)

                def prob_transpose(t, u, edge):
                    for k in range(G):
                        pe.wait_ge(s["exp_ready"], 2 * t + k + 1)
                        if edge is None or t >= 1:
                            pe.wait_ge(s["prT_ready"], 2 * t + k - 1)
                        flat = pr[:, u, k].rearrange("p h k -> p (h k)")
                        for a in range(4):
                            mm = nc.tensor.transpose(ps_t[:, k, P * a:P * a + P], flat[:, P * a:P * a + P], ident)
                        mm.then_inc(s["pT_ready"], 1)

                def mix(i, u, edge):
                    if edge is None or i >= 1:
                        pe.wait_ge(s["mix_taken"], 4 * i)
                    mm = None
                    if live(edge, i - 2):
                        for b in range(2):
                            mm = nc.tensor.matmul(V[:, b * D:b * D + D], ctx2[:, u, b].rearrange("p a k -> p (a k)"),
                                                  wv, start=True, stop=True)
                    if live(edge, i):
                        pe.wait_ge(s["xn_ready"], i + 1)
                        mm = nc.tensor.transpose(XT, xn[:, u, :], ident)
                    if live(edge, i - 4):
                        pe.wait_ge(s["on_ready"], 2 * (i - 4) + 2)
                        mm = nc.tensor.transpose(OT, o[:, u, :], ident)
                    if mm is None:
                        pe.sem_inc(s["mix_ready"], 1)
                    else:
                        mm.then_inc(s["mix_ready"], 1)

                def weigh(t, u, edge):
                    pe.wait_ge(s["prT_ready"], 2 * t + 2)
                    if edge is None or t >= 1:
                        pe.wait_ge(s["on_ready"], 2 * t)
                    for a in range(H // 2):
                        mm = nc.tensor.matmul(O[:, 36 * a:36 * a + 36], prT[:, u, a, :],
                                              vb[:, u, a].rearrange("p b h d -> p (b h d)"), start=True, stop=True)
                    mm.then_inc(s["o_ready"], 1)

                def out_project(t, u, edge):
                    pe.wait_ge(s["mix_taken"], 4 * t + 20)
                    if edge is None or t >= 1:
                        pe.wait_ge(s["x_ready"], t)
                    else:
                        pe.wait_ge(s["ybias_ready"], 1)
                    nc.tensor.matmul(ps_y[:, 0:D], oT[:, u, :], wo, start=True, stop=True).then_inc(s["y_ready"], 1)

                def body(i, u, edge):
                    if live(edge, i - 1):
                        project(i - 1, 1 - u, edge)
                    if live(edge, i - 2):
                        scores(i - 2, u, edge, 0)
                    if live(edge, i - 3):
                        prob_transpose(i - 3, 1 - u, edge)
                    if live(edge, i - 2):
                        scores(i - 2, u, edge, 1)
                    mix(i, u, edge)
                    if live(edge, i - 3):
                        weigh(i - 3, 1 - u, edge)
                    if live(edge, i - 4):
                        out_project(i - 4, u, edge)
                pipeline(pe, body, 0, NT + 4)


class Steps:

    def __init__(self, eng, sem):
        self.eng, self.sem, self.n = eng, sem, 0

    def then(self, instruction):
        self.n += 1
        instruction.then_inc(self.sem, 1)
        self.eng.wait_ge(self.sem, self.n)


def routed_experts(nc, tag, g, choices, cap, w_router, w_gate, w_up, w_down, weights_loaded, slots_in, slots_out,
                   slots_cleared, spare, norm_gain=None, norm_shift=None, prefetch=None):
    with stage(nc) as (stack, sems):
        sb, ps, sem = alloc(nc, stack, sems)
        x, c, ident = g["x"], g["c"], g["c"]("ident")
        E, E8, NF, CH = 8, NT * 8, 4, 320
        chunks = E * cap // CH
        again = norm_gain is not None
        swish = w_up is not None
        bounds = E * cap - 1
        mv, rstd, stats_on_vector, stats_on_scalar = norm_stats(nc, stack, sems, tag, x)
        xn = sb(f"{tag}_xn", [P, NT, D])
        if again:
            mv2, rstd2, stats2_on_vector, stats2_on_scalar = norm_stats(nc, stack, sems, tag + "_again", xn)
        xT = sb(f"{tag}_xT", [P, NT * P])
        rows = sb(f"{tag}_rows", [P, 2, 3, D])
        rT = sb(f"{tag}_rT", [P, 2, CH])
        hT = sb(f"{tag}_hT", [P, 2, NF, CH])
        sg = sb(f"{tag}_sg", [P, 2, CH])
        y = sb(f"{tag}_y", [P, 2, 3, D])
        lg = sb(f"{tag}_lg", [P, NT, E])
        W = [sb(f"{tag}_work{i}", [P, NT, E]) for i in range(7)]
        M = [sb(f"{tag}_max{i}", [P, NT]) for i in range(4)]
        gates = [sb(f"{tag}_gate{k}", [P, NT]) for k in range(choices)]
        slot = [sb(f"{tag}_slot{k}", [P, NT], mybir.dt.int32) for k in range(choices)]
        back = [spare[:, NT * D * k:NT * D * (k + 1)].rearrange("p (t d) -> p t d", t=NT) for k in range(choices)]

        ps_g = ps(f"{tag}_ps_g", [P, 2, 512])
        ps_u = ps(f"{tag}_ps_u", [P, 2, 512])
        ps_y = ps(f"{tag}_ps_y", [P, 2, 512])
        ps_t = ps(f"{tag}_ps_t", [P, 2, 512])
        ps_r = ps_g[:, 0, :]

        names = ("cleared", "xn_ready", "xT_ps_ready", "xT_ready", "logits_ready", "step", "exp_in", "exp_out",
                 "sel_ready", "ranks_ready", "slots_ready", "sent", "rT_ps_ready", "rT_ready", "g_ready", "u_ready",
                 "act_ready", "h_ready", "y_ps_ready", "y_ready", "x_ready")
        s = {n: sem(f"{tag}_{n}") for n in names}
        rows_in = [sem(f"{tag}_rows_in{u}") for u in range(2)]
        y_out = [sem(f"{tag}_y_out{u}") for u in range(2)]
        fetched = [sem(f"{tag}_fetched{t}") for t in range(4)]

        def loop_chunks(eng, body, lag=0):
            for ch in range(4):
                body(ch, ch % 2, ch)
            with eng.Fori(4, chunks - 1, 2) as ch:
                for u in range(2):
                    body(ch + u, u, None)
            for ch in range(chunks, chunks + lag):
                body(ch, ch % 2, ch)

        def live(edge, ch):
            return edge is None or 0 <= ch < chunks

        with nc.Block() as block:
            @block.sync
            def _(sp):
                sp.wait_ge(s["sent"], 16 * NT * choices)

                def load(ch, u):
                    part = slots_in[bass.ds(ch * CH, CH), :]
                    sp.dma_start(rows[:, u, 0:2, :], part[0:256, :].rearrange("(a p) d -> p a d", p=P)
                                 ).then_inc(rows_in[u], 16)
                    sp.dma_start(rows[0:64, u, 2, :], part[256:CH, :]).then_inc(rows_in[u], 16)

                def body(ch, u, edge):
                    if live(edge, ch):
                        if edge is None or ch >= 2:
                            sp.wait_ge(s["rT_ps_ready"], ch - 1)
                        load(ch, u)
                loop_chunks(sp, body)

            @block.gpsimd
            def _(pool):
                for k in range(choices):
                    nc.gpsimd.memset(back[k][:], 0.0).then_inc(s["cleared"], 1)
                if prefetch is not None:
                    prefetch(pool)
                pool.wait_ge(slots_cleared, 16)
                pool.wait_ge(s["xn_ready"], NT * (1 + again))
                pool.wait_ge(s["slots_ready"], choices)
                for t in range(NT):
                    for k in range(choices):
                        nc.gpsimd.indirect_dma_start(
                            out=slots_in, out_offset=bass.IndirectOffsetOnAxis(ap=slot[k][:, t:t + 1], axis=0),
                            in_=xn[:, t, :], in_offset=None, bounds_check=bounds, oob_is_err=False
                            ).then_inc(s["sent"], 16)
                pool.wait_ge(s["cleared"], choices)

                def store(ch, u, edge):
                    pool.wait_ge(s["y_ready"], ch + 1)
                    part = slots_out[bass.ds(ch * CH, CH), :]
                    nc.gpsimd.dma_start(part[0:256, :].rearrange("(a p) d -> p a d", p=P), y[:, u, 0:2, :]
                                        ).then_inc(y_out[u], 16)
                    nc.gpsimd.dma_start(part[256:CH, :], y[0:64, u, 2, :]).then_inc(y_out[u], 16)
                loop_chunks(pool, store)
                for u in range(2):
                    pool.wait_ge(y_out[u], 32 * (chunks // 2))
                for t in range(NT):
                    for k in range(choices):
                        nc.gpsimd.indirect_dma_start(
                            out=back[k][:, t, :], out_offset=None, in_=slots_out,
                            in_offset=bass.IndirectOffsetOnAxis(ap=slot[k][:, t:t + 1], axis=0),
                            bounds_check=bounds, oob_is_err=False).then_inc(fetched[t // 4], 16)

            @block.vector
            def _(dve):
                step = Steps(dve, s["step"])
                stats_on_vector(dve)
                for t in range(NT):
                    nc.vector.tensor_scalar(xn[:, t, :], x[:, t, :], mv[:, t, 0:1], rstd[:, t:t + 1],
                                            ALU.subtract, ALU.mult).then_inc(s["xn_ready"], 1)
                if again:
                    dve.wait_ge(s["xn_ready"], NT)
                    stats2_on_vector(dve)
                    for t in range(NT):
                        nc.vector.tensor_scalar(xn[:, t, :], xn[:, t, :], mv2[:, t, 0:1], rstd2[:, t:t + 1],
                                                ALU.subtract, ALU.mult).then_inc(s["xn_ready"], 1)
                dve.wait_ge(s["logits_ready"], 1)
                logits = ps_r[:, 0:E8].rearrange("p (t e) -> p t e", e=E)
                full = [P, NT, E]

                def over(m):
                    return m.unsqueeze(2).broadcast_to(full)

                def per_expert(name):
                    return c(name).unsqueeze(1).broadcast_to(full)

                def tt(out, a, b, op):
                    step.then(nc.vector.tensor_tensor(out, a, b, op))

                def ts(out, a, s1, s2, op0, op1=ALU.bypass):
                    step.then(nc.vector.tensor_scalar(out, a, s1, s2, op0, op1))

                def red(out, a, op=ALU.max):
                    step.then(nc.vector.tensor_reduce(out, a, AX.X, op))

                def first_of_max(values, m, first, tmp):
                    red(m, values)
                    tt(first, values, over(m), ALU.is_equal)
                    tt(first, first, per_expert("down8"), ALU.mult)
                    red(tmp, first)
                    tt(first, first, over(tmp), ALU.is_equal)

                lo, ex, chosen, ranks = lg[:], W[5][:], W[2][:], W[4][:]
                first = [W[0][:], W[1][:]]
                if again:
                    ts(lo, logits, 10000.0, -10000.0, ALU.min, ALU.max)
                else:
                    step.then(nc.vector.tensor_copy(lo, logits))
                red(M[0][:], lo)
                nc.vector.tensor_tensor(ex, lo, over(M[0][:]), ALU.subtract).then_inc(s["exp_in"], 1)
                dve.wait_ge(s["exp_out"], 1)
                if choices == 1:
                    first_of_max(lo, M[2][:], first[0], M[3][:])
                    sel = first[0]
                else:
                    first_of_max(ex, M[2][:], first[0], M[3][:])
                    ts(first[1], first[0], -2.0, None, ALU.mult)
                    tt(W[3][:], first[1], ex, ALU.add)
                    first_of_max(W[3][:], M[2][:], first[1], M[3][:])
                    sel = chosen
                    tt(chosen, first[0], first[1], ALU.add)
                nc.vector.tensor_copy(W[6][:], sel).then_inc(s["sel_ready"], 1)
                red(M[1][:], ex, ALU.add)
                if choices == 2:
                    ts(M[1][:], M[1][:], 1e-12, None, ALU.add)
                step.then(nc.vector.reciprocal(M[1][:], M[1][:]))
                dve.wait_ge(s["ranks_ready"], 1)
                by_expert = lambda a: a.rearrange("p t e -> p (t e)").rearrange("p (e t) -> p e t", t=NT)
                flat = lambda a: a.rearrange("p t e -> p (t e)")
                tot, run, keep = W[2][:], W[3][:], W[6][:]
                step.then(nc.vector.tensor_copy(by_expert(tot), ps_r[:, 2 * E8:3 * E8].rearrange("p (t e) -> p e t", e=E)))
                step.then(nc.vector.memset(keep, 1.0))
                step.then(nc.vector.memset(by_expert(keep)[:, :, 0:1], 0.0))
                step.then(nc.vector.tensor_tensor_scan(flat(run), flat(keep), flat(tot), 0.0, ALU.mult, ALU.add))
                tt(run, run, tot, ALU.subtract)
                tt(ranks, ps_r[:, E8:2 * E8].rearrange("p (t e) -> p t e", e=E),
                   flat(run).rearrange("p (e t) -> p t e", t=NT), ALU.add)
                ts(W[2][:], ranks, float(cap), None, ALU.is_le)
                tt(ranks, ranks, per_expert(f"first_slot{cap}"), ALU.add)
                tt(W[3][:], ex, over(M[1][:]), ALU.mult)
                for k in range(choices):
                    tt(W[6][:], first[k], W[2][:], ALU.mult)
                    red(M[2][:], W[6][:], ALU.add)
                    tt(W[6][:], W[6][:], W[3][:], ALU.mult)
                    red(gates[k][:], W[6][:], ALU.add)
                    tt(W[6][:], first[k], ranks, ALU.mult)
                    red(M[0][:], W[6][:], ALU.add)
                    ts(M[3][:], M[2][:], -1.0e6, 1.0e6, ALU.mult, ALU.add)
                    tt(M[0][:], M[0][:], M[3][:], ALU.add)
                    nc.vector.tensor_copy(slot[k][:], M[0][:]).then_inc(s["slots_ready"], 1)
                    dve.wait_ge(s["slots_ready"], k + 1)
                if choices == 1:
                    ts(M[2][:], M[2][:], -1.0, 1.0, ALU.mult, ALU.add)
                    for t in range(NT):
                        nc.vector.scalar_tensor_tensor(out=x[:, t, :], in0=xn[:, t, :], scalar=M[2][:, t:t + 1],
                                                       in1=x[:, t, :], op0=ALU.mult, op1=ALU.add
                                                       ).then_inc(s["x_ready"], 1)
                    dve.wait_ge(s["x_ready"], NT)

                def body(ch, u, edge):
                    if live(edge, ch):
                        for f in range(NF):
                            if swish:
                                dve.wait_ge(s["act_ready"], NF * ch + f + 1)
                                dve.wait_ge(s["u_ready"], NF * ch + f + 1)
                            elif f % 2:
                                dve.wait_ge(s["g_ready"], NF * ch + f + 1)
                            else:
                                continue
                            if f < 2 and (edge is None or ch >= 2):
                                dve.wait_ge(s["y_ps_ready"], ch - 1)
                            if swish:
                                ins = nc.vector.tensor_tensor(hT[:, u, f, :], sg[:, f % 2, :], ps_u[:, f % 2, 0:CH],
                                                              ALU.mult)
                            else:
                                ins = nc.vector.tensor_scalar(hT[:, u, f, :], ps_g[:, f % 2, 0:CH], 0.0, None, ALU.max)
                            ins.then_inc(s["h_ready"], 1)
                    if live(edge, ch - 1):
                        v = 1 - u
                        dve.wait_ge(s["y_ps_ready"], ch)
                        if edge is None or ch >= 3:
                            dve.wait_ge(y_out[v], 16 * (ch - 1 - v))
                        nc.vector.tensor_copy(y[:, v, 0:2, :], ps_y[:, v, 0:256].rearrange("p (a d) -> p a d", a=2))
                        nc.vector.tensor_copy(y[0:64, v, 2, :], ps_y[0:64, v, 256:384]).then_inc(s["y_ready"], 1)
                loop_chunks(dve, body, 1)
                base = NT if choices == 1 else 0
                for t in range(NT):
                    dve.wait_ge(fetched[t // 4], 16 * choices * 4)
                    for k in range(choices):
                        if k:
                            dve.wait_ge(s["x_ready"], base + choices * t + k)
                        nc.vector.scalar_tensor_tensor(out=x[:, t, :], in0=back[k][:, t, :], scalar=gates[k][:, t:t + 1],
                                                       in1=x[:, t, :], op0=ALU.mult, op1=ALU.add
                                                       ).then_inc(s["x_ready"], 1)

            @block.scalar
            def _(act):
                stats_on_scalar(act)
                if again:
                    stats2_on_scalar(act)
                for q in range(4):
                    act.wait_ge(s["xT_ps_ready"], q + 1)
                    if again:
                        nc.scalar.activation(xT[:, 512 * q:512 * q + 512], ps_t[:, q % 2, :], ACT.Identity,
                                             bias=norm_shift, scale=norm_gain).then_inc(s["xT_ready"], 1)
                    else:
                        nc.scalar.copy(xT[:, 512 * q:512 * q + 512], ps_t[:, q % 2, :]).then_inc(s["xT_ready"], 1)
                act.wait_ge(s["exp_in"], 1)
                nc.scalar.activation(W[5][:], W[5][:], ACT.Exp).then_inc(s["exp_out"], 1)

                def body(ch, u, edge):
                    if live(edge, ch):
                        act.wait_ge(s["rT_ps_ready"], ch + 1)
                        if edge is None or ch >= 2:
                            act.wait_ge(s["g_ready"], NF * (ch - 1))
                            if swish:
                                act.wait_ge(s["u_ready"], NF * (ch - 1))
                        if again:
                            nc.scalar.activation(rT[:, u, :], ps_t[:, u, 0:CH], ACT.Identity, bias=norm_shift,
                                                 scale=norm_gain).then_inc(s["rT_ready"], 1)
                        else:
                            nc.scalar.copy(rT[:, u, :], ps_t[:, u, 0:CH]).then_inc(s["rT_ready"], 1)
                    if live(edge, ch - 1):
                        t, v = ch - 1, 1 - u
                        for f in range(0, NF, 1 if swish else 2):
                            m = NF * t + f
                            act.wait_ge(s["g_ready"], m + 1)
                            if swish:
                                if edge is None or m >= 2:
                                    act.wait_ge(s["h_ready"], m - 1)
                                nc.scalar.activation(sg[:, f % 2, :], ps_g[:, f % 2, 0:CH], ACT.Silu
                                                     ).then_inc(s["act_ready"], 1)
                            else:
                                if f == 0 and (edge is None or t >= 2):
                                    act.wait_ge(s["y_ps_ready"], t - 1)
                                nc.scalar.activation(hT[:, v, f, :], ps_g[:, f % 2, 0:CH], ACT.Relu
                                                     ).then_inc(s["act_ready"], 1)
                loop_chunks(act, body, 1)

            @block.tensor
            def _(pe):
                pe.wait_ge(weights_loaded, 16)
                for q in range(4):
                    if q >= 2:
                        pe.wait_ge(s["xT_ready"], q - 1)
                    for k in range(4):
                        t = 4 * q + k
                        pe.wait_ge(s["xn_ready"], t + 1 + (NT if again else 0))
                        mm = nc.tensor.transpose(ps_t[:, q % 2, P * k:P * k + P], xn[:, t, :], ident)
                    mm.then_inc(s["xT_ps_ready"], 1)
                for t in range(NT):
                    pe.wait_ge(s["xT_ready"], t // 4 + 1)
                    mm = nc.tensor.matmul(ps_r[:, E * t:E * t + E], xT[:, P * t:P * t + P], w_router,
                                          start=True, stop=True)
                mm.then_inc(s["logits_ready"], 1)
                pe.wait_ge(s["sel_ready"], 1)
                sel = W[6][:].rearrange("p t e -> p (t e)")
                nc.tensor.matmul(ps_r[:, E8:2 * E8], c("tri"), sel, start=True, stop=True)
                nc.tensor.matmul(ps_r[:, 2 * E8:3 * E8], c("ones"), sel, start=True, stop=True
                                 ).then_inc(s["ranks_ready"], 1)
                pe.wait_ge(s["slots_ready"], choices)

                def turn(ch):
                    pe.wait_ge(rows_in[ch % 2], 32 * (ch // 2 + 1))
                    if ch >= 2:
                        pe.wait_ge(s["rT_ready"], ch - 1)
                    for a in range(3):
                        n = P if a < 2 else 64
                        mm = nc.tensor.transpose(ps_t[:, ch % 2, P * a:P * a + n], rows[0:n, ch % 2, a, :],
                                                 ident[0:n, 0:n])
                    mm.then_inc(s["rT_ps_ready"], 1)

                def up(ch):
                    e = ch * CH // cap
                    pe.wait_ge(s["rT_ready"], ch + 1)
                    for f in range(NF):
                        m = NF * ch + f
                        if m >= 2:
                            if swish:
                                pe.wait_ge(s["act_ready"], m - 1)
                            elif f % 2:
                                pe.wait_ge(s["h_ready"], 2 * ch + (f - 1) // 2)
                            else:
                                pe.wait_ge(s["act_ready"], 2 * ch + f // 2)
                        nc.tensor.matmul(ps_g[:, f % 2, 0:CH], w_gate(e, f), rT[:, ch % 2, :], start=True, stop=True
                                         ).then_inc(s["g_ready"], 1)
                        if swish:
                            if m >= 2:
                                pe.wait_ge(s["h_ready"], m - 1)
                            nc.tensor.matmul(ps_u[:, f % 2, 0:CH], w_up(e, f), rT[:, ch % 2, :], start=True, stop=True
                                             ).then_inc(s["u_ready"], 1)

                def down(ch):
                    e = ch * CH // cap
                    pe.wait_ge(s["h_ready"], (NF if swish else NF // 2) * (ch + 1))
                    if not swish:
                        pe.wait_ge(s["act_ready"], NF // 2 * (ch + 1))
                    if ch >= 2:
                        pe.wait_ge(s["y_ready"], ch - 1)
                    for a in range(3):
                        n = P if a < 2 else 64
                        for f in range(NF):
                            mm = nc.tensor.matmul(ps_y[0:n, ch % 2, P * a:P * a + P],
                                                  hT[:, ch % 2, f, P * a:P * a + n], w_down(e, f),
                                                  start=f == 0, stop=f == NF - 1)
                    mm.then_inc(s["y_ps_ready"], 1)

                turn(0)
                for ch in range(chunks):
                    if ch + 1 < chunks:
                        turn(ch + 1)
                    up(ch)
                    if ch:
                        down(ch - 1)
                down(chunks - 1)


def experts(nc, tag, g, kind, n_exp, nf, n_route, w_router, w_gate, w_up, w_down, weights_loaded, cols=None, capacity=None, spare=None):
    with stage(nc) as (stack, sems):
        sb, ps, sem = alloc(nc, stack, sems)
        x, c, ident = g["x"], g["c"], g["c"]("ident")
        E, E8 = n_route, NT * n_route
        again = kind == "capacity2"
        silu = kind != "capacity1"
        grouped = kind == "grouped"
        mv, rstd, stats_on_vector, stats_on_scalar = norm_stats(nc, stack, sems, tag, x)
        xn = sb(f"{tag}_xn", [P, NT, D])
        if again:
            mv2, rstd2, stats2_on_vector, stats2_on_scalar = norm_stats(nc, stack, sems, tag + "_again", xn)
        xT = sb(f"{tag}_xT", [P, NT * P])
        hT = sb(f"{tag}_hT", [P, 2, nf, 512])
        sg = sb(f"{tag}_sg", [P, 2, 512])
        lg = sb(f"{tag}_lg", [P, NT, E])
        gate = sb(f"{tag}_gate", [P, NT, E])
        W = [sb(f"{tag}_work{i}", [P, NT, E]) for i in range(6)]
        M = [sb(f"{tag}_max{i}", [P, NT]) for i in range(5)]
        grp = [sb(f"{tag}_grp{i}", [P, NT, 4]) for i in range(4)] if grouped else None
        gateT = sb(f"{tag}_gateT", [16, NT * P]) if grouped else None

        ps_g = ps(f"{tag}_ps_g", [P, 2, 512])
        ps_u = ps(f"{tag}_ps_u", [P, 2, 512])
        ps_y = ps(f"{tag}_ps_y", [P, 2, 512])
        ps_t = ps(f"{tag}_ps_t", [P, 512])
        ps_r = ps(f"{tag}_ps_r", [P, 512])

        names = ("xn_ready", "xT_ps_ready", "xT_ready", "logits_ready", "step", "exp_in", "exp_out", "sel_ready",
                 "ranks_ready", "gate_ready", "gateT_ps_ready", "gateT_ready", "dropped_ready",
                 "g_ready", "u_ready", "act_ready", "h_ready", "y_ready", "x_ready", "c_ready", "prod_ready")
        s = {n: sem(f"{tag}_{n}") for n in names}

        with nc.Block() as block:
            @block.vector
            def _(dve):
                step = Steps(dve, s["step"])
                stats_on_vector(dve)
                for t in range(NT):
                    nc.vector.tensor_scalar(xn[:, t, :], x[:, t, :], mv[:, t, 0:1], rstd[:, t:t + 1],
                                            ALU.subtract, ALU.mult).then_inc(s["xn_ready"], 1)
                if again:
                    dve.wait_ge(s["xn_ready"], NT)
                    stats2_on_vector(dve)
                    for t in range(NT):
                        nc.vector.tensor_scalar(xn[:, t, :], xn[:, t, :], mv2[:, t, 0:1], rstd2[:, t:t + 1],
                                                ALU.subtract, ALU.mult).then_inc(s["xn_ready"], 1)
                dve.wait_ge(s["logits_ready"], 1)
                logits = ps_r[:, 0:E8].rearrange("p (t e) -> p t e", e=E)
                full = [P, NT, E]

                def over(m, like=full):
                    return m.unsqueeze(2).broadcast_to(like)

                def tt(out, a, b, op):
                    step.then(nc.vector.tensor_tensor(out, a, b, op))

                def ts(out, a, s1, s2, op0, op1=ALU.bypass):
                    step.then(nc.vector.tensor_scalar(out, a, s1, s2, op0, op1))

                def red(out, a, op=ALU.max):
                    step.then(nc.vector.tensor_reduce(out, a, AX.X, op))

                def first_of_max(values, m, first, tmp, down, shape=full):
                    red(m, values)
                    tt(first, values, over(m, shape), ALU.is_equal)
                    tt(first, first, down, ALU.mult)
                    red(tmp, first)
                    tt(first, first, over(tmp, shape), ALU.is_equal)

                down = c(f"down{E}").unsqueeze(1).broadcast_to(full)
                if again:
                    ts(lg[:], logits, 10000.0, -10000.0, ALU.min, ALU.max)
                else:
                    step.then(nc.vector.tensor_copy(lg[:], logits))

                def ask_exp(n):
                    nc.vector.tensor_copy(W[5][:], W[4][:]).then_inc(s["exp_in"], 1)
                    dve.wait_ge(s["exp_out"], n)

                if kind in ("capacity1", "capacity2"):
                    red(M[0][:], lg[:])
                    tt(W[4][:], lg[:], over(M[0][:]), ALU.subtract)
                    ask_exp(1)
                    red(M[1][:], W[5][:], ALU.add)
                    if kind == "capacity2":
                        ts(M[1][:], M[1][:], 1e-12, None, ALU.add)
                    step.then(nc.vector.reciprocal(M[1][:], M[1][:]))
                    src = lg if kind == "capacity1" else W[5]
                    first_of_max(src[:], M[2][:], W[0][:], M[3][:], down)
                    if kind == "capacity2":
                        ts(W[1][:], W[0][:], -2.0, None, ALU.mult)
                        tt(W[1][:], W[1][:], W[5][:], ALU.add)
                        first_of_max(W[1][:], M[2][:], W[2][:], M[3][:], down)
                        tt(W[0][:], W[0][:], W[2][:], ALU.add)
                    nc.vector.tensor_copy(W[1][:], W[0][:]).then_inc(s["sel_ready"], 1)
                    dve.wait_ge(s["ranks_ready"], 1)
                    prefix = ps_r[:, E8:2 * E8].rearrange("p (t e) -> p t e", e=E)
                    totals = ps_r[:, 2 * E8:3 * E8].rearrange("p (t e) -> p e t", e=E)
                    tot = W[2][:].rearrange("p t e -> p (t e)").rearrange("p (e t) -> p e t", t=NT)
                    inc = W[3][:].rearrange("p t e -> p (t e)")
                    keep = W[4][:].rearrange("p t e -> p (t e)").rearrange("p (e t) -> p e t", t=NT)
                    step.then(nc.vector.tensor_copy(tot, totals))
                    step.then(nc.vector.memset(keep, 1.0))
                    step.then(nc.vector.memset(keep[:, :, 0:1], 0.0))
                    step.then(nc.vector.tensor_tensor_scan(
                        inc, W[4][:].rearrange("p t e -> p (t e)"), W[2][:].rearrange("p t e -> p (t e)"), 0.0,
                        ALU.mult, ALU.add))
                    tt(inc.rearrange("p (e t) -> p e t", t=NT), inc.rearrange("p (e t) -> p e t", t=NT), tot,
                       ALU.subtract)
                    tt(W[4][:], prefix, inc.rearrange("p (e t) -> p t e", t=NT), ALU.add)
                    ts(W[4][:], W[4][:], float(capacity), None, ALU.is_le)
                    tt(W[0][:], W[0][:], W[4][:], ALU.mult)
                    if kind == "capacity1":
                        red(M[2][:], W[0][:], ALU.add)
                        ts(M[2][:], M[2][:], -1.0, 1.0, ALU.mult, ALU.add)
                        tt(gate[:], W[0][:], over(M[1][:]), ALU.mult)
                        for t in range(NT):
                            nc.vector.scalar_tensor_tensor(out=x[:, t, :], in0=xn[:, t, :], scalar=M[2][:, t:t + 1],
                                                           in1=x[:, t, :], op0=ALU.mult, op1=ALU.add
                                                           ).then_inc(s["dropped_ready"], 1)
                        dve.wait_ge(s["dropped_ready"], NT)
                    else:
                        tt(W[1][:], W[5][:], over(M[1][:]), ALU.mult)
                        tt(gate[:], W[0][:], W[1][:], ALU.mult)
                elif kind == "top2":
                    first_of_max(lg[:], M[0][:], W[0][:], M[3][:], down)
                    ts(W[1][:], W[0][:], 2.0 * NEG, None, ALU.mult)
                    tt(W[1][:], W[1][:], lg[:], ALU.add)
                    first_of_max(W[1][:], M[1][:], W[2][:], M[3][:], down)
                    tt(M[1][:], M[1][:], M[0][:], ALU.subtract)
                    step.then(nc.vector.tensor_copy(W[4][:], over(M[1][:])))
                    ask_exp(1)
                    ts(M[2][:], W[5][:, :, 0], 1.0, None, ALU.add)
                    step.then(nc.vector.reciprocal(M[2][:], M[2][:]))
                    tt(M[3][:], M[2][:], W[5][:, :, 0], ALU.mult)
                    tt(W[0][:], W[0][:], over(M[2][:]), ALU.mult)
                    tt(W[2][:], W[2][:], over(M[3][:]), ALU.mult)
                    tt(gate[:], W[0][:], W[2][:], ALU.add)
                else:
                    ts(W[4][:], lg[:], -1.0, None, ALU.mult)
                    ask_exp(1)
                    ts(W[5][:], W[5][:], 1.0, None, ALU.add)
                    step.then(nc.vector.reciprocal(W[0][:], W[5][:]))
                    bias = cols["bias"].unsqueeze(1).broadcast_to(full)
                    tt(W[1][:], W[0][:], bias, ALU.add)
                    four = [P, NT * 4, 4]

                    def by4(a):
                        return a.rearrange("p t (g e) -> p (t g) e", e=4)
                    down4 = c("down4").unsqueeze(1)
                    sb4, f4, r4 = by4(W[1][:]), by4(W[2][:]), by4(W[3][:])
                    m1 = W[4][:, :, 0:4]
                    g1 = grp[0][:]
                    g2 = grp[1][:]
                    g3 = grp[2][:]
                    g4 = grp[3][:]
                    flat = lambda a: a.rearrange("p t g -> p (t g)")
                    first_of_max(sb4, flat(g1), f4, flat(g2), down4.broadcast_to(four), four)
                    ts(f4, f4, NEG, None, ALU.mult)
                    tt(r4, f4, sb4, ALU.add)
                    red(flat(g2), r4)
                    tt(g1, g1, g2, ALU.add)
                    small = [P, NT, 4]
                    d4 = down4.broadcast_to(small)
                    first_of_max(g1, M[0][:], g2, M[1][:], d4, small)
                    ts(g3, g2, NEG, None, ALU.mult)
                    tt(g3, g3, g1, ALU.add)
                    first_of_max(g3, M[0][:], g4, M[1][:], d4, small)
                    tt(g2, g2, g4, ALU.add)
                    ts(g2, g2, -NEG, NEG, ALU.mult, ALU.add)
                    tt(r4, sb4, flat(g2).unsqueeze(2).broadcast_to(four), ALU.add)
                    step.then(nc.vector.memset(gate[:], 0.0))
                    for k in range(4):
                        first_of_max(W[3][:], M[0][:], W[2][:], M[1][:], down)
                        tt(gate[:], gate[:], W[2][:], ALU.add)
                        ts(W[2][:], W[2][:], 4.0 * NEG, None, ALU.mult)
                        tt(W[3][:], W[3][:], W[2][:], ALU.add)
                    tt(gate[:], gate[:], W[0][:], ALU.mult)
                    red(M[0][:], gate[:], ALU.add)
                    ts(M[0][:], M[0][:], 1e-20, None, ALU.add)
                    step.then(nc.vector.reciprocal(M[0][:], M[0][:]))
                    tt(gate[:], gate[:], over(M[0][:]), ALU.mult)
                    nc.vector.tensor_copy(W[1][:], gate[:]).then_inc(s["gate_ready"], 1)

                def hidden(b, e):
                    n = b * n_exp + e
                    for f in range(nf):
                        m = n * nf + f
                        if not silu and f % 2 == 0:
                            continue
                        dve.wait_ge(s["act_ready"] if silu else s["g_ready"], m + 1)
                        if f < 2 and not (isinstance(n, int) and n < 2):
                            dve.wait_ge(s["y_ready"], n - 1)
                        if silu:
                            dve.wait_ge(s["u_ready"], m + 1)
                            ins = nc.vector.tensor_tensor(hT[:, e % 2 if n_exp > 1 else 0, f, :], sg[:, f % 2, :],
                                                          ps_u[:, f % 2, :], ALU.mult)
                            ins.then_inc(s["h_ready"], 1)
                        elif f % 2:
                            nc.vector.tensor_scalar(hT[:, e % 2, f, :], ps_g[:, f % 2, :], 0.0, None, ALU.max
                                                    ).then_inc(s["h_ready"], 1)

                def combine(b, e):
                    n = b * n_exp + e
                    dve.wait_ge(s["y_ready"], n + 1)
                    for k in range(4):
                        if not (isinstance(n, int) and n == 0):
                            dve.wait_ge(s["x_ready"], 4 * n + k - 3)
                        xt = x[:, bass.ds(4 * b + k, 1), :].rearrange("p a d -> p (a d)")
                        y = ps_y[:, e % 2, P * k:P * k + P]
                        gk = gate[:, bass.ds(4 * b + k, 1), e:e + 1].rearrange("p a b -> p (a b)")
                        nc.vector.scalar_tensor_tensor(out=xt, in0=y, scalar=gk, in1=xt, op0=ALU.mult, op1=ALU.add
                                                       ).then_inc(s["x_ready"], 1)

                def add_block(b):
                    dve.wait_ge(s["y_ready"], b + 1)
                    nc.vector.tensor_tensor(x[:, 4 * b:4 * b + 4, :],
                                            ps_y[:, b % 2, :].rearrange("p (t d) -> p t d", d=D),
                                            x[:, 4 * b:4 * b + 4, :], ALU.add).then_inc(s["x_ready"], 4)

                if not grouped:
                    blocks_of_experts(dve, n_exp, hidden, combine)
                else:
                    for b in range(4):
                        for f in range(nf):
                            m = b * nf + f
                            dve.wait_ge(s["act_ready"], m + 1)
                            if f == 0 and b >= 2:
                                dve.wait_ge(s["y_ready"], b - 1)
                            dve.wait_ge(s["u_ready"], m + 1)
                            h = hT[:, b % 2, f, :]
                            ins = nc.vector.tensor_tensor(h, sg[:, f % 2, :], ps_u[:, f % 2, :], ALU.mult)
                            if f < 4:
                                ins.then_inc(s["prod_ready"], 1)
                                dve.wait_ge(s["prod_ready"], 1 + 4 * b + f)
                                dve.wait_ge(s["c_ready"], 4 * b + f + 1)
                                ins = nc.vector.tensor_tensor(h, h, (ps_t if f % 2 else ps_r)[:, 0:512], ALU.mult)
                            ins.then_inc(s["h_ready"], 1)
                        if b:
                            add_block(b - 1)
                    add_block(3)

            @block.scalar
            def _(act):
                stats_on_scalar(act)
                if again:
                    stats2_on_scalar(act)
                for q in range(4):
                    act.wait_ge(s["xT_ps_ready"], q + 1)
                    if again:
                        nc.scalar.activation(xT[:, 512 * q:512 * q + 512], ps_t[:], ACT.Identity,
                                             bias=cols["beta"], scale=cols["gamma"]).then_inc(s["xT_ready"], 1)
                    else:
                        nc.scalar.copy(xT[:, 512 * q:512 * q + 512], ps_t[:]).then_inc(s["xT_ready"], 1)
                act.wait_ge(s["exp_in"], 1)
                nc.scalar.activation(W[5][:], W[5][:], ACT.Exp).then_inc(s["exp_out"], 1)
                if grouped:
                    for q in range(4):
                        act.wait_ge(s["gateT_ps_ready"], q + 1)
                        nc.scalar.copy(gateT[:, 512 * q:512 * q + 512], ps_t[0:E, :]).then_inc(s["gateT_ready"], 1)

                def hidden(b, e):
                    n = b * n_exp + e
                    for f in range(nf):
                        m = n * nf + f
                        if not silu and f % 2:
                            continue
                        act.wait_ge(s["g_ready"], m + 1)
                        if silu:
                            if not (isinstance(m, int) and m < 2):
                                act.wait_ge(s["h_ready"], m - 1)
                            nc.scalar.activation(sg[:, f % 2, :], ps_g[:, f % 2, :], ACT.Silu
                                                 ).then_inc(s["act_ready"], 1)
                        else:
                            if not (isinstance(n, int) and n < 2):
                                act.wait_ge(s["y_ready"], n - 1)
                            nc.scalar.activation(hT[:, e % 2, f, :], ps_g[:, f % 2, :], ACT.Relu
                                                 ).then_inc(s["act_ready"], 1)

                if grouped:
                    for b in range(4):
                        hidden(b, 0)
                else:
                    blocks_of_experts(act, n_exp, hidden, None)

            @block.tensor
            def _(pe):
                pe.wait_ge(weights_loaded, 16)
                for q in range(4):
                    if q >= 1:
                        pe.wait_ge(s["xT_ready"], q)
                    for k in range(4):
                        t = 4 * q + k
                        pe.wait_ge(s["xn_ready"], t + 1 + (NT if again else 0))
                        mm = nc.tensor.transpose(ps_t[:, P * k:P * k + P], xn[:, t, :], ident)
                    mm.then_inc(s["xT_ps_ready"], 1)
                for t in range(NT):
                    pe.wait_ge(s["xT_ready"], t // 4 + 1)
                    mm = nc.tensor.matmul(ps_r[:, E * t:E * t + E], xT[:, P * t:P * t + P], w_router,
                                          start=True, stop=True)
                mm.then_inc(s["logits_ready"], 1)
                if kind in ("capacity1", "capacity2"):
                    pe.wait_ge(s["sel_ready"], 1)
                    sel = W[1][:].rearrange("p t e -> p (t e)")
                    nc.tensor.matmul(ps_r[:, E8:2 * E8], c("tri"), sel, start=True, stop=True)
                    nc.tensor.matmul(ps_r[:, 2 * E8:3 * E8], c("ones"), sel, start=True, stop=True
                                     ).then_inc(s["ranks_ready"], 1)
                if grouped:
                    pe.wait_ge(s["gate_ready"], 1)
                    for q in range(4):
                        if q:
                            pe.wait_ge(s["gateT_ready"], q)
                        for k in range(4):
                            mm = nc.tensor.transpose(ps_t[0:E, P * k:P * k + P], W[1][:, 4 * q + k, :], ident)
                        mm.then_inc(s["gateT_ps_ready"], 1)
                    pe.wait_ge(s["gateT_ready"], 4)

                def up(b, e):
                    n = b * n_exp + e
                    tokens = xT[:, bass.ds(b * 512, 512)]
                    for f in range(nf):
                        m = n * nf + f
                        if not (isinstance(m, int) and m < 2):
                            if silu:
                                pe.wait_ge(s["act_ready"], m - 1)
                            elif f % 2:
                                pe.wait_ge(s["h_ready"], 2 * n + (f - 1) // 2)
                            else:
                                pe.wait_ge(s["act_ready"], 2 * n + f // 2)
                        nc.tensor.matmul(ps_g[:, f % 2, :], w_gate(e, f), tokens, start=True, stop=True
                                         ).then_inc(s["g_ready"], 1)
                        if silu:
                            if not (isinstance(m, int) and m < 2):
                                pe.wait_ge(s["h_ready"], m - 1)
                            nc.tensor.matmul(ps_u[:, f % 2, :], w_up(e, f), tokens, start=True, stop=True
                                             ).then_inc(s["u_ready"], 1)
                        if grouped and f < 4:
                            if b or f >= 2:
                                pe.wait_ge(s["h_ready"], b * nf + f - 1 if f >= 2 else b * nf - 4 + f + 1)
                            nc.tensor.matmul((ps_t if f % 2 else ps_r)[:, 0:512], c("spread")[0:E, P * f:P * f + P],
                                             gateT[:, 512 * b:512 * b + 512], start=True, stop=True
                                             ).then_inc(s["c_ready"], 1)

                def down(b, e):
                    n = b * n_exp + e
                    if silu:
                        pe.wait_ge(s["h_ready"], nf * (n + 1))
                    else:
                        pe.wait_ge(s["h_ready"], nf // 2 * (n + 1))
                        pe.wait_ge(s["act_ready"], nf // 2 * (n + 1))
                    if not (isinstance(n, int) and n < 2):
                        pe.wait_ge(s["x_ready"], 4 * (n - 1))
                    par = (b if n_exp == 1 else e) % 2
                    for k in range(4):
                        for f in range(nf):
                            mm = nc.tensor.matmul(ps_y[:, par, P * k:P * k + P], hT[:, par, f, P * k:P * k + P],
                                                  w_down(e, f), start=f == 0, stop=f == nf - 1)
                    mm.then_inc(s["y_ready"], 1)

                if grouped:
                    for b in range(4):
                        up(b, 0)
                        if b:
                            down(b - 1, 0)
                    down(3, 0)
                else:
                    blocks_of_experts(pe, n_exp, up, down)


def blocks_of_experts(eng, n_exp, ahead, behind):
    def turn(b, first):
        for e in range(n_exp):
            ahead(b, e)
            if behind is not None and not (first and e == 0):
                behind(*((b, e - 1) if e else (b - 1, n_exp - 1)))
    turn(0, True)
    with eng.Fori(1, 4, 1) as b:
        turn(b, False)
    if behind is not None:
        behind(3, n_exp - 1)


class Routing:

    def __init__(self, nc, dve, sem):
        self.nc, self.step = nc, Steps(dve, sem)

    def tt(self, out, a, b, op):
        self.step.then(self.nc.vector.tensor_tensor(out, a, b, op))

    def ts(self, out, a, s1, s2, op0, op1=ALU.bypass):
        self.step.then(self.nc.vector.tensor_scalar(out, a, s1, s2, op0, op1))

    def red(self, out, a, op=ALU.max):
        self.step.then(self.nc.vector.tensor_reduce(out, a, AX.X, op))

    def copy(self, out, a):
        self.step.then(self.nc.vector.tensor_copy(out, a))

    def reciprocal(self, out, a):
        self.step.then(self.nc.vector.reciprocal(out, a))

    def first_of_max(self, values, m, first, tmp, down):
        shape = list(values.shape)
        self.red(m, values)
        self.tt(first, values, m.unsqueeze(2).broadcast_to(shape), ALU.is_equal)
        self.tt(first, first, down, ALU.mult)
        self.red(tmp, first)
        self.tt(first, first, tmp.unsqueeze(2).broadcast_to(shape), ALU.is_equal)


class SplitProducts:

    def __init__(self, sb, tag, w_cols):
        self.w_hi, self.w_lo = (sb(f"{tag}_w_{n}", [P, w_cols], F32R) for n in ("hi", "lo"))
        self.x_hi, self.x_lo = (sb(f"{tag}_x_{n}", [P, NT * P], F32R) for n in ("hi", "lo"))

    @staticmethod
    def matmul(nc, out, lhs, rhs):
        (lh, ll), (rh, rl) = lhs, rhs
        nc.tensor.matmul(out, lh, rh, start=True, stop=False)
        nc.tensor.matmul(out, lh, rl, start=False, stop=False)
        return nc.tensor.matmul(out, ll, rh, start=False, stop=True)


def top2_experts(nc, tag, g, w_router, weights, weights_loaded):
    E, NF = 8, 2
    with stage(nc) as (stack, sems):
        sb, ps, sem = alloc(nc, stack, sems)
        x, c, ident = g["x"], g["c"], g["c"]("ident")
        mv, rstd, stats_on_vector, stats_on_scalar = norm_stats(nc, stack, sems, tag, x)
        xn = sb(f"{tag}_xn", [P, NT, D])
        xT = sb(f"{tag}_xT", [P, NT * P])
        sp3 = SplitProducts(sb, tag, 2 * E * NF * P)
        h = sb(f"{tag}_h", [P, 2, NF, 512])
        sg = sb(f"{tag}_sg", [P, 2, 512])
        lg = sb(f"{tag}_lg", [P, NT, E])
        gate = sb(f"{tag}_gate", [P, NT, E])
        first, second, work = (sb(f"{tag}_work{i}", [P, NT, E]) for i in range(3))
        M = [sb(f"{tag}_max{i}", [P, NT]) for i in range(4)]

        ps_g = ps(f"{tag}_ps_g", [P, 2, 512])
        ps_u = ps(f"{tag}_ps_u", [P, 2, 512])
        ps_y = ps(f"{tag}_ps_y", [P, 2, 512])
        ps_t = ps(f"{tag}_ps_t", [P, 512])
        ps_r = ps(f"{tag}_ps_r", [P, 512])

        names = ("xn_ready", "xT_ps_ready", "xT_ready", "x_hi_ready", "x_lo_ready", "w_hi_ready", "w_lo_ready",
                 "logits_ready", "step", "exp_in", "exp_out", "g_ready", "u_ready", "act_ready", "h_ready",
                 "y_ready", "x_ready")
        s = {n: sem(f"{tag}_{n}") for n in names}

        def of_expert(w, e):
            return w[:, 0:2 * E * NF * P].rearrange("p (k e n) -> p k e n", k=2, e=E)[:, :, e, :]

        def w_down(e, f):
            lo = (2 * E + e) * NF * P + f * P
            return weights[:, lo:lo + P]

        def w(k, e, f):
            lo = (k * E + e) * NF * P + f * P
            return sp3.w_hi[:, lo:lo + P], sp3.w_lo[:, lo:lo + P]

        def later(n, least):
            return not isinstance(n, int) or n >= least

        with nc.Block() as block:
            @block.vector
            def _(dve):
                r = Routing(nc, dve, s["step"])
                stats_on_vector(dve)
                for t in range(NT):
                    nc.vector.tensor_scalar(xn[:, t, :], x[:, t, :], mv[:, t, 0:1], rstd[:, t:t + 1],
                                            ALU.subtract, ALU.mult).then_inc(s["xn_ready"], 1)
                dve.wait_ge(s["logits_ready"], 1)
                full = [P, NT, E]

                def over(m):
                    return m.unsqueeze(2).broadcast_to(full)
                down = c("down8").unsqueeze(1).broadcast_to(full)
                r.copy(lg[:], ps_r[:, 0:NT * E].rearrange("p (t e) -> p t e", e=E))
                r.first_of_max(lg[:], M[0][:], first[:], M[3][:], down)
                r.ts(work[:], first[:], 2.0 * NEG, None, ALU.mult)
                r.tt(work[:], work[:], lg[:], ALU.add)
                r.first_of_max(work[:], M[1][:], second[:], M[3][:], down)
                nc.vector.tensor_tensor(M[1][:], M[1][:], M[0][:], ALU.subtract).then_inc(s["exp_in"], 1)
                dve.wait_ge(s["exp_out"], 1)
                r.ts(M[2][:], M[1][:], 1.0, None, ALU.add)
                r.reciprocal(M[2][:], M[2][:])
                r.tt(M[3][:], M[2][:], M[1][:], ALU.mult)
                r.tt(first[:], first[:], over(M[2][:]), ALU.mult)
                r.tt(second[:], second[:], over(M[3][:]), ALU.mult)
                r.tt(gate[:], first[:], second[:], ALU.add)

                def hidden(b, e):
                    n = b * E + e
                    for f in range(NF):
                        m = n * NF + f
                        dve.wait_ge(s["act_ready"], m + 1)
                        dve.wait_ge(s["u_ready"], m + 1)
                        if later(n, 2):
                            dve.wait_ge(s["y_ready"], n - 1)
                        nc.vector.tensor_tensor(h[:, e % 2, f, :], sg[:, f % 2, :], ps_u[:, f % 2, :], ALU.mult
                                                ).then_inc(s["h_ready"], 1)

                def combine(b, e):
                    n = b * E + e
                    dve.wait_ge(s["y_ready"], n + 1)
                    for k in range(4):
                        if later(n, 1):
                            dve.wait_ge(s["x_ready"], 4 * n + k - 3)
                        xt = x[:, bass.ds(4 * b + k, 1), :].rearrange("p a d -> p (a d)")
                        y = ps_y[:, e % 2, P * k:P * k + P]
                        gk = gate[:, bass.ds(4 * b + k, 1), e:e + 1].rearrange("p a b -> p (a b)")
                        nc.vector.scalar_tensor_tensor(out=xt, in0=y, scalar=gk, in1=xt, op0=ALU.mult, op1=ALU.add
                                                       ).then_inc(s["x_ready"], 1)
                blocks_of_experts(dve, E, hidden, combine)

            @block.gpsimd
            def _(pool):
                def split_weights(e):
                    pool.wait_ge(s["w_hi_ready"], e + 1)
                    nc.gpsimd.tensor_tensor(of_expert(sp3.w_lo[:], e), of_expert(weights, e), of_expert(sp3.w_hi[:], e),
                                            ALU.subtract).then_inc(s["w_lo_ready"], 1)
                for e in range(2):
                    split_weights(e)
                for q in range(4):
                    pool.wait_ge(s["xT_ready"], q + 1)
                    pool.wait_ge(s["x_hi_ready"], q + 1)
                    r = slice(512 * q, 512 * q + 512)
                    nc.gpsimd.tensor_tensor(sp3.x_lo[:, r], xT[:, r], sp3.x_hi[:, r], ALU.subtract
                                            ).then_inc(s["x_lo_ready"], 1)
                for e in range(2, E):
                    split_weights(e)

            @block.scalar
            def _(act):
                def round_weights(e):
                    nc.scalar.copy(of_expert(sp3.w_hi[:], e), of_expert(weights, e)).then_inc(s["w_hi_ready"], 1)
                act.wait_ge(weights_loaded, 16)
                for e in range(4):
                    round_weights(e)
                stats_on_scalar(act)
                for e in range(4, E):
                    round_weights(e)
                for q in range(4):
                    act.wait_ge(s["xT_ps_ready"], q + 1)
                    r = slice(512 * q, 512 * q + 512)
                    nc.scalar.copy(sp3.x_hi[:, r], ps_t[:]).then_inc(s["x_hi_ready"], 1)
                    nc.scalar.copy(xT[:, r], ps_t[:]).then_inc(s["xT_ready"], 1)
                act.wait_ge(s["exp_in"], 1)
                nc.scalar.activation(M[1][:], M[1][:], ACT.Exp).then_inc(s["exp_out"], 1)

                def hidden(b, e):
                    n = b * E + e
                    for f in range(NF):
                        m = n * NF + f
                        act.wait_ge(s["g_ready"], m + 1)
                        if later(m, 2):
                            act.wait_ge(s["h_ready"], m - 1)
                        nc.scalar.activation(sg[:, f % 2, :], ps_g[:, f % 2, :], ACT.Silu).then_inc(s["act_ready"], 1)
                blocks_of_experts(act, E, hidden, None)

            @block.tensor
            def _(pe):
                for q in range(4):
                    if q >= 1:
                        pe.wait_ge(s["xT_ready"], q)
                    for k in range(4):
                        t = 4 * q + k
                        pe.wait_ge(s["xn_ready"], t + 1)
                        mm = nc.tensor.transpose(ps_t[:, P * k:P * k + P], xn[:, t, :], ident)
                    mm.then_inc(s["xT_ps_ready"], 1)
                for t in range(NT):
                    pe.wait_ge(s["xT_ready"], t // 4 + 1)
                    mm = nc.tensor.matmul(ps_r[:, E * t:E * t + E], xT[:, P * t:P * t + P], w_router,
                                          start=True, stop=True)
                mm.then_inc(s["logits_ready"], 1)

                def up(b, e):
                    n = b * E + e
                    tokens = sp3.x_hi[:, bass.ds(b * 512, 512)], sp3.x_lo[:, bass.ds(b * 512, 512)]
                    if isinstance(b, int):
                        pe.wait_ge(s["w_lo_ready"], e + 1)
                        pe.wait_ge(s["x_lo_ready"], 1)
                    elif e == 0:
                        pe.wait_ge(s["x_lo_ready"], 4)
                    for f in range(NF):
                        m = n * NF + f
                        if later(m, 2):
                            pe.wait_ge(s["act_ready"], m - 1)
                        SplitProducts.matmul(nc, ps_g[:, f % 2, :], w(0, e, f), tokens).then_inc(s["g_ready"], 1)
                        if later(m, 2):
                            pe.wait_ge(s["h_ready"], m - 1)
                        SplitProducts.matmul(nc, ps_u[:, f % 2, :], w(1, e, f), tokens).then_inc(s["u_ready"], 1)

                def down(b, e):
                    n = b * E + e
                    pe.wait_ge(s["h_ready"], NF * (n + 1))
                    if later(n, 2):
                        pe.wait_ge(s["x_ready"], 4 * (n - 1))
                    for k in range(4):
                        for f in range(NF):
                            r = slice(P * k, P * k + P)
                            mm = nc.tensor.matmul(ps_y[:, e % 2, r], h[:, e % 2, f, r], w_down(e, f),
                                                  start=f == 0, stop=f == NF - 1)
                    mm.then_inc(s["y_ready"], 1)
                blocks_of_experts(pe, E, up, down)


def mlstm(nc, g, a, weights_free_arena, pe_rows, pe_rows_ready, gate_w, gate_row, ln_w, ln_b):
    NH, C = 8, 16
    XR = 4
    AHEAD = 4
    FLOOR_AT = 5
    SPLIT = 11
    with stage(nc) as (stack, sems):
        sb, ps, sem = alloc(nc, stack, sems)
        x, ctxT, c, ident = g["x"], g["ctxT"], g["c"], g["c"]("ident")
        arena = weights_free_arena
        mv, rstd, stats_on_vector, stats_on_scalar = norm_stats(nc, stack, sems, "l2a", x)
        qz = arena[:, 0:16384].rearrange("p (b h s) -> p b h s", b=2 * NT, h=NH)
        work = arena[:, 16384:20480].rearrange("p (k u n) -> p k u n", k=4, u=2)
        mb, dt, sc, cw = (work[:, k] for k in range(4))
        small = work[:, 3].rearrange("p u (k n) -> p (u k) n", k=4)
        khop = sb("l2a_khop", [P, NT, NH, S])
        xn = sb("l2a_xn", [P, 2, D])
        xT = sb("l2a_xT", [P, XR, P])
        pe_T = pe_rows[:].rearrange("p j d -> p (j d)")
        sums = pe_T[:, 0:NT * NH * (C + 1)].rearrange("p (t n) -> p t n", t=NT)
        gw_ctx = sb("l2a_gw_ctx", [P, 16])
        cum = sb("l2a_cum", [P, P])
        key_gate = sb("l2a_key_gate", [P, NT, NH])
        maxT = sb("l2a_maxT", [P, P])
        floor_ = sb("l2a_floor", [P, NT, NH])
        vb = sb("l2a_vb", [P, 2, NH, C + 1])
        norm = sb("l2a_norm", [P, NT, NH])
        var = sb("l2a_var", [P, NT, NH])
        rs = sb("l2a_rs", [P, NT, NH])
        sq = sb("l2a_sq", [P, 2, D])

        ps_a = ps("l2a_ps_a", [P, 2, 512])
        ps_k = ps("l2a_ps_k", [P, 2, 512])
        ps_g = ps("l2a_ps_g", [P, 512])
        ps_c = ps("l2a_ps_c", [P, 512])
        ps_x = ps("l2a_ps_x", [P, 2, 512])

        names = ("w_ready", "xn_ready", "xT_ps_ready", "q0_ready", "q1_ready", "xT_ready", "step", "act_in", "act_out",
                 "logf_ready", "cum_ready", "a_ready", "aT_ready", "maxT_ready", "max_ps_ready", "max_stored",
                 "peT_ps_ready", "peT_ready", "khop_ps_ready", "khop_ready", "shift_ready",
                 "s_ready", "m1_ready", "exp_ready", "sc_ready", "cw_ready", "o_ready", "sums_ready",
                 "chain", "cen_ready", "sq_ready", "var_ready", "root_ready", "rs_ready", "gained", "scaled0", "scaled1", "gates_done", "gate_mm")
        s = {n: sem(f"l2a_{n}") for n in names}
        tile_in = [sem(f"l2a_tile_in{k}") for k in range(2)]
        v_in = [sem(f"l2a_v_in{k}") for k in range(2)]
        scratch = nc.dram_tensor("max_scratch", (2, NT, NH, S), F32).ap()

        def spread_q(eng, k, b):
            return eng.tensor_tensor(
                qz[:, 2 * k + b], xT[:, k % XR, S * b:S * b + S].unsqueeze(1).broadcast_to([P, NH, S]),
                c("mask16").unsqueeze(2).broadcast_to([P, NH, S]), ALU.mult)

        def heads(tiles):
            return sums[:, tiles, :].rearrange("p t (h c) -> p t h c", h=NH)[:, :, :, 0:C]

        def add_heads(eng, ops, tiles, scaled):
            eng.wait_ge(s["rs_ready"], 1)
            n = tiles.stop - tiles.start
            y = heads(tiles)
            ops.tensor_tensor(y, y, rs[:, tiles, :].unsqueeze(3).broadcast_to([P, n, NH, C]), ALU.mult
                              ).then_inc(scaled, 1)
            eng.wait_ge(scaled, 1)
            xt = x[:, tiles, :].rearrange("p t (h c) -> p t h c", h=NH)
            ops.tensor_tensor(xt, xt, y, ALU.add).then_inc(scaled, 1)

        with nc.Block() as block:
            @block.sync
            def _(sp):
                def load_v(t, u):
                    sp.dma_start(vb[:, u].rearrange("p h c -> p (h c)"),
                                 a["ctx_one"][:, bass.ds(t, 1), :].rearrange("p a d -> p (a d)")
                                 ).then_inc(v_in[u], 16)
                for u in range(2):
                    load_v(u, u)
                sp.wait_ge(s["maxT_ready"], 2)
                sp.dma_start(scratch.rearrange("b t h s -> (t h) b s"),
                             maxT[:].rearrange("p (b s) -> p b s", b=2)).then_inc(s["max_stored"], 16)
                sp.wait_ge(s["max_stored"], 16)

                def body(t, u, edge):
                    if edge is None or t >= 2:
                        sp.wait_ge(s["m1_ready"], t - 1)
                    for b in range(2):
                        src = scratch[b, bass.ds(t, 1)].rearrange("a h s -> a (h s)").broadcast_to([S, NH * S])
                        sp.dma_start(mb[S * b:S * b + S, u, :], src).then_inc(tile_in[u], 16)
                    if edge is None or t >= 2:
                        sp.wait_ge(s["o_ready"], t - 1)
                        load_v(t, u)
                pipeline(sp, body, 0, NT)

            @block.gpsimd
            def _(pool):
                for k in range(NT):
                    pool.wait_ge(s["xT_ready"], k + 1)
                    spread_q(nc.gpsimd, k, 1).then_inc(s["q1_ready"], 1)
                pool.wait_ge(s["xn_ready"], NT)
                nc.gpsimd.tensor_tensor(x[:], x[:], ln_b.unsqueeze(1).broadcast_to([P, NT, D]), ALU.add
                                        ).then_inc(s["shift_ready"], 1)
                pool.wait_ge(s["shift_ready"], 1)
                pool.wait_ge(s["gates_done"], 1)

                def weights(t, u, edge):
                    pool.wait_ge(s["exp_ready"], t + 1)
                    pool.wait_ge(s["sc_ready"], t + 1)
                    if edge is None or t >= 2:
                        pool.wait_ge(s["o_ready"], t - 1)
                    nc.gpsimd.tensor_tensor(cw[:, u], sc[:, u], dt[:, u], ALU.mult).then_inc(s["cw_ready"], 1)

                def gain(t):
                    pool.wait_ge(s["var_ready"], t + 2)
                    y = heads(bass.ds(t, 2))
                    w = ln_w.rearrange("p (h c) -> p h c", h=NH).unsqueeze(1).broadcast_to([P, 2, NH, C])
                    nc.gpsimd.tensor_tensor(y, y, w, ALU.mult).then_inc(s["gained"], 2)

                def body(i, u, edge):
                    if edge is None or 1 <= i < NT + 1:
                        weights(i - 1, 1 - u, edge)
                    if u == 1 and (edge is None or i >= 5):
                        gain(i - 5)
                pipeline(pool, body, 0, NT + 4)
                pool.wait_ge(s["gained"], NT)
                add_heads(pool, nc.gpsimd, slice(SPLIT, NT), s["scaled1"])

            @block.vector
            def _(dve):
                step = Steps(dve, s["step"])
                nc.vector.tensor_tensor(gw_ctx[:], gate_w[:, 1, :], gate_w[:, 2, :], ALU.add).then_inc(s["w_ready"], 1)
                stats_on_vector(dve)
                for t in range(NT + 1):
                    if t < NT:
                        if t >= 2:
                            dve.wait_ge(s["xT_ps_ready"], t - 1)
                        nc.vector.tensor_scalar(xn[:, t % 2, :], x[:, t, :], mv[:, t, 0:1], rstd[:, t:t + 1],
                                                ALU.subtract, ALU.mult).then_inc(s["xn_ready"], 1)
                    if t >= 1:
                        dve.wait_ge(s["xT_ready"], t)
                        spread_q(nc.vector, t - 1, 0).then_inc(s["q0_ready"], 1)
                dve.wait_ge(s["gate_mm"], NT)
                gates = ps_g[:, 0:256].rearrange("p (t e) -> p t e", e=16)
                ig, fg, nab, ex, lf = (small[:, k].rearrange("p (t h) -> p t h", h=NH) for k in range(5))
                row = gate_row.unsqueeze(1)
                step.then(nc.vector.tensor_tensor(ig, gates[:, :, 0:8], row[:, :, 0:8].broadcast_to([P, NT, NH]), ALU.add))
                step.then(nc.vector.tensor_tensor(fg, gates[:, :, 8:16], row[:, :, 8:16].broadcast_to([P, NT, NH]),
                                                  ALU.add))
                nc.vector.scalar_tensor_tensor(out=nab, in0=fg, scalar=-1.0, in1=fg, op0=ALU.mult, op1=ALU.min
                                               ).then_inc(s["act_in"], 1)
                dve.wait_ge(s["act_out"], 2)
                nc.vector.scalar_tensor_tensor(out=lf, in0=fg, scalar=0.0, in1=ex, op0=ALU.min, op1=ALU.subtract
                                               ).then_inc(s["logf_ready"], 1)
                dve.wait_ge(s["cum_ready"], 1)
                step.then(nc.vector.tensor_copy(cum[:], ps_c[:, 0:P]))
                nc.vector.tensor_tensor(key_gate[:], ig, cum[:].rearrange("p (t h) -> p t h", h=NH), ALU.subtract
                                        ).then_inc(s["a_ready"], 1)
                dve.wait_ge(s["aT_ready"], 1)
                for b in range(2):
                    nc.vector.tensor_tensor_scan(maxT[:, S * b:S * b + S], c("ones")[:, 0:S],
                                                 ps_c[:, P + S * b:P + S * b + S], -3.0e38, ALU.mult, ALU.max
                                                 ).then_inc(s["maxT_ready"], 1)
                dve.wait_ge(s["max_ps_ready"], 1)
                nc.vector.tensor_tensor(floor_[:], ps_c[:, 2 * P:3 * P].rearrange("p (t h) -> p t h", h=NH),
                                        cum[:].rearrange("p (t h) -> p t h", h=NH), ALU.add).then_inc(s["act_in"], 1)
                dve.wait_ge(s["act_out"], 3)
                nc.vector.tensor_scalar(floor_[:], floor_[:], 1e-6, None, ALU.add).then_inc(s["gates_done"], 1)
                dve.wait_ge(s["gates_done"], 1)

                def mask_max(t, u, edge):
                    dve.wait_ge(tile_in[u], 16 * (t - u) + 32)
                    if edge is None or t >= 2:
                        dve.wait_ge(s["cw_ready"], t - 1)
                    nc.vector.tensor_tensor(dt[:, u].rearrange("p (h s) -> p h s", h=NH),
                                            mb[:, u].rearrange("p (h s) -> p h s", h=NH),
                                            c("later").unsqueeze(1).broadcast_to([P, NH, S]), ALU.add
                                            ).then_inc(s["m1_ready"], 1)

                def scores(t, u, edge):
                    dve.wait_ge(s["s_ready"], t + 1)
                    if edge is not None and t == 0:
                        dve.wait_ge(s["khop_ready"], 16)
                    kh = khop[:, bass.ds(t, 1)].rearrange("p a h s -> p (a h s)")
                    nc.vector.scalar_tensor_tensor(out=sc[:, u], in0=ps_a[:, u, :], scalar=0.25, in1=kh,
                                                   op0=ALU.mult, op1=ALU.add).then_inc(s["sc_ready"], 1)

                def divide(t):
                    n = [0]

                    def then(ins):
                        n[0] += 1
                        ins.then_inc(s["chain"], 2)
                        dve.wait_ge(s["chain"], 5 * t + 2 * n[0])
                    dve.wait_ge(s["sums_ready"], t + 2)
                    pair = bass.ds(t, 2)
                    total = sums[:, pair, :].rearrange("p t (h c) -> p t h c", h=NH)[:, :, :, C]
                    nr, h4 = norm[:, pair, :], heads(pair)
                    then(nc.vector.scalar_tensor_tensor(out=nr, in0=total, scalar=-1.0, in1=total,
                                                        op0=ALU.mult, op1=ALU.max))
                    then(nc.vector.scalar_tensor_tensor(out=nr, in0=nr, scalar=1e-6, in1=floor_[:, pair, :],
                                                        op0=ALU.add, op1=ALU.max))
                    then(nc.vector.reciprocal(nr, nr))
                    then(nc.vector.tensor_tensor(h4, h4, nr.unsqueeze(3).broadcast_to([P, 2, NH, C]), ALU.mult))
                    then(nc.vector.tensor_reduce(nr, h4, AX.X, ALU.add))

                def variance(t):
                    pair = bass.ds(t, 2)
                    nr, h4, q4 = norm[:, pair, :], heads(pair), sq[:].rearrange("p t (h c) -> p t h c", h=NH)
                    nc.vector.scalar_tensor_tensor(out=h4, in0=nr.unsqueeze(3).broadcast_to([P, 2, NH, C]),
                                                   scalar=-1.0 / C, in1=h4, op0=ALU.mult, op1=ALU.add
                                                   ).then_inc(s["cen_ready"], 2)
                    dve.wait_ge(s["cen_ready"], t + 2)
                    nc.vector.tensor_tensor(q4, h4, h4, ALU.mult).then_inc(s["sq_ready"], 2)
                    dve.wait_ge(s["sq_ready"], 2 * t + 2)
                    nc.vector.tensor_reduce(var[:, pair, :], q4, AX.X, ALU.add).then_inc(s["sq_ready"], 2)
                    dve.wait_ge(s["sq_ready"], 2 * t + 4)
                    nc.vector.tensor_scalar(var[:, pair, :], var[:, pair, :], 1.0 / C, 1e-5, ALU.mult, ALU.add
                                            ).then_inc(s["var_ready"], 2)

                def body(i, u, edge):
                    if edge is None or i < NT:
                        mask_max(i, u, edge)
                    if u == 0 and (edge is None or i >= 4):
                        variance(i - 4)
                    if edge is None or i < NT:
                        scores(i, u, edge)
                    if u == 1 and (edge is None or i >= 3):
                        divide(i - 3)
                pipeline(dve, body, 0, NT + 3)
                dve.wait_ge(s["root_ready"], 1)
                nc.vector.reciprocal(rs[:], rs[:]).then_inc(s["rs_ready"], 1)
                dve.wait_ge(s["gained"], NT)
                dve.wait_ge(s["shift_ready"], 1)
                add_heads(dve, nc.vector, slice(0, SPLIT), s["scaled0"])

            @block.scalar
            def _(act):
                def copy_peT(j):
                    act.wait_ge(s["peT_ps_ready"], j + 1)
                    nc.scalar.copy(pe_T[:, 256 * j:256 * j + 256], ps_a[:, j % 2, 0:4 * S]).then_inc(s["peT_ready"], 1)
                for j in range(AHEAD):
                    copy_peT(j)
                stats_on_scalar(act)
                for t in range(NT):
                    act.wait_ge(s["xT_ps_ready"], t + 1)
                    if t >= XR:
                        act.wait_ge(s["gate_mm"], t - XR + 1)
                        act.wait_ge(s["q0_ready"], t - XR + 1)
                        act.wait_ge(s["q1_ready"], t - XR + 1)
                    nc.scalar.copy(xT[:, t % XR, :], ps_x[:, t % 2, 0:P]).then_inc(s["xT_ready"], 1)
                    if t + AHEAD < 16:
                        copy_peT(t + AHEAD)
                nab, ex = small[:, 2], small[:, 3]
                act.wait_ge(s["act_in"], 1)
                nc.scalar.activation(ex, nab, ACT.Exp).then_inc(s["act_out"], 1)
                act.wait_ge(s["act_out"], 1)
                nc.scalar.activation(ex, ex, ACT.Ln, bias=1.0).then_inc(s["act_out"], 1)
                for j in range(16):
                    if j == FLOOR_AT:
                        act.wait_ge(s["act_in"], 2)
                        nc.scalar.activation(floor_[:], floor_[:], ACT.Exp, scale=-1.0).then_inc(s["act_out"], 1)
                    act.wait_ge(s["khop_ps_ready"], j + 1)
                    nc.scalar.copy(khop[:].rearrange("p t h v -> p v (t h)")[:, 4 * j:4 * j + 4, :],
                                   ps_k[:, j % 2, :].rearrange("p (v n) -> p v n", v=4)
                                   ).then_inc(s["khop_ready"], 1)

                def body(i, u, edge):
                    if edge is None or i < NT:
                        act.wait_ge(s["m1_ready"], i + 1)
                        for h in range(NH):
                            r = slice(S * h, S * h + S)
                            e = nc.scalar.activation(dt[:, u, r], dt[:, u, r], ACT.Exp, scale=-1.0,
                                                     bias=key_gate[:, bass.ds(i, 1), h:h + 1].rearrange("p a h -> p (a h)"))
                        e.then_inc(s["exp_ready"], 1)
                    if edge is None or 2 <= i < NT + 2:
                        act.wait_ge(s["o_ready"], i - 1)
                        nc.scalar.copy(sums[:, bass.ds(i - 2, 1), :].rearrange("p a n -> p (a n)"),
                                       ps_k[:, u, 0:NH * (C + 1)]).then_inc(s["sums_ready"], 1)
                pipeline(act, body, 0, NT + 2)
                act.wait_ge(s["var_ready"], NT)
                nc.scalar.activation(rs[:], var[:], ACT.Sqrt).then_inc(s["root_ready"], 1)

            @block.tensor
            def _(pe):
                pe.wait_ge(pe_rows_ready, 16 * 32)

                def turn_positions(j):
                    if j >= 2:
                        pe.wait_ge(s["peT_ready"], j - 1)
                    for k in range(2):
                        mm = nc.tensor.transpose(ps_a[:, j % 2, P * k:P * k + P], pe_rows[:, 2 * j + k, :], ident)
                    mm.then_inc(s["peT_ps_ready"], 1)
                for j in range(AHEAD):
                    turn_positions(j)
                pe.wait_ge(s["w_ready"], 1)

                def gate_mm(t):
                    pe.wait_ge(s["xT_ready"], t + 1)
                    dst = ps_g[:, 16 * t:16 * t + 16]
                    nc.tensor.matmul(dst, xT[:, t % XR, :], gate_w[:, 0, :], start=True, stop=False)
                    nc.tensor.matmul(dst, ctxT[:, P * t:P * t + P], gw_ctx[:], start=False, stop=True
                                     ).then_inc(s["gate_mm"], 1)
                for t in range(NT):
                    pe.wait_ge(s["xn_ready"], t + 1)
                    if t >= 2:
                        pe.wait_ge(s["xT_ready"], t - 1)
                    nc.tensor.transpose(ps_x[:, t % 2, 0:P], xn[:, t % 2, :], ident).then_inc(s["xT_ps_ready"], 1)
                    if t + AHEAD < 16:
                        turn_positions(t + AHEAD)
                    if t >= 1:
                        gate_mm(t - 1)
                gate_mm(NT - 1)

                def hop(j):
                    pe.wait_ge(s["peT_ready"], j + 1)
                    if j >= 2:
                        pe.wait_ge(s["khop_ready"], j - 1)
                    for v in range(4):
                        for b in range(2):
                            q = qz[:, b:2 * NT:2, :, 4 * j + v]
                            mm = nc.tensor.matmul(
                                ps_k[S * b:S * b + S, j % 2, P * v:P * v + P].rearrange("p (t h) -> p t h", h=NH),
                                pe_T[:, 4 * S * j + S * v:4 * S * j + S * v + S], q, start=True, stop=True)
                    mm.then_inc(s["khop_ps_ready"], 1)
                pe.wait_ge(s["q0_ready"], NT)
                pe.wait_ge(s["q1_ready"], NT)
                for j in range(16):
                    if j == 2:
                        pe.wait_ge(s["logf_ready"], 1)
                        nc.tensor.matmul(ps_c[:, 0:P], c("tri_seq"), small[:, 4], start=True, stop=True
                                         ).then_inc(s["cum_ready"], 1)
                    if j == 3:
                        pe.wait_ge(s["a_ready"], 1)
                        nc.tensor.transpose(ps_c[:, P:2 * P], key_gate[:].rearrange("p t h -> p (t h)"), ident
                                            ).then_inc(s["aT_ready"], 1)
                    if j == 4:
                        pe.wait_ge(s["maxT_ready"], 2)
                        nc.tensor.transpose(ps_c[:, 2 * P:3 * P], maxT[:], ident).then_inc(s["max_ps_ready"], 1)
                    hop(j)

                for t in range(NT + 1):
                    if t < NT:
                        if t >= 2:
                            pe.wait_ge(s["sc_ready"], t - 1)
                        for b in range(2):
                            mm = nc.tensor.matmul(ps_a[S * b:S * b + S, t % 2, :].rearrange("p (h s) -> p h s", h=NH),
                                                  ctxT[:, P * t + S * b:P * t + S * b + S], qz[:, 2 * t + b],
                                                  start=True, stop=True)
                        mm.then_inc(s["s_ready"], 1)
                    if t >= 1:
                        k = t - 1
                        pe.wait_ge(s["cw_ready"], k + 1)
                        pe.wait_ge(v_in[k % 2], 16 * (k // 2 + 1))
                        if k >= 2:
                            pe.wait_ge(s["sums_ready"], k - 1)
                        else:
                            pe.wait_ge(s["khop_ready"], 16)
                        for b in range(2):
                            r = slice(S * b, S * b + S)
                            for h in range(NH):
                                mm = nc.tensor.matmul(ps_k[r, k % 2, (C + 1) * h:(C + 1) * (h + 1)],
                                                      cw[r, k % 2, S * h:S * h + S], vb[r, k % 2, h, :],
                                                      start=True, stop=True)
                        mm.then_inc(s["o_ready"], 1)


ATT = ["L0_q", "L0_q_turned", "L0_k", "L0_k_turned", "L0_v", "L0_o", "L1_q", "L1_k", "L1_v", "L1_o",
       "L3_q", "L3_k", "L3_v", "L3_o"]
ROWS = ["L0_o", "L1_o", "L3_o"]
STOP = 8
L0_W, L1_W, L2_W, L3_W = 8192, 12288, 6144, 2304


def build(nc, a, out):
    with ExitStack() as stack:
        sb, ps, sem = alloc(nc, stack)
        g = {}
        x = g["x"] = sb("x", [P, NT, D])
        ctxT = g["ctxT"] = sb("ctxT", [P, NT * P])
        consts = sb("consts", [P, CONSTS.shape[1]])
        att_w = sb("att_w", [P, len(ATT), D])
        att_col = sb("att_col", [P, 19])
        rows = sb("rows", [1, len(ROWS), D])
        ident_bf = sb("ident_bf", [P, P], BF16)
        causal_bf = sb("causal_bf", [P, S], BF16)
        g["ident_bf"], g["causal_bf"] = ident_bf[:], causal_bf[:]
        loaded = sem("loaded")
        casts = sem("casts")
        stored = sem("stored")

        def c(name):
            lo, hi = CONST_COLS[name]
            return consts[:, lo:hi]
        g["c"] = c
        late_w = sb("late_w", [P, L2_W + L3_W])
        routers = sb("routers", [P, 8 + 8 + 8 + 16])
        gate_w = sb("gate_w", [P, 3, 16])
        gate_row = sb("gate_row", [P, 17, 16])
        expert_col = sb("expert_col", [P, 2 + 16])
        ffn_loaded = {n: sem(f"ffn_loaded_{n}") for n in ("L0", "L1", "L2", "L3")}

        slots_cleared = {n: sem(f"slots_cleared_{n}") for n in ("L0", "L1")}
        zeros_ready = sem("zeros_ready")
        l0_in, l0_out = (nc.dram_tensor(f"l0_slots_{n}", (8 * L0_CAP, D), F32).ap() for n in ("in", "out"))
        l1_in, l1_out = (nc.dram_tensor(f"l1_slots_{n}", (8 * L1_CAP, D), F32).ap() for n in ("in", "out"))
        hops = sb("hops", [P, 32], mybir.dt.int32)
        early = stack.enter_context(ExitStack())
        arena = early.enter_context(nc.sbuf_tensor("arena", [P, L0_W + L1_W], F32))
        pe_rows = early.enter_context(nc.sbuf_tensor("pe_rows", [P, 32, D], F32))
        zeros = pe_rows[:, 0:4, :].rearrange("p a d -> p (a d)")
        hops_ready, pe_rows_ready = sem("hops_ready"), sem("pe_rows_ready")

        with nc.Block() as block:
            @block.gpsimd
            def _(pool):
                nc.gpsimd.memset(zeros, 0.0).then_inc(zeros_ready, 1)

            @block.scalar
            def _(act):
                act.wait_ge(zeros_ready, 1)
                for n, dst, cap in (("L0", l0_in, L0_CAP), ("L1", l1_in, L1_CAP)):
                    blocks = 8 * cap * D // (P * 512)
                    act.dma_start(dst.rearrange("(p a r) d -> p a (r d)", p=P, a=blocks),
                                  zeros.unsqueeze(1).broadcast_to([P, blocks, 512])).then_inc(slots_cleared[n], 16)

            @block.sync
            def _(sp):
                for dst, src in ((consts, "consts"), (x, "x"), (ctxT, "ctxT"), (att_w, "att_w"),
                                 (att_col, "att_col"), (rows, "rows")):
                    sp.dma_start(dst[:], a[src]).then_inc(loaded, 16)
                sp.dma_start(routers[:], a["routers"]).then_inc(loaded, 16)
                sp.dma_start(expert_col[:], a["expert_col"]).then_inc(loaded, 16)
                sp.dma_start(gate_w[:], a["gate_w"]).then_inc(loaded, 16)
                sp.dma_start(gate_row[:], a["gate_row"]).then_inc(loaded, 16)
                sp.dma_start(hops[:], a["hops"]).then_inc(hops_ready, 16)
                sp.wait_ge(loaded, 16 * 10)
                for n, dst in (("L0", arena[:, 0:L0_W]), ("L1", arena[:, L0_W:L0_W + L1_W]),
                               ("L2", late_w[:, 0:L2_W]), ("L3", late_w[:, L2_W:L2_W + L3_W])):
                    sp.dma_start(dst, a[f"{n}_experts"]).then_inc(ffn_loaded[n], 16)

            @block.vector
            def _(dve):
                dve.wait_ge(loaded, 16 * 10)
                nc.vector.tensor_scalar(gate_row[:, 1:9, :], gate_row[:, 1:9, :], 1.0, None, ALU.add
                                        ).then_inc(casts, 1)
                nc.vector.tensor_copy(ident_bf[:], c("ident")).then_inc(casts, 1)
                nc.vector.tensor_copy(causal_bf[:], c("causal")).then_inc(casts, 1)
                dve.wait_ge(casts, 3)

        w = {n: att_w[:, i, :] for i, n in enumerate(ATT)}
        r = {n: rows[:, i, :] for i, n in enumerate(ROWS)}
        attention(nc, "l0a", g, (w["L0_q"], w["L0_q_turned"], w["L0_k"], w["L0_k_turned"], w["L0_v"], w["L0_o"]),
                  att_col[:, 0:8], att_col[:, 16:17], r["L0_o"], rope=True)

        def gather_positions(pool):
            pool.wait_ge(hops_ready, 16)
            for n in ("L0", "L1"):
                pool.wait_ge(slots_cleared[n], 16)
            for j in range(32):
                nc.gpsimd.indirect_dma_start(
                    out=pe_rows[:, j, :], out_offset=None, in_=a["rpe"],
                    in_offset=bass.IndirectOffsetOnAxis(ap=hops[:, j:j + 1], axis=0)
                    ).then_inc(pe_rows_ready, 16)

        l0w, l1w = arena[:, 0:L0_W], arena[:, L0_W:L0_W + L1_W]
        l2w, l3w = late_w[:, 0:L2_W], late_w[:, L2_W:L2_W + L3_W]

        if STOP >= 2:
            routed_experts(nc, "l0f", g, 1, L0_CAP, routers[:, 0:8],
                           lambda e, f: l0w[:, e * 512 + f * P:e * 512 + f * P + P], None,
                           lambda e, f: l0w[:, 4096 + (e * 4 + f) * P:4096 + (e * 4 + f) * P + P],
                           ffn_loaded["L0"], l0_in, l0_out, slots_cleared["L0"],
                           pe_rows[:, 16:32, :].rearrange("p a d -> p (a d)"))
        if STOP >= 3:
            attention(nc, "l1a", g, (w["L1_q"], None, w["L1_k"], None, w["L1_v"], w["L1_o"]),
                      att_col[:, 8:12], att_col[:, 17:18], r["L1_o"], rope=False)
        if STOP >= 4:
            routed_experts(nc, "l1f", g, 2, L1_CAP, routers[:, 8:16],
                           lambda e, f: l1w[:, e * 1024 + f * P:e * 1024 + f * P + P],
                           lambda e, f: l1w[:, e * 1024 + 512 + f * P:e * 1024 + 512 + f * P + P],
                           lambda e, f: l1w[:, 8192 + (e * 4 + f) * P:8192 + (e * 4 + f) * P + P],
                           ffn_loaded["L1"], l1_in, l1_out, slots_cleared["L1"],
                           l0w, norm_gain=expert_col[:, 0:1], norm_shift=expert_col[:, 1:2],
                           prefetch=gather_positions)
        if STOP >= 5:
            mlstm(nc, g, a, arena, pe_rows, pe_rows_ready, gate_w, gate_row[:, 0, :], gate_row[:, 1:9, :].rearrange("p a b -> p (a b)"),
                  gate_row[:, 9:17, :].rearrange("p a b -> p (a b)"))
        early.close()
        if STOP >= 6:
            top2_experts(nc, "l2f", g, routers[:, 16:24], l2w, ffn_loaded["L2"])
        if STOP >= 7:
            attention(nc, "l3a", g, (w["L3_q"], None, w["L3_k"], None, w["L3_v"], w["L3_o"]),
                      att_col[:, 12:16], att_col[:, 18:19], r["L3_o"], rope=False)
        if STOP >= 8:
            experts(nc, "l3f", g, "grouped", 1, 6, 16, routers[:, 24:40],
                    lambda e, f: l3w[:, f * P:f * P + P],
                    lambda e, f: l3w[:, 768 + f * P:768 + f * P + P],
                    lambda e, f: l3w[:, 1536 + f * P:1536 + f * P + P],
                    ffn_loaded["L3"], cols={"bias": expert_col[:, 2:18]})

        with nc.Block() as block:
            @block.sync
            def _(sp):
                sp.dma_start(out, x[:]).then_inc(stored, 16)
                sp.wait_ge(stored, 16)


def kernel(**inputs):
    import concourse.bacc as bacc
    from concourse.bass_utils import run_bass_kernel_spmd

    def two_halves(v):
        return np.concatenate([v.reshape(G, S).T] * 2, 0)

    v = {k: np.asarray(w) for k, w in inputs.items()}
    turn = (np.arange(D) // DH) * DH + (np.arange(D) + DH // 2) % DH
    att = {"L0_q": v["L0_xattn_q_w"].T, "L0_q_turned": v["L0_xattn_q_w"][turn].T,
           "L0_k": v["L0_xattn_k_w"].T, "L0_k_turned": v["L0_xattn_k_w"][turn].T,
           "L0_v": v["L0_xattn_v_w"].T, "L0_o": v["L0_xattn_o_w"].T,
           "L1_q": v["L1_xattn_w_q"].T, "L1_k": v["L1_xattn_w_k"].T, "L1_v": v["L1_xattn_w_v"].T,
           "L1_o": v["L1_xattn_w_o"].T, "L3_q": v["L3_xattn_Wq"], "L3_k": v["L3_xattn_Wk"],
           "L3_v": v["L3_xattn_Wv"], "L3_o": v["L3_xattn_Wo"]}
    arrays = {
        "consts": CONSTS,
        "x": v["x"].reshape(NT, P, D).transpose(1, 0, 2),
        "ctxT": v["ctx_1024"].reshape(NT * P, D).T,
        "att_w": np.stack([att[n] for n in ATT], 1),
        "att_col": np.concatenate([two_halves(w) for w in (
            v["L0_xattn_q_b"], v["L0_xattn_q_b"][turn], v["L0_xattn_k_b"], v["L0_xattn_k_b"][turn],
            v["L1_xattn_b_q"], v["L1_xattn_b_k"], v["L3_xattn_bq"], v["L3_xattn_bk"])]
            + [v[n][:, None] for n in ("L0_xattn_v_b", "L1_xattn_b_v", "L3_xattn_bv")], 1),
        "rows": np.stack([v["L0_xattn_o_b"], v["L1_xattn_b_o"], v["L3_xattn_bo"]])[None],
    }

    def wide(w):
        return w.transpose(1, 0, 2).reshape(w.shape[1], -1)

    def tall(w):
        e, f, d = w.shape
        return w.reshape(e, f // P, P, d).transpose(2, 0, 1, 3).reshape(P, -1)

    arrays["L0_experts"] = np.concatenate([wide(v["L0_ffn_W1"]), tall(v["L0_ffn_W2"])], 1)
    arrays["L1_experts"] = np.concatenate([wide(v["L1_ffn_W12"].transpose(0, 2, 1)),
                                           tall(v["L1_ffn_W3"].transpose(0, 2, 1))], 1)
    arrays["L2_experts"] = np.concatenate([wide(v["L2_ffn_w1"]), wide(v["L2_ffn_w3"]), tall(v["L2_ffn_w2"])], 1)
    arrays["L3_experts"] = np.concatenate([
        wide(v["L3_ffn_gate_w"]), v["L3_ffn_shared_gate_w"].T, wide(v["L3_ffn_up_w"]), v["L3_ffn_shared_up_w"].T,
        tall(v["L3_ffn_down_w"].reshape(1, 512, D)), tall(v["L3_ffn_shared_down_w"].T[None])], 1)
    arrays["routers"] = np.concatenate([v["L0_ffn_Wr"], v["L1_ffn_Wr"].T, v["L2_ffn_w_gate"],
                                        v["L3_ffn_router_w"].T], 1)
    arrays["ctx_one"] = np.concatenate([v["ctx_1024"].reshape(NT, P, 8, 16), np.ones((NT, P, 8, 1), np.float32)],
                                       3).transpose(1, 0, 2, 3).reshape(P, NT, 8 * 17)
    arrays["rpe"] = v["L2_xattn_rpe"]
    arrays["hops"] = v["itok_SxS2_0_2016"].reshape(32, P).T
    arrays["gate_w"] = np.concatenate([v["L2_xattn_igate_w"], v["L2_xattn_fgate_w"]]).reshape(16, 3, P).transpose(2, 1, 0)
    arrays["gate_row"] = np.broadcast_to(np.concatenate([
        v["L2_xattn_igate_b"], v["L2_xattn_fgate_b"], v["L2_xattn_ln_w"], v["L2_xattn_ln_b"]]
        ).reshape(17, 16), (P, 17, 16))
    arrays["expert_col"] = np.concatenate([
        v["L1_ffn_ln_gamma"][:, None], v["L1_ffn_ln_beta"][:, None],
        np.broadcast_to(v["L3_ffn_correction_bias"], (P, 16))], 1)
    nc = bacc.Bacc("TRN2", target_bir_lowering=False, num_devices=1)
    dram = {}
    for name, arr in list(arrays.items()):
        arrays[f"in_{name}"] = arr = np.ascontiguousarray(arrays.pop(name))
        dram[name] = nc.dram_tensor(f"in_{name}", arr.shape, mybir.dt.from_np(arr.dtype), kind="ExternalInput").ap()
    out = nc.dram_tensor("out", (P, NT, D), F32, kind="ExternalOutput").ap()
    build(nc, dram, out)
    result = run_bass_kernel_spmd(nc, [arrays], core_ids=[0]).results[0]["out"]
    return np.ascontiguousarray(result.transpose(1, 0, 2)).reshape(2 * NT, S, D)
```

```python
from contextlib import ExitStack, contextmanager

import numpy as np
import concourse.bass as bass
from concourse import mybir

F32 = mybir.dt.float32
BF16 = mybir.dt.bfloat16
F32R = mybir.dt.float32r
ALU = mybir.AluOpType
ACT = mybir.ActivationFunctionType
AX = mybir.AxisListType

P = 128
D = 128
S = 64
NT = 16
H = 16
DH = D // H
G = 2
HG = H // G
NEG = -1.0e30
L0_CAP = int(1.25 * NT * P / 8)
L1_CAP = -(-int(np.ceil(NT * P * 2 * 1.25)) // 8)

CONST_COLS = {}


def host_constants():
    p = np.arange(P)
    parts = []

    def add(name, a):
        a = np.asarray(a, np.float32).reshape(P, -1)
        start = sum(x.shape[1] for x in parts)
        CONST_COLS[name] = (start, start + a.shape[1])
        parts.append(a)

    add("ident", np.eye(P))
    add("ones", np.ones((P, P)))
    add("tri", p[:, None] <= p[None, :])
    seq = p // S
    add("tri_seq", (p[:, None] <= p[None, :]) & (seq[:, None] == seq[None, :]))
    add("causal", np.where(np.arange(S)[None, :] <= (p % S)[:, None], 0.0, NEG))
    add("head_mask", ((p % S) // DH)[:, None] == np.arange(HG)[None, :])
    add("pair_mask", (p // S)[:, None] == np.arange(2)[None, :])
    half = DH // 2
    freqs = (1.0 / np.float32(10000.0) ** (np.arange(half, dtype=np.float32) / np.float32(half))).astype(np.float32)
    dim = (p % DH)
    ang = (np.arange(S, dtype=np.float32)[None, :] * freqs[dim % half][:, None]).astype(np.float32)
    cos, sin = np.cos(ang), np.sin(ang) * np.where(dim < half, -1.0, 1.0)[:, None]
    add("rope", np.stack([cos, cos, sin, sin, cos, cos, sin, sin], 1))
    add("down8", np.broadcast_to(8.0 - np.arange(8), (P, 8)))
    add("down16", np.broadcast_to(16.0 - np.arange(16), (P, 16)))
    add("down4", np.broadcast_to(4.0 - np.arange(4), (P, 4)))
    for cap in (L0_CAP, L1_CAP):
        add(f"first_slot{cap}", np.broadcast_to(np.arange(8.0) * cap - 1.0, (P, 8)))
    add("mask16", (p // 16)[:, None] == np.arange(8)[None, :])
    add("later", np.where((p % S)[:, None] <= np.arange(S)[None, :], 0.0, -NEG))
    r = np.zeros((P, 4, P))
    for q in range(4):
        for e in range(4):
            r[4 * q + e, q, 32 * e:32 * e + 32] = 1
    add("spread", r)
    return np.concatenate(parts, 1)


CONSTS = host_constants()


def alloc(nc, stack, sems=None):
    def sb(name, shape, dt=F32):
        return stack.enter_context(nc.sbuf_tensor(name, shape, dt))

    def ps(name, shape, dt=F32):
        return stack.enter_context(nc.psum_tensor(name, shape, dt))

    def sem(name):
        if sems is None:
            return stack.enter_context(nc.semaphore(name))
        sems.append(nc.alloc_semaphore(name))
        return sems[-1]
    return sb, ps, sem


@contextmanager
def stage(nc):
    sems = []
    with ExitStack() as stack:
        yield stack, sems
    nc.clear_and_free_semaphores(sems)
    nc.all_engine_barrier()


def pipeline(eng, body, first, last, peel=4):
    head = 6 if last > NT + 2 else peel
    tail = NT if (NT - head) % 2 == 0 else NT - 1
    for i in range(first, head):
        body(i, i % 2, i)
    with eng.Fori(head, tail - 1, 2) as i:
        for u in range(2):
            body(i + u, u, None)
    for i in range(tail, last):
        body(i, i % 2, i)


def norm_stats(nc, stack, sems, tag, stats, twice=False):
    sb, ps, sem = alloc(nc, stack, sems)
    mv = sb(f"{tag}_mv", [P, NT, 2])
    std = sb(f"{tag}_std", [P, NT])
    rstd = sb(f"{tag}_rstd", [P, NT])
    mv_ready = sem(f"{tag}_mv_ready")
    std_ready, rstd_ready = sem(f"{tag}_std_ready"), sem(f"{tag}_rstd_ready")

    def on_vector(dve):
        for t in range(NT):
            nc.vector.bn_aggr(mv[:, t, :], stats[:, t, :]).then_inc(mv_ready, 1)
        dve.wait_ge(mv_ready, NT)
        nc.vector.tensor_scalar(std[:], mv[:, :, 1], 1e-5, None, ALU.add).then_inc(mv_ready, 1)
        dve.wait_ge(std_ready, 1)
        nc.vector.reciprocal(rstd[:], std[:]).then_inc(rstd_ready, 1)
        dve.wait_ge(rstd_ready, 1)
        if twice:
            nc.vector.tensor_tensor(std[:], mv[:, :, 1], rstd[:], ALU.mult).then_inc(rstd_ready, 1)
            dve.wait_ge(rstd_ready, 2)
            nc.vector.tensor_tensor(std[:], std[:], rstd[:], ALU.mult).then_inc(rstd_ready, 1)
            dve.wait_ge(rstd_ready, 3)
            nc.vector.tensor_scalar(std[:], std[:], 1e-5, None, ALU.add).then_inc(mv_ready, 1)
            dve.wait_ge(std_ready, 2)
            nc.vector.reciprocal(std[:], std[:]).then_inc(rstd_ready, 1)
            dve.wait_ge(rstd_ready, 4)
            nc.vector.tensor_tensor(rstd[:], rstd[:], std[:], ALU.mult).then_inc(rstd_ready, 1)
            dve.wait_ge(rstd_ready, 5)

    def on_scalar(act):
        for k in range(1 + twice):
            act.wait_ge(mv_ready, NT + 1 + k)
            nc.scalar.activation(std[:], std[:], ACT.Sqrt).then_inc(std_ready, 1)

    return mv, rstd, on_vector, on_scalar


def attention(nc, tag, g, weights, cols, vcol, orow, rope):
    with stage(nc) as (stack, sems):
        sb, ps, sem = alloc(nc, stack, sems)
        x, ctxT, c, ident = g["x"], g["ctxT"], g["c"], g["c"]("ident")
        ones_row = c("ones")[0:1, :]
        wq, wqr, wk, wkr, wv, wo = weights
        mv, rstd, stats_on_vector, stats_on_scalar = norm_stats(nc, stack, sems, tag, g["stats"])
        scale = float(DH) ** -0.5

        xn = sb(f"{tag}_xn", [P, 2, D])
        xnT = sb(f"{tag}_xnT", [P, 2, P])
        ctx2 = sb(f"{tag}_ctx2", [P, 2, 2, 2, S])
        qk = sb(f"{tag}_qk", [P, 2, 8, S]) if rope else None
        qkr = sb(f"{tag}_qkr", [P, 2, 8, S]) if rope else None
        qb = sb(f"{tag}_qb", [P, 2, G, P])
        kT = sb(f"{tag}_kT", [P, 2, G, S])
        km = sb(f"{tag}_km", [P, 2, G, HG, S])
        vb = sb(f"{tag}_vb", [P, 2, H // 2, 2, 2, DH + 1])
        mx = sb(f"{tag}_mx", [P, 2, H])
        pr = sb(f"{tag}_pr", [P, 2, G, HG, S])
        prT = sb(f"{tag}_prT", [P, 2, H // 2, P])
        rec = sb(f"{tag}_rec", [P, 2, H // 2, 2])
        o = sb(f"{tag}_o", [P, 2, D])
        oT = sb(f"{tag}_oT", [P, 2, P])
        vcols = sb(f"{tag}_vcols", [P, P])
        ybias = sb(f"{tag}_ybias", [P, D])

        ps_s = ps(f"{tag}_ps_s", [P, G, 512])
        ps_t = ps(f"{tag}_ps_t", [P, G, 512])
        ps_qk = ps(f"{tag}_ps_qk", [P, 8, S])
        ps_mix = ps(f"{tag}_ps_mix", [P, 512])
        ps_o = ps(f"{tag}_ps_o", [P, 512])
        ps_y = ps(f"{tag}_ps_y", [P, 512])
        V, XT, OT, O = ps_mix[:, 0:2 * D], ps_mix[:, 256:384], ps_mix[:, 384:512], ps_o[:, 0:288]

        names = ("cleared", "ctx_ready", "xn_ready", "xT_ready", "qk_ready", "biased", "turned",
                 "q_ready", "k_ready", "km_ready", "s_ready", "max_ready", "sub_ready", "exp_ready",
                 "pT_ready", "prT_ready", "mix_ready", "mix_taken", "o_ready", "rec_ready", "on_ready",
                 "y_ready", "x_ready", "ybias_ps_ready", "ybias_ready", "x_biased")
        s = {n: sem(f"{tag}_{n}") for n in names}

        def live(edge, t):
            return edge is None or 0 <= t < NT

        with nc.Block() as block:
            @block.vector
            def _(dve):
                nc.vector.tensor_copy(vcols[:], vcol.broadcast_to([P, P])).then_inc(s["cleared"], 1)
                nc.vector.memset(qb[:], 0.0).then_inc(s["cleared"], 1)
                for u in range(2):
                    for b in range(2):
                        nc.vector.tensor_copy(vb[:, u, :, b, :, DH],
                                              c("pair_mask").unsqueeze(1).broadcast_to([P, H // 2, 2])
                                              ).then_inc(s["cleared"], 1)
                stats_on_vector(dve)
                dve.wait_ge(s["ybias_ps_ready"], 1)
                nc.vector.tensor_copy(ybias[:], ps_y[:, 0:D]).then_inc(s["ybias_ready"], 1)
                dve.wait_ge(s["cleared"], 6)

                def normalise(t, u, edge):
                    if edge is None or t >= 2:
                        dve.wait_ge(s["mix_ready"], t - 1)
                    m = mv[:, bass.ds(t, 1), 0:1].rearrange("p a b -> p (a b)")
                    nc.vector.tensor_scalar(xn[:, u, :], x[:, bass.ds(t, 1), :].rearrange("p a d -> p (a d)"),
                                            m, rstd[:, bass.ds(t, 1)], ALU.subtract, ALU.mult
                                            ).then_inc(s["xn_ready"], 1)

                def bias_qk(t, u, edge):
                    dve.wait_ge(s["qk_ready"], t + 1)
                    nc.vector.tensor_tensor(qk[:, u], ps_qk[:], cols.unsqueeze(2).broadcast_to([P, 8, S]),
                                            ALU.add).then_inc(s["biased"], 1)

                def spread_qk(t, u, edge):
                    if edge is None or t >= 2:
                        dve.wait_ge(s["s_ready"], 2 * t - 2)
                        dve.wait_ge(s["km_ready"], 2 * t - 2)
                    if rope:
                        dve.wait_ge(s["turned"], t + 1)
                        a, b, ka, kb = (qkr[:, u, 2 * i:2 * i + 2, :] for i in range(4))
                    else:
                        dve.wait_ge(s["qk_ready"], t + 1)
                        a, ka = ps_qk[:, 0:2, :], ps_qk[:, 2:4, :]
                        b = cols[:, 0:2].unsqueeze(2).broadcast_to([P, 2, S])
                        kb = cols[:, 2:4].unsqueeze(2).broadcast_to([P, 2, S])
                    nc.vector.tensor_tensor(kT[:, u], ka, kb, ALU.add).then_inc(s["k_ready"], 1)
                    for n in range(2):
                        r = slice(S * n, S * n + S)
                        nc.vector.tensor_tensor(qb[r, u, :, r], a[r], b[r], ALU.add).then_inc(s["q_ready"], 1)

                def softmax_shift(t, u, edge, k):
                    dve.wait_ge(s["s_ready"], 2 * t + k + 1)
                    sc = ps_s[:, k, :].rearrange("p (h k) -> p h k", k=S)
                    m = mx[:, u, HG * k:HG * k + HG]
                    nc.vector.tensor_reduce(m, sc, AX.X, ALU.max).then_inc(s["max_ready"], 1)
                    dve.wait_ge(s["max_ready"], 2 * t + k + 1)
                    if edge is None or t >= 2:
                        dve.wait_ge(s["pT_ready"], 2 * t + k - 3)
                    nc.vector.tensor_tensor(pr[:, u, k], sc, m.unsqueeze(2).broadcast_to([P, HG, S]),
                                            ALU.subtract).then_inc(s["sub_ready"], 1)

                def normalise_o(t, u, edge):
                    dve.wait_ge(s["o_ready"], t + 1)
                    for b in range(2):
                        r = slice(S * b, S * b + S)
                        ob = O[r].rearrange("p (a b h d) -> p a b h d", a=8, b=2, h=2)[:, :, b]
                        nc.vector.reciprocal(rec[r, u], ob[:, :, :, DH]).then_inc(s["rec_ready"], 1)
                    for b in range(2):
                        r = slice(S * b, S * b + S)
                        ob = O[r].rearrange("p (a b h d) -> p a b h d", a=8, b=2, h=2)[:, :, b]
                        dve.wait_ge(s["rec_ready"], 2 * t + b + 1)
                        nc.vector.tensor_tensor(
                            o[r, u, :].rearrange("p (a h d) -> p a h d", h=2, d=DH), ob[:, :, :, 0:DH],
                            rec[r, u].unsqueeze(3).broadcast_to([S, H // 2, 2, DH]),
                            ALU.mult).then_inc(s["on_ready"], 1)

                def take_stats(t):
                    dve.wait_ge(s["x_ready"], t + 1)
                    nc.vector.bn_stats(g["stats"][:, bass.ds(t, 1), :].rearrange("p a d -> p (a d)"),
                                       x[:, bass.ds(t, 1), :].rearrange("p a d -> p (a d)"))

                def residual(t, u, edge):
                    dve.wait_ge(s["y_ready"], t + 1)
                    dve.wait_ge(s["x_biased"], t + 1)
                    if edge is None or t >= 1:
                        take_stats(t - 1)
                    xt = x[:, bass.ds(t, 1), :].rearrange("p a d -> p (a d)")
                    nc.vector.tensor_tensor(xt, ps_y[:, 0:D], xt, ALU.add).then_inc(s["x_ready"], 1)

                def body(i, u, edge):
                    if rope and live(edge, i - 1):
                        bias_qk(i - 1, 1 - u, edge)
                    if live(edge, i):
                        normalise(i, u, edge)
                    if not rope and live(edge, i - 1):
                        spread_qk(i - 1, 1 - u, edge)
                    if live(edge, i - 2):
                        softmax_shift(i - 2, u, edge, 0)
                    if rope and live(edge, i - 1):
                        spread_qk(i - 1, 1 - u, edge)
                    if live(edge, i - 2):
                        softmax_shift(i - 2, u, edge, 1)
                    if live(edge, i - 3):
                        normalise_o(i - 3, 1 - u, edge)
                    if live(edge, i - 4):
                        residual(i - 4, u, edge)
                pipeline(dve, body, 0, NT + 4)
                take_stats(NT - 1)

            @block.gpsimd
            def _(pool):
                pool.wait_ge(s["ybias_ready"], 1)

                def body(i, u, edge):
                    if live(edge, i - 1):
                        t, v = i - 1, 1 - u
                        if rope:
                            pool.wait_ge(s["biased"], t + 1)
                            nc.gpsimd.tensor_tensor(qkr[:, v], qk[:, v], c("rope").rearrange("p (a s) -> p a s", a=8),
                                                    ALU.mult).then_inc(s["turned"], 1)
                        pool.wait_ge(s["k_ready"], t + 1)
                        if edge is None or t >= 2:
                            pool.wait_ge(s["s_ready"], 2 * t - 2)
                        for k in range(G):
                            nc.gpsimd.tensor_tensor(km[:, v, k], kT[:, v, k].unsqueeze(1).broadcast_to([P, HG, S]),
                                                    c("head_mask").unsqueeze(2).broadcast_to([P, HG, S]), ALU.mult
                                                    ).then_inc(s["km_ready"], 1)
                    if live(edge, i):
                        pool.wait_ge(s["xn_ready"], i + 1)
                        xt = x[:, bass.ds(i, 1), :].rearrange("p a d -> p (a d)")
                        nc.gpsimd.tensor_tensor(xt, xt, ybias[:], ALU.add).then_inc(s["x_biased"], 1)
                pipeline(pool, body, 0, NT + 1, peel=6)

            @block.scalar
            def _(act):
                stats_on_scalar(act)

                def body(i, u, edge):
                    if live(edge, i - 3):
                        t, v = i - 3, 1 - u
                        for k in range(G):
                            act.wait_ge(s["pT_ready"], 2 * t + k + 1)
                            if edge is None or t >= 2:
                                act.wait_ge(s["o_ready"], t - 1)
                            nc.scalar.copy(prT[:, v, 4 * k:4 * k + 4, :],
                                           ps_t[:, k, :].rearrange("p (a q) -> p a q", a=4)
                                           ).then_inc(s["prT_ready"], 1)
                    if live(edge, i - 2):
                        exponential(i - 2, u, 0)
                    act.wait_ge(s["mix_ready"], i + 1)
                    n = 0
                    if live(edge, i - 4):
                        if edge is None or i >= 6:
                            act.wait_ge(s["y_ready"], i - 5)
                        nc.scalar.copy(oT[:, u, :], OT).then_inc(s["mix_taken"], 1)
                        n += 1
                    if live(edge, i):
                        if edge is None or i >= 2:
                            act.wait_ge(s["qk_ready"], i - 1)
                        nc.scalar.copy(xnT[:, u, :], XT).then_inc(s["mix_taken"], 1)
                        n += 1
                    if live(edge, i - 2):
                        if edge is None or i >= 4:
                            act.wait_ge(s["o_ready"], i - 3)
                        for h in range(2):
                            nc.scalar.activation(vb[:, u, :, :, h, 0:DH].rearrange("p a b d -> p b a d"),
                                                 V.rearrange("p (b a h d) -> p b a h d", b=2, h=2, d=DH)[:, :, :, h],
                                                 ACT.Copy, scale=c("pair_mask")[:, h:h + 1]
                                                 ).then_inc(s["mix_taken"], 1)
                            n += 1
                    if n < 4:
                        act.sem_inc(s["mix_taken"], 4 - n)
                    if live(edge, i):
                        nc.scalar.copy(ctx2[:, u], ctxT[:, bass.ds(i * P, P)].rearrange("p (b k) -> p b k", b=2)
                                       .unsqueeze(2).broadcast_to([P, 2, 2, S])).then_inc(s["ctx_ready"], 1)
                    if live(edge, i - 2):
                        exponential(i - 2, u, 1)

                def exponential(t, u, k):
                    act.wait_ge(s["sub_ready"], 2 * t + k + 1)
                    nc.scalar.activation(pr[:, u, k], pr[:, u, k], ACT.Exp, scale=scale).then_inc(s["exp_ready"], 1)
                pipeline(act, body, 0, NT + 4)

            @block.tensor
            def _(pe):
                pe.wait_ge(s["cleared"], 6)
                nc.tensor.matmul(ps_y[:, 0:D], vcols[:], wo, start=True, stop=False)
                nc.tensor.matmul(ps_y[:, 0:D], ones_row, orow, start=False, stop=True
                                 ).then_inc(s["ybias_ps_ready"], 1)

                def project(t, u, edge):
                    pe.wait_ge(s["mix_taken"], 4 * t + 4)
                    pe.wait_ge(s["ctx_ready"], t + 1)
                    if edge is None or t >= 1:
                        if rope:
                            pe.wait_ge(s["biased"], t)
                        else:
                            pe.wait_ge(s["q_ready"], 2 * t)
                            pe.wait_ge(s["k_ready"], t)
                    n = 0
                    for w, is_key in ((wq, False), (wqr, False), (wk, True), (wkr, True)):
                        if w is None:
                            continue
                        for k in range(G):
                            for b in range(2):
                                rhs = ctx2[:, u, b, 0] if is_key else xnT[:, u, S * b:S * b + S]
                                mm = nc.tensor.matmul(ps_qk[S * b:S * b + S, n, :], w[:, S * k:S * k + S], rhs,
                                                      start=True, stop=True)
                            n += 1
                    mm.then_inc(s["qk_ready"], 1)

                def scores(t, u, edge, k):
                    pe.wait_ge(s["q_ready"], 2 * t + 2)
                    pe.wait_ge(s["km_ready"], 2 * t + k + 1)
                    if edge is None or t >= 1:
                        pe.wait_ge(s["sub_ready"], 2 * t + k - 1)
                    if rope:
                        nc.tensor.matmul(ps_s[:, k, :].rearrange("p (h k) -> p h k", k=S), g["ident_bf"],
                                         g["causal_bf"].unsqueeze(1).broadcast_to([P, HG, S]),
                                         start=True, stop=False)
                    nc.tensor.matmul(ps_s[:, k, :].rearrange("p (h k) -> p h k", k=S), qb[:, u, k, :],
                                     km[:, u, k], start=not rope, stop=True).then_inc(s["s_ready"], 1)

                def prob_transpose(t, u, edge):
                    for k in range(G):
                        pe.wait_ge(s["exp_ready"], 2 * t + k + 1)
                        if edge is None or t >= 1:
                            pe.wait_ge(s["prT_ready"], 2 * t + k - 1)
                        flat = pr[:, u, k].rearrange("p h k -> p (h k)")
                        for a in range(4):
                            mm = nc.tensor.transpose(ps_t[:, k, P * a:P * a + P], flat[:, P * a:P * a + P], ident)
                        mm.then_inc(s["pT_ready"], 1)

                def mix(i, u, edge):
                    if edge is None or i >= 1:
                        pe.wait_ge(s["mix_taken"], 4 * i)
                    mm = None
                    if live(edge, i - 2):
                        for b in range(2):
                            mm = nc.tensor.matmul(V[:, b * D:b * D + D], ctx2[:, u, b].rearrange("p a k -> p (a k)"),
                                                  wv, start=True, stop=True)
                    if live(edge, i):
                        pe.wait_ge(s["xn_ready"], i + 1)
                        mm = nc.tensor.transpose(XT, xn[:, u, :], ident)
                    if live(edge, i - 4):
                        pe.wait_ge(s["on_ready"], 2 * (i - 4) + 2)
                        mm = nc.tensor.transpose(OT, o[:, u, :], ident)
                    if mm is None:
                        pe.sem_inc(s["mix_ready"], 1)
                    else:
                        mm.then_inc(s["mix_ready"], 1)

                def weigh(t, u, edge):
                    pe.wait_ge(s["prT_ready"], 2 * t + 2)
                    if edge is None or t >= 1:
                        pe.wait_ge(s["on_ready"], 2 * t)
                    for a in range(H // 2):
                        mm = nc.tensor.matmul(O[:, 36 * a:36 * a + 36], prT[:, u, a, :],
                                              vb[:, u, a].rearrange("p b h d -> p (b h d)"), start=True, stop=True)
                    mm.then_inc(s["o_ready"], 1)

                def out_project(t, u, edge):
                    pe.wait_ge(s["mix_taken"], 4 * t + 20)
                    if edge is None or t >= 1:
                        pe.wait_ge(s["x_ready"], t)
                    else:
                        pe.wait_ge(s["ybias_ready"], 1)
                    nc.tensor.matmul(ps_y[:, 0:D], oT[:, u, :], wo, start=True, stop=True).then_inc(s["y_ready"], 1)

                def body(i, u, edge):
                    if live(edge, i - 1):
                        project(i - 1, 1 - u, edge)
                    if live(edge, i - 2):
                        scores(i - 2, u, edge, 0)
                    if live(edge, i - 3):
                        prob_transpose(i - 3, 1 - u, edge)
                    if live(edge, i - 2):
                        scores(i - 2, u, edge, 1)
                    mix(i, u, edge)
                    if live(edge, i - 3):
                        weigh(i - 3, 1 - u, edge)
                    if live(edge, i - 4):
                        out_project(i - 4, u, edge)
                pipeline(pe, body, 0, NT + 4)


class Steps:

    def __init__(self, eng, sem):
        self.eng, self.sem, self.n = eng, sem, 0

    def then(self, instruction):
        self.n += 1
        instruction.then_inc(self.sem, 1)
        self.eng.wait_ge(self.sem, self.n)


def routed_experts(nc, tag, g, choices, cap, w_router, w_gate, w_up, w_down, weights_loaded, slots_in, slots_out,
                   slots_cleared, spare, norm_gain=None, norm_shift=None, prefetch=None, handed_over=None):
    with stage(nc) as (stack, sems):
        sb, ps, sem = alloc(nc, stack, sems)
        x, c, ident = g["x"], g["c"], g["c"]("ident")
        E, E8, NF, CH = 8, NT * 8, 4, 320
        chunks = E * cap // CH
        again = norm_gain is not None
        swish = w_up is not None
        bounds = E * cap - 1
        mv, rstd, stats_on_vector, stats_on_scalar = norm_stats(nc, stack, sems, tag, g["stats"], twice=again)
        xn = sb(f"{tag}_xn", [P, NT, D])
        xT = sb(f"{tag}_xT", [P, NT * P])
        rows = sb(f"{tag}_rows", [P, 2, 3, D])
        rT = sb(f"{tag}_rT", [P, 2, CH])
        hT = sb(f"{tag}_hT", [P, 2, NF, CH])
        sg = sb(f"{tag}_sg", [P, 2, CH])
        y = sb(f"{tag}_y", [P, 2, 3, D])
        lg = sb(f"{tag}_lg", [P, NT, E])
        W = [sb(f"{tag}_work{i}", [P, NT, E]) for i in range(7)]
        M = [sb(f"{tag}_max{i}", [P, NT]) for i in range(4)]
        if handed_over is None:
            gates = [sb(f"{tag}_gate{k}", [P, NT]) for k in range(choices)]
            slot = [sb(f"{tag}_slot{k}", [P, NT], mybir.dt.int32) for k in range(choices)]
            back = [spare[:, NT * D * k:NT * D * (k + 1)].rearrange("p (t d) -> p t d", t=NT)
                    for k in range(choices)]
        else:
            gates, slot = handed_over

        ps_g = ps(f"{tag}_ps_g", [P, 2, 512])
        ps_u = ps(f"{tag}_ps_u", [P, 2, 512])
        ps_y = ps(f"{tag}_ps_y", [P, 2, 512])
        ps_t = ps(f"{tag}_ps_t", [P, 2, 512])
        ps_r = ps_g[:, 0, :]

        names = ("cleared", "xn_ready", "xT_ps_ready", "xT_ready", "logits_ready", "step", "exp_in", "exp_out",
                 "sel_ready", "ranks_ready", "slots_ready", "sent", "rT_ps_ready", "rT_ready", "g_ready", "u_ready",
                 "act_ready", "h_ready", "y_ps_ready", "y_ready", "x_ready")
        s = {n: sem(f"{tag}_{n}") for n in names}
        rows_in = [sem(f"{tag}_rows_in{u}") for u in range(2)]
        y_out = [sem(f"{tag}_y_out{u}") for u in range(2)]
        fetched = [sem(f"{tag}_fetched{t}") for t in range(4)]

        def loop_chunks(eng, body, lag=0):
            for ch in range(4):
                body(ch, ch % 2, ch)
            with eng.Fori(4, chunks - 1, 2) as ch:
                for u in range(2):
                    body(ch + u, u, None)
            for ch in range(chunks, chunks + lag):
                body(ch, ch % 2, ch)

        def live(edge, ch):
            return edge is None or 0 <= ch < chunks

        with nc.Block() as block:
            @block.sync
            def _(sp):
                sp.wait_ge(s["sent"], 16 * NT * choices)

                def load(ch, u):
                    part = slots_in[bass.ds(ch * CH, CH), :]
                    sp.dma_start(rows[:, u, 0:2, :], part[0:256, :].rearrange("(a p) d -> p a d", p=P)
                                 ).then_inc(rows_in[u], 16)
                    sp.dma_start(rows[0:64, u, 2, :], part[256:CH, :]).then_inc(rows_in[u], 16)

                def body(ch, u, edge):
                    if live(edge, ch):
                        if edge is None or ch >= 2:
                            sp.wait_ge(s["rT_ps_ready"], ch - 1)
                        load(ch, u)
                loop_chunks(sp, body)

            @block.gpsimd
            def _(pool):
                if handed_over is None:
                    for k in range(choices):
                        nc.gpsimd.memset(back[k][:], 0.0).then_inc(s["cleared"], 1)
                if prefetch is not None:
                    prefetch(pool)
                pool.wait_ge(slots_cleared, 16)
                pool.wait_ge(s["xn_ready"], NT)
                for k in range(choices):
                    pool.wait_ge(s["slots_ready"], k + 1)
                    for t in range(NT):
                        nc.gpsimd.indirect_dma_start(
                            out=slots_in, out_offset=bass.IndirectOffsetOnAxis(ap=slot[k][:, t:t + 1], axis=0),
                            in_=xn[:, t, :], in_offset=None, bounds_check=bounds, oob_is_err=False
                            ).then_inc(s["sent"], 16)
                def store(ch, u, edge):
                    pool.wait_ge(s["y_ready"], ch + 1)
                    part = slots_out[bass.ds(ch * CH, CH), :]
                    nc.gpsimd.dma_start(part[0:256, :].rearrange("(a p) d -> p a d", p=P), y[:, u, 0:2, :]
                                        ).then_inc(y_out[u], 16)
                    nc.gpsimd.dma_start(part[256:CH, :], y[0:64, u, 2, :]).then_inc(y_out[u], 16)
                loop_chunks(pool, store)
                for u in range(2):
                    pool.wait_ge(y_out[u], 32 * (chunks // 2))
                if handed_over is not None:
                    return
                pool.wait_ge(s["cleared"], choices)
                for t in range(NT):
                    for k in range(choices):
                        nc.gpsimd.indirect_dma_start(
                            out=back[k][:, t, :], out_offset=None, in_=slots_out,
                            in_offset=bass.IndirectOffsetOnAxis(ap=slot[k][:, t:t + 1], axis=0),
                            bounds_check=bounds, oob_is_err=False).then_inc(fetched[t // 4], 16)

            @block.vector
            def _(dve):
                step = Steps(dve, s["step"])
                stats_on_vector(dve)
                for t in range(NT):
                    nc.vector.tensor_scalar(xn[:, t, :], x[:, t, :], mv[:, t, 0:1], rstd[:, t:t + 1],
                                            ALU.subtract, ALU.mult).then_inc(s["xn_ready"], 1)
                dve.wait_ge(s["logits_ready"], 1)
                logits = ps_r[:, 0:E8].rearrange("p (t e) -> p t e", e=E)
                full = [P, NT, E]

                def over(m):
                    return m.unsqueeze(2).broadcast_to(full)

                def per_expert(name):
                    return c(name).unsqueeze(1).broadcast_to(full)

                def tt(out, a, b, op):
                    step.then(nc.vector.tensor_tensor(out, a, b, op))

                def ts(out, a, s1, s2, op0, op1=ALU.bypass):
                    step.then(nc.vector.tensor_scalar(out, a, s1, s2, op0, op1))

                def red(out, a, op=ALU.max):
                    step.then(nc.vector.tensor_reduce(out, a, AX.X, op))

                def first_of_max(values, m, first, tmp):
                    red(m, values)
                    tt(first, values, over(m), ALU.is_equal)
                    tt(first, first, per_expert("down8"), ALU.mult)
                    red(tmp, first)
                    tt(first, first, over(tmp), ALU.is_equal)

                lo, ex, chosen, ranks = lg[:], W[5][:], W[2][:], W[4][:]
                first = [W[0][:], W[1][:]]
                if again:
                    ts(lo, logits, 10000.0, -10000.0, ALU.min, ALU.max)
                else:
                    step.then(nc.vector.tensor_copy(lo, logits))
                red(M[0][:], lo)
                nc.vector.tensor_tensor(ex, lo, over(M[0][:]), ALU.subtract).then_inc(s["exp_in"], 1)
                dve.wait_ge(s["exp_out"], 1)
                if choices == 1:
                    first_of_max(lo, M[2][:], first[0], M[3][:])
                    sel = first[0]
                else:
                    first_of_max(ex, M[2][:], first[0], M[3][:])
                    ts(first[1], first[0], -2.0, None, ALU.mult)
                    tt(W[3][:], first[1], ex, ALU.add)
                    first_of_max(W[3][:], M[2][:], first[1], M[3][:])
                    sel = chosen
                    tt(chosen, first[0], first[1], ALU.add)
                nc.vector.tensor_copy(W[6][:], sel).then_inc(s["sel_ready"], 1)
                red(M[1][:], ex, ALU.add)
                if choices == 2:
                    ts(M[1][:], M[1][:], 1e-12, None, ALU.add)
                step.then(nc.vector.reciprocal(M[1][:], M[1][:]))
                dve.wait_ge(s["ranks_ready"], 1)
                by_expert = lambda a: a.rearrange("p t e -> p (t e)").rearrange("p (e t) -> p e t", t=NT)
                flat = lambda a: a.rearrange("p t e -> p (t e)")
                tot, run, keep = W[2][:], W[3][:], W[6][:]
                step.then(nc.vector.tensor_copy(by_expert(tot), ps_r[:, 2 * E8:3 * E8].rearrange("p (t e) -> p e t", e=E)))
                step.then(nc.vector.memset(keep, 1.0))
                step.then(nc.vector.memset(by_expert(keep)[:, :, 0:1], 0.0))
                step.then(nc.vector.tensor_tensor_scan(flat(run), flat(keep), flat(tot), 0.0, ALU.mult, ALU.add))
                tt(run, run, tot, ALU.subtract)
                tt(ranks, ps_r[:, E8:2 * E8].rearrange("p (t e) -> p t e", e=E),
                   flat(run).rearrange("p (e t) -> p t e", t=NT), ALU.add)
                ts(W[2][:], ranks, float(cap), None, ALU.is_le)
                tt(ranks, ranks, per_expert(f"first_slot{cap}"), ALU.add)
                tt(W[3][:], ex, over(M[1][:]), ALU.mult)
                for k in range(choices):
                    tt(W[6][:], first[k], W[2][:], ALU.mult)
                    red(M[2][:], W[6][:], ALU.add)
                    tt(W[6][:], W[6][:], W[3][:], ALU.mult)
                    red(gates[k][:], W[6][:], ALU.add)
                    tt(W[6][:], first[k], ranks, ALU.mult)
                    red(M[0][:], W[6][:], ALU.add)
                    ts(M[3][:], M[2][:], -1.0e6, 1.0e6, ALU.mult, ALU.add)
                    tt(M[0][:], M[0][:], M[3][:], ALU.add)
                    nc.vector.tensor_copy(slot[k][:], M[0][:]).then_inc(s["slots_ready"], 1)
                    dve.wait_ge(s["slots_ready"], k + 1)
                if choices == 1:
                    ts(M[2][:], M[2][:], -1.0, 1.0, ALU.mult, ALU.add)
                    for t in range(NT):
                        nc.vector.scalar_tensor_tensor(out=x[:, t, :], in0=xn[:, t, :], scalar=M[2][:, t:t + 1],
                                                       in1=x[:, t, :], op0=ALU.mult, op1=ALU.add
                                                       ).then_inc(s["x_ready"], 1)
                    dve.wait_ge(s["x_ready"], NT)

                def body(ch, u, edge):
                    if live(edge, ch):
                        for f in range(NF):
                            if swish:
                                dve.wait_ge(s["act_ready"], NF * ch + f + 1)
                                dve.wait_ge(s["u_ready"], NF * ch + f + 1)
                            elif f % 2:
                                dve.wait_ge(s["g_ready"], NF * ch + f + 1)
                            else:
                                continue
                            if f < 2 and (edge is None or ch >= 2):
                                dve.wait_ge(s["y_ps_ready"], ch - 1)
                            if swish:
                                ins = nc.vector.tensor_tensor(hT[:, u, f, :], sg[:, f % 2, :], ps_u[:, f % 2, 0:CH],
                                                              ALU.mult)
                            else:
                                ins = nc.vector.tensor_scalar(hT[:, u, f, :], ps_g[:, f % 2, 0:CH], 0.0, None, ALU.max)
                            ins.then_inc(s["h_ready"], 1)
                    if live(edge, ch - 1):
                        v = 1 - u
                        dve.wait_ge(s["y_ps_ready"], ch)
                        if edge is None or ch >= 3:
                            dve.wait_ge(y_out[v], 16 * (ch - 1 - v))
                        nc.vector.tensor_copy(y[:, v, 0:2, :], ps_y[:, v, 0:256].rearrange("p (a d) -> p a d", a=2))
                        nc.vector.tensor_copy(y[0:64, v, 2, :], ps_y[0:64, v, 256:384]).then_inc(s["y_ready"], 1)
                loop_chunks(dve, body, 1)
                if handed_over is not None:
                    return
                base = NT if choices == 1 else 0

                def take_stats(t):
                    dve.wait_ge(s["x_ready"], base + choices * (t + 1))
                    nc.vector.bn_stats(g["stats"][:, t, :], x[:, t, :])
                for t in range(NT):
                    dve.wait_ge(fetched[t // 4], 16 * choices * 4)
                    for k in range(choices):
                        if k:
                            dve.wait_ge(s["x_ready"], base + choices * t + k)
                        nc.vector.scalar_tensor_tensor(out=x[:, t, :], in0=back[k][:, t, :], scalar=gates[k][:, t:t + 1],
                                                       in1=x[:, t, :], op0=ALU.mult, op1=ALU.add
                                                       ).then_inc(s["x_ready"], 1)
                    if t:
                        take_stats(t - 1)
                take_stats(NT - 1)

            @block.scalar
            def _(act):
                stats_on_scalar(act)
                for q in range(4):
                    act.wait_ge(s["xT_ps_ready"], q + 1)
                    if again:
                        nc.scalar.activation(xT[:, 512 * q:512 * q + 512], ps_t[:, q % 2, :], ACT.Identity,
                                             bias=norm_shift, scale=norm_gain).then_inc(s["xT_ready"], 1)
                    else:
                        nc.scalar.copy(xT[:, 512 * q:512 * q + 512], ps_t[:, q % 2, :]).then_inc(s["xT_ready"], 1)
                act.wait_ge(s["exp_in"], 1)
                nc.scalar.activation(W[5][:], W[5][:], ACT.Exp).then_inc(s["exp_out"], 1)

                def body(ch, u, edge):
                    if live(edge, ch):
                        act.wait_ge(s["rT_ps_ready"], ch + 1)
                        if edge is None or ch >= 2:
                            act.wait_ge(s["g_ready"], NF * (ch - 1))
                            if swish:
                                act.wait_ge(s["u_ready"], NF * (ch - 1))
                        if again:
                            nc.scalar.activation(rT[:, u, :], ps_t[:, u, 0:CH], ACT.Identity, bias=norm_shift,
                                                 scale=norm_gain).then_inc(s["rT_ready"], 1)
                        else:
                            nc.scalar.copy(rT[:, u, :], ps_t[:, u, 0:CH]).then_inc(s["rT_ready"], 1)
                    if live(edge, ch - 1):
                        t, v = ch - 1, 1 - u
                        for f in range(0, NF, 1 if swish else 2):
                            m = NF * t + f
                            act.wait_ge(s["g_ready"], m + 1)
                            if swish:
                                if edge is None or m >= 2:
                                    act.wait_ge(s["h_ready"], m - 1)
                                nc.scalar.activation(sg[:, f % 2, :], ps_g[:, f % 2, 0:CH], ACT.Silu
                                                     ).then_inc(s["act_ready"], 1)
                            else:
                                if f == 0 and (edge is None or t >= 2):
                                    act.wait_ge(s["y_ps_ready"], t - 1)
                                nc.scalar.activation(hT[:, v, f, :], ps_g[:, f % 2, 0:CH], ACT.Relu
                                                     ).then_inc(s["act_ready"], 1)
                loop_chunks(act, body, 1)

            @block.tensor
            def _(pe):
                pe.wait_ge(weights_loaded, 16)
                for q in range(4):
                    if q >= 2:
                        pe.wait_ge(s["xT_ready"], q - 1)
                    for k in range(4):
                        t = 4 * q + k
                        pe.wait_ge(s["xn_ready"], t + 1)
                        mm = nc.tensor.transpose(ps_t[:, q % 2, P * k:P * k + P], xn[:, t, :], ident)
                    mm.then_inc(s["xT_ps_ready"], 1)
                for t in range(NT):
                    pe.wait_ge(s["xT_ready"], t // 4 + 1)
                    mm = nc.tensor.matmul(ps_r[:, E * t:E * t + E], xT[:, P * t:P * t + P], w_router,
                                          start=True, stop=True)
                mm.then_inc(s["logits_ready"], 1)
                pe.wait_ge(s["sel_ready"], 1)
                sel = W[6][:].rearrange("p t e -> p (t e)")
                nc.tensor.matmul(ps_r[:, E8:2 * E8], c("tri"), sel, start=True, stop=True)
                nc.tensor.matmul(ps_r[:, 2 * E8:3 * E8], c("ones"), sel, start=True, stop=True
                                 ).then_inc(s["ranks_ready"], 1)
                pe.wait_ge(s["slots_ready"], choices)

                def turn(ch):
                    pe.wait_ge(rows_in[ch % 2], 32 * (ch // 2 + 1))
                    if ch >= 2:
                        pe.wait_ge(s["rT_ready"], ch - 1)
                    for a in range(3):
                        n = P if a < 2 else 64
                        mm = nc.tensor.transpose(ps_t[:, ch % 2, P * a:P * a + n], rows[0:n, ch % 2, a, :],
                                                 ident[0:n, 0:n])
                    mm.then_inc(s["rT_ps_ready"], 1)

                def up(ch):
                    e = ch * CH // cap
                    pe.wait_ge(s["rT_ready"], ch + 1)
                    for f in range(NF):
                        m = NF * ch + f
                        if m >= 2:
                            if swish:
                                pe.wait_ge(s["act_ready"], m - 1)
                            elif f % 2:
                                pe.wait_ge(s["h_ready"], 2 * ch + (f - 1) // 2)
                            else:
                                pe.wait_ge(s["act_ready"], 2 * ch + f // 2)
                        nc.tensor.matmul(ps_g[:, f % 2, 0:CH], w_gate(e, f), rT[:, ch % 2, :], start=True, stop=True
                                         ).then_inc(s["g_ready"], 1)
                        if swish:
                            if m >= 2:
                                pe.wait_ge(s["h_ready"], m - 1)
                            nc.tensor.matmul(ps_u[:, f % 2, 0:CH], w_up(e, f), rT[:, ch % 2, :], start=True, stop=True
                                             ).then_inc(s["u_ready"], 1)

                def down(ch):
                    e = ch * CH // cap
                    pe.wait_ge(s["h_ready"], (NF if swish else NF // 2) * (ch + 1))
                    if not swish:
                        pe.wait_ge(s["act_ready"], NF // 2 * (ch + 1))
                    if ch >= 2:
                        pe.wait_ge(s["y_ready"], ch - 1)
                    for a in range(3):
                        n = P if a < 2 else 64
                        for f in range(NF):
                            mm = nc.tensor.matmul(ps_y[0:n, ch % 2, P * a:P * a + P],
                                                  hT[:, ch % 2, f, P * a:P * a + n], w_down(e, f),
                                                  start=f == 0, stop=f == NF - 1)
                    mm.then_inc(s["y_ps_ready"], 1)

                turn(0)
                for ch in range(chunks):
                    if ch + 1 < chunks:
                        turn(ch + 1)
                    up(ch)
                    if ch:
                        down(ch - 1)
                down(chunks - 1)


def blocks_of_experts(eng, n_exp, ahead, behind):
    def turn(b, first):
        for e in range(n_exp):
            ahead(b, e)
            if behind is not None and not (first and e == 0):
                behind(*((b, e - 1) if e else (b - 1, n_exp - 1)))
    turn(0, True)
    with eng.Fori(1, 4, 1) as b:
        turn(b, False)
    if behind is not None:
        behind(3, n_exp - 1)


class Routing:

    def __init__(self, nc, dve, sem):
        self.nc, self.step = nc, Steps(dve, sem)

    def tt(self, out, a, b, op):
        self.step.then(self.nc.vector.tensor_tensor(out, a, b, op))

    def ts(self, out, a, s1, s2, op0, op1=ALU.bypass):
        self.step.then(self.nc.vector.tensor_scalar(out, a, s1, s2, op0, op1))

    def red(self, out, a, op=ALU.max):
        self.step.then(self.nc.vector.tensor_reduce(out, a, AX.X, op))

    def copy(self, out, a):
        self.step.then(self.nc.vector.tensor_copy(out, a))

    def reciprocal(self, out, a):
        self.step.then(self.nc.vector.reciprocal(out, a))

    def first_of_max(self, values, m, first, tmp, down):
        shape = list(values.shape)
        self.red(m, values)
        self.tt(first, values, m.unsqueeze(2).broadcast_to(shape), ALU.is_equal)
        self.tt(first, first, down, ALU.mult)
        self.red(tmp, first)
        self.tt(first, first, tmp.unsqueeze(2).broadcast_to(shape), ALU.is_equal)


class SplitProducts:

    def __init__(self, sb, tag, w_cols):
        self.w_hi, self.w_lo = (sb(f"{tag}_w_{n}", [P, w_cols], F32R) for n in ("hi", "lo"))
        self.x_hi, self.x_lo = (sb(f"{tag}_x_{n}", [P, NT * P], F32R) for n in ("hi", "lo"))

    @staticmethod
    def matmul(nc, out, lhs, rhs):
        (lh, ll), (rh, rl) = lhs, rhs
        nc.tensor.matmul(out, lh, rh, start=True, stop=False)
        nc.tensor.matmul(out, lh, rl, start=False, stop=False)
        return nc.tensor.matmul(out, ll, rh, start=False, stop=True)


def top2_experts(nc, tag, g, w_router, weights, weights_loaded):
    E, NF = 8, 2
    with stage(nc) as (stack, sems):
        sb, ps, sem = alloc(nc, stack, sems)
        x, c, ident = g["x"], g["c"], g["c"]("ident")
        mv, rstd, stats_on_vector, stats_on_scalar = norm_stats(nc, stack, sems, tag, g["stats"])
        xn = sb(f"{tag}_xn", [P, NT, D])
        xT = sb(f"{tag}_xT", [P, NT * P])
        split = SplitProducts(sb, tag, 2 * E * NF * P)
        h = sb(f"{tag}_h", [P, 2, NF, 512])
        sg = sb(f"{tag}_sg", [P, 2, 512])
        lg = sb(f"{tag}_lg", [P, NT, E])
        gate = sb(f"{tag}_gate", [P, NT, E])
        first, second, work = (sb(f"{tag}_work{i}", [P, NT, E]) for i in range(3))
        M = [sb(f"{tag}_max{i}", [P, NT]) for i in range(4)]

        ps_g = ps(f"{tag}_ps_g", [P, 2, 512])
        ps_u = ps(f"{tag}_ps_u", [P, 2, 512])
        ps_y = ps(f"{tag}_ps_y", [P, 2, 512])
        ps_t = ps(f"{tag}_ps_t", [P, 512])
        ps_r = ps(f"{tag}_ps_r", [P, 512])

        names = ("xn_ready", "xT_ps_ready", "xT_ready", "x_hi_ready", "x_lo_ready", "w_hi_ready", "w_lo_ready",
                 "logits_ready", "step", "exp_in", "exp_out", "g_ready", "u_ready", "act_ready", "h_ready",
                 "y_ready", "x_ready")
        s = {n: sem(f"{tag}_{n}") for n in names}

        def of_expert(w, e):
            return w[:, 0:2 * E * NF * P].rearrange("p (k e n) -> p k e n", k=2, e=E)[:, :, e, :]

        def w_down(e, f):
            lo = (2 * E + e) * NF * P + f * P
            return weights[:, lo:lo + P]

        def w(k, e, f):
            lo = (k * E + e) * NF * P + f * P
            return split.w_hi[:, lo:lo + P], split.w_lo[:, lo:lo + P]

        def later(n, least):
            return not isinstance(n, int) or n >= least

        with nc.Block() as block:
            @block.vector
            def _(dve):
                r = Routing(nc, dve, s["step"])
                stats_on_vector(dve)
                for t in range(NT):
                    nc.vector.tensor_scalar(xn[:, t, :], x[:, t, :], mv[:, t, 0:1], rstd[:, t:t + 1],
                                            ALU.subtract, ALU.mult).then_inc(s["xn_ready"], 1)
                dve.wait_ge(s["logits_ready"], 1)
                full = [P, NT, E]

                def over(m):
                    return m.unsqueeze(2).broadcast_to(full)
                down = c("down8").unsqueeze(1).broadcast_to(full)
                r.copy(lg[:], ps_r[:, 0:NT * E].rearrange("p (t e) -> p t e", e=E))
                r.first_of_max(lg[:], M[0][:], first[:], M[3][:], down)
                r.ts(work[:], first[:], 2.0 * NEG, None, ALU.mult)
                r.tt(work[:], work[:], lg[:], ALU.add)
                r.first_of_max(work[:], M[1][:], second[:], M[3][:], down)
                nc.vector.tensor_tensor(M[1][:], M[1][:], M[0][:], ALU.subtract).then_inc(s["exp_in"], 1)
                dve.wait_ge(s["exp_out"], 1)
                r.ts(M[2][:], M[1][:], 1.0, None, ALU.add)
                r.reciprocal(M[2][:], M[2][:])
                r.tt(M[3][:], M[2][:], M[1][:], ALU.mult)
                r.tt(first[:], first[:], over(M[2][:]), ALU.mult)
                r.tt(second[:], second[:], over(M[3][:]), ALU.mult)
                r.tt(gate[:], first[:], second[:], ALU.add)

                def hidden(b, e):
                    n = b * E + e
                    for f in range(NF):
                        m = n * NF + f
                        dve.wait_ge(s["act_ready"], m + 1)
                        dve.wait_ge(s["u_ready"], m + 1)
                        if later(n, 2):
                            dve.wait_ge(s["y_ready"], n - 1)
                        nc.vector.tensor_tensor(h[:, e % 2, f, :], sg[:, f % 2, :], ps_u[:, f % 2, :], ALU.mult
                                                ).then_inc(s["h_ready"], 1)

                def combine(b, e):
                    n = b * E + e
                    dve.wait_ge(s["y_ready"], n + 1)
                    for k in range(4):
                        if later(n, 1):
                            dve.wait_ge(s["x_ready"], 4 * n + k - 3)
                        xt = x[:, bass.ds(4 * b + k, 1), :].rearrange("p a d -> p (a d)")
                        y = ps_y[:, e % 2, P * k:P * k + P]
                        gk = gate[:, bass.ds(4 * b + k, 1), e:e + 1].rearrange("p a b -> p (a b)")
                        nc.vector.scalar_tensor_tensor(out=xt, in0=y, scalar=gk, in1=xt, op0=ALU.mult, op1=ALU.add
                                                       ).then_inc(s["x_ready"], 1)
                    if e == E - 1:
                        dve.wait_ge(s["x_ready"], 4 * n + 4)
                        for k in range(4):
                            nc.vector.bn_stats(g["stats"][:, bass.ds(4 * b + k, 1), :].rearrange("p a d -> p (a d)"),
                                               x[:, bass.ds(4 * b + k, 1), :].rearrange("p a d -> p (a d)"))
                blocks_of_experts(dve, E, hidden, combine)

            @block.gpsimd
            def _(pool):
                def split_weights(e):
                    pool.wait_ge(s["w_hi_ready"], e + 1)
                    nc.gpsimd.tensor_tensor(of_expert(split.w_lo[:], e), of_expert(weights, e), of_expert(split.w_hi[:], e),
                                            ALU.subtract).then_inc(s["w_lo_ready"], 1)
                for e in range(2):
                    split_weights(e)
                for q in range(4):
                    pool.wait_ge(s["xT_ready"], q + 1)
                    pool.wait_ge(s["x_hi_ready"], q + 1)
                    r = slice(512 * q, 512 * q + 512)
                    nc.gpsimd.tensor_tensor(split.x_lo[:, r], xT[:, r], split.x_hi[:, r], ALU.subtract
                                            ).then_inc(s["x_lo_ready"], 1)
                for e in range(2, E):
                    split_weights(e)

            @block.scalar
            def _(act):
                def round_weights(e):
                    nc.scalar.copy(of_expert(split.w_hi[:], e), of_expert(weights, e)).then_inc(s["w_hi_ready"], 1)
                act.wait_ge(weights_loaded, 16)
                for e in range(4):
                    round_weights(e)
                stats_on_scalar(act)
                for e in range(4, E):
                    round_weights(e)
                for q in range(4):
                    act.wait_ge(s["xT_ps_ready"], q + 1)
                    r = slice(512 * q, 512 * q + 512)
                    nc.scalar.copy(split.x_hi[:, r], ps_t[:]).then_inc(s["x_hi_ready"], 1)
                    nc.scalar.copy(xT[:, r], ps_t[:]).then_inc(s["xT_ready"], 1)
                act.wait_ge(s["exp_in"], 1)
                nc.scalar.activation(M[1][:], M[1][:], ACT.Exp).then_inc(s["exp_out"], 1)

                def hidden(b, e):
                    n = b * E + e
                    for f in range(NF):
                        m = n * NF + f
                        act.wait_ge(s["g_ready"], m + 1)
                        if later(m, 2):
                            act.wait_ge(s["h_ready"], m - 1)
                        nc.scalar.activation(sg[:, f % 2, :], ps_g[:, f % 2, :], ACT.Silu).then_inc(s["act_ready"], 1)
                blocks_of_experts(act, E, hidden, None)

            @block.tensor
            def _(pe):
                for q in range(4):
                    if q >= 1:
                        pe.wait_ge(s["xT_ready"], q)
                    for k in range(4):
                        t = 4 * q + k
                        pe.wait_ge(s["xn_ready"], t + 1)
                        mm = nc.tensor.transpose(ps_t[:, P * k:P * k + P], xn[:, t, :], ident)
                    mm.then_inc(s["xT_ps_ready"], 1)
                for t in range(NT):
                    pe.wait_ge(s["xT_ready"], t // 4 + 1)
                    mm = nc.tensor.matmul(ps_r[:, E * t:E * t + E], xT[:, P * t:P * t + P], w_router,
                                          start=True, stop=True)
                mm.then_inc(s["logits_ready"], 1)

                def up(b, e):
                    n = b * E + e
                    tokens = split.x_hi[:, bass.ds(b * 512, 512)], split.x_lo[:, bass.ds(b * 512, 512)]
                    if isinstance(b, int):
                        pe.wait_ge(s["w_lo_ready"], e + 1)
                        pe.wait_ge(s["x_lo_ready"], 1)
                    elif e == 0:
                        pe.wait_ge(s["x_lo_ready"], 4)
                    for f in range(NF):
                        m = n * NF + f
                        if later(m, 2):
                            pe.wait_ge(s["act_ready"], m - 1)
                        SplitProducts.matmul(nc, ps_g[:, f % 2, :], w(0, e, f), tokens).then_inc(s["g_ready"], 1)
                        if later(m, 2):
                            pe.wait_ge(s["h_ready"], m - 1)
                        SplitProducts.matmul(nc, ps_u[:, f % 2, :], w(1, e, f), tokens).then_inc(s["u_ready"], 1)

                def down(b, e):
                    n = b * E + e
                    pe.wait_ge(s["h_ready"], NF * (n + 1))
                    if later(n, 2):
                        pe.wait_ge(s["x_ready"], 4 * (n - 1))
                    for k in range(4):
                        for f in range(NF):
                            r = slice(P * k, P * k + P)
                            mm = nc.tensor.matmul(ps_y[:, e % 2, r], h[:, e % 2, f, r], w_down(e, f),
                                                  start=f == 0, stop=f == NF - 1)
                    mm.then_inc(s["y_ready"], 1)
                blocks_of_experts(pe, E, up, down)


def grouped_experts(nc, tag, g, w_router, weights, weights_loaded, correction):
    E, NF, NR, NB = 16, 6, 4, 4
    with stage(nc) as (stack, sems):
        sb, ps, sem = alloc(nc, stack, sems)
        x, c, ident = g["x"], g["c"], g["c"]("ident")
        mv, rstd, stats_on_vector, stats_on_scalar = norm_stats(nc, stack, sems, tag, g["stats"])
        xn = sb(f"{tag}_xn", [P, NT, D])
        xT = sb(f"{tag}_xT", [P, NT * P])
        split = SplitProducts(sb, tag, 2 * NF * P)
        h = sb(f"{tag}_h", [P, NB * NF, 512])
        sg = sb(f"{tag}_sg", [P, 2, 512])
        up_sb = sb(f"{tag}_up", [P, 2, 512])
        spread = sb(f"{tag}_spread", [E, NR * P], F32R)
        gate_hi = sb(f"{tag}_gate_hi", [E, NB, 512], F32R)
        gate_lo = sb(f"{tag}_gate_lo", [E, NB, 512], F32R)
        gate = sb(f"{tag}_gate", [P, NT, E])
        sigm, biased, first, rest, work = (sb(f"{tag}_work{i}", [P, NT, E]) for i in range(5))
        M = [sb(f"{tag}_max{i}", [P, NT]) for i in range(2)]
        group, group2, keep, keep2 = (sb(f"{tag}_group{i}", [P, NT, 4]) for i in range(4))

        ps_g = ps(f"{tag}_ps_g", [P, 2, 512])
        ps_u = ps(f"{tag}_ps_u", [P, 2, 512])
        ps_y = ps(f"{tag}_ps_y", [P, 2, 512])
        ps_t = ps(f"{tag}_ps_t", [P, 512])
        ps_r = ps(f"{tag}_ps_r", [P, 512])
        ps_c = ps_g

        names = ("xn_ready", "xT_ps_ready", "xT_ready", "x_hi_ready", "x_lo_ready", "w_hi_ready", "w_lo_ready",
                 "spread_ready", "logits_ready", "step", "exp_in", "exp_out", "gate_ready", "gateT_ps_ready",
                 "gate_hi_ready", "gate_lo_ready", "g_ready", "u_ready", "act_ready", "up_ready", "h_ready",
                 "c_ready", "hc_ready", "y_ready", "x_ready")
        s = {n: sem(f"{tag}_{n}") for n in names}

        def w(k, f):
            lo = (k * NF + f) * P
            return split.w_hi[:, lo:lo + P], split.w_lo[:, lo:lo + P]

        with nc.Block() as block:
            @block.vector
            def _(dve):
                r = Routing(nc, dve, s["step"])
                stats_on_vector(dve)
                for t in range(NT):
                    nc.vector.tensor_scalar(xn[:, t, :], x[:, t, :], mv[:, t, 0:1], rstd[:, t:t + 1],
                                            ALU.subtract, ALU.mult).then_inc(s["xn_ready"], 1)
                dve.wait_ge(s["logits_ready"], 1)
                full, four, small = [P, NT, E], [P, NT * 4, 4], [P, NT, 4]
                nc.vector.tensor_scalar(work[:], ps_r[:, 0:NT * E].rearrange("p (t e) -> p t e", e=E), -1.0, None,
                                        ALU.mult).then_inc(s["exp_in"], 1)
                dve.wait_ge(s["exp_out"], 1)
                r.ts(work[:], work[:], 1.0, None, ALU.add)
                r.reciprocal(sigm[:], work[:])
                r.tt(biased[:], sigm[:], correction.unsqueeze(1).broadcast_to(full), ALU.add)

                def by_group(a):
                    return a[:].rearrange("p t (g e) -> p (t g) e", e=4)

                def flat(a):
                    return a[:].rearrange("p t g -> p (t g)")
                b4, f4, r4 = by_group(biased), by_group(first), by_group(rest)
                down4 = c("down4").unsqueeze(1)
                r.first_of_max(b4, flat(group), f4, flat(group2), down4.broadcast_to(four))
                r.ts(f4, f4, NEG, None, ALU.mult)
                r.tt(r4, f4, b4, ALU.add)
                r.red(flat(group2), r4)
                r.tt(group[:], group[:], group2[:], ALU.add)
                d4 = down4.broadcast_to(small)
                r.first_of_max(group[:], M[0][:], keep[:], M[1][:], d4)
                r.ts(group2[:], keep[:], NEG, None, ALU.mult)
                r.tt(group2[:], group2[:], group[:], ALU.add)
                r.first_of_max(group2[:], M[0][:], keep2[:], M[1][:], d4)
                r.tt(keep[:], keep[:], keep2[:], ALU.add)
                r.ts(keep[:], keep[:], -NEG, NEG, ALU.mult, ALU.add)
                r.tt(r4, b4, flat(keep).unsqueeze(2).broadcast_to(four), ALU.add)
                down = c("down16").unsqueeze(1).broadcast_to(full)
                for k in range(4):
                    one = gate if k == 0 else first
                    r.first_of_max(rest[:], M[0][:], one[:], M[1][:], down)
                    if k:
                        r.tt(gate[:], gate[:], first[:], ALU.add)
                    if k < 3:
                        r.ts(work[:], one[:], 4.0 * NEG, None, ALU.mult)
                        r.tt(rest[:], rest[:], work[:], ALU.add)
                r.tt(gate[:], gate[:], sigm[:], ALU.mult)
                r.red(M[0][:], gate[:], ALU.add)
                r.ts(M[0][:], M[0][:], 1e-20, None, ALU.add)
                r.reciprocal(M[0][:], M[0][:])
                nc.vector.tensor_tensor(gate[:], gate[:], M[0][:].unsqueeze(2).broadcast_to(full), ALU.mult
                                        ).then_inc(s["gate_ready"], 1)
                for q in range(NB):
                    dve.wait_ge(s["gate_hi_ready"], q + 1)
                    nc.vector.tensor_tensor(gate_lo[:, q, :], ps_t[0:E, :] if q % 2 == 0 else ps_r[0:E, :],
                                            gate_hi[:, q, :], ALU.subtract).then_inc(s["gate_lo_ready"], 1)
                for b in range(NB + 1):
                    if b < NB:
                        for f in range(NR):
                            n = NR * b + f
                            dve.wait_ge(s["c_ready"], n + 1)
                            dve.wait_ge(s["h_ready"], NF * b + f + 1)
                            hb = h[:, NF * b + f, :]
                            nc.vector.tensor_tensor(hb, hb, ps_c[:, n % 2, :], ALU.mult).then_inc(s["hc_ready"], 1)
                    if b:
                        dve.wait_ge(s["y_ready"], b)
                        xb = x[:, 4 * (b - 1):4 * b, :]
                        nc.vector.tensor_tensor(xb, ps_y[:, (b - 1) % 2, :].rearrange("p (t d) -> p t d", d=D), xb,
                                                ALU.add).then_inc(s["x_ready"], 1)

            @block.gpsimd
            def _(pool):
                pool.wait_ge(s["w_hi_ready"], 1)
                nc.gpsimd.tensor_tensor(split.w_lo[:], weights[:, 0:2 * NF * P], split.w_hi[:], ALU.subtract
                                        ).then_inc(s["w_lo_ready"], 1)
                for q in range(4):
                    pool.wait_ge(s["xT_ready"], q + 1)
                    pool.wait_ge(s["x_hi_ready"], q + 1)
                    r = slice(512 * q, 512 * q + 512)
                    nc.gpsimd.tensor_tensor(split.x_lo[:, r], xT[:, r], split.x_hi[:, r], ALU.subtract
                                            ).then_inc(s["x_lo_ready"], 1)
                for m in range(NB * NF):
                    pool.wait_ge(s["act_ready"], m + 1)
                    pool.wait_ge(s["up_ready"], m + 1)
                    nc.gpsimd.tensor_tensor(h[:, m, :], sg[:, m % 2, :], up_sb[:, m % 2, :], ALU.mult
                                            ).then_inc(s["h_ready"], 1)

            @block.scalar
            def _(act):
                act.wait_ge(weights_loaded, 16)
                nc.scalar.copy(split.w_hi[:], weights[:, 0:2 * NF * P]).then_inc(s["w_hi_ready"], 1)
                nc.scalar.copy(spread[:], c("spread")[0:E, :]).then_inc(s["spread_ready"], 1)
                stats_on_scalar(act)
                for q in range(4):
                    act.wait_ge(s["xT_ps_ready"], q + 1)
                    r = slice(512 * q, 512 * q + 512)
                    nc.scalar.copy(split.x_hi[:, r], ps_t[:]).then_inc(s["x_hi_ready"], 1)
                    nc.scalar.copy(xT[:, r], ps_t[:]).then_inc(s["xT_ready"], 1)
                act.wait_ge(s["exp_in"], 1)
                nc.scalar.activation(work[:], work[:], ACT.Exp).then_inc(s["exp_out"], 1)
                for m in range(NB * NF):
                    act.wait_ge(s["g_ready"], m + 1)
                    if m >= 2:
                        act.wait_ge(s["h_ready"], m - 1)
                    nc.scalar.activation(sg[:, m % 2, :], ps_g[:, m % 2, :], ACT.Silu).then_inc(s["act_ready"], 1)
                    act.wait_ge(s["u_ready"], m + 1)
                    nc.scalar.copy(up_sb[:, m % 2, :], ps_u[:, m % 2, :]).then_inc(s["up_ready"], 1)
                for q in range(NB):
                    act.wait_ge(s["gateT_ps_ready"], q + 1)
                    nc.scalar.copy(gate_hi[:, q, :], ps_t[0:E, :] if q % 2 == 0 else ps_r[0:E, :]
                                   ).then_inc(s["gate_hi_ready"], 1)

            @block.tensor
            def _(pe):
                for q in range(4):
                    if q >= 1:
                        pe.wait_ge(s["xT_ready"], q)
                    for k in range(4):
                        t = 4 * q + k
                        pe.wait_ge(s["xn_ready"], t + 1)
                        mm = nc.tensor.transpose(ps_t[:, P * k:P * k + P], xn[:, t, :], ident)
                    mm.then_inc(s["xT_ps_ready"], 1)
                for t in range(NT):
                    pe.wait_ge(s["xT_ready"], t // 4 + 1)
                    mm = nc.tensor.matmul(ps_r[:, E * t:E * t + E], xT[:, P * t:P * t + P], w_router,
                                          start=True, stop=True)
                mm.then_inc(s["logits_ready"], 1)
                pe.wait_ge(s["w_lo_ready"], 1)
                for m in range(NB * NF):
                    b, f = m // NF, m % NF
                    pe.wait_ge(s["x_lo_ready"], b + 1)
                    tokens = split.x_hi[:, 512 * b:512 * b + 512], split.x_lo[:, 512 * b:512 * b + 512]
                    if m >= 2:
                        pe.wait_ge(s["act_ready"], m - 1)
                    SplitProducts.matmul(nc, ps_g[:, m % 2, :], w(0, f), tokens).then_inc(s["g_ready"], 1)
                    if m >= 2:
                        pe.wait_ge(s["up_ready"], m - 1)
                    SplitProducts.matmul(nc, ps_u[:, m % 2, :], w(1, f), tokens).then_inc(s["u_ready"], 1)
                pe.wait_ge(s["gate_ready"], 1)
                for q in range(NB):
                    if q >= 2:
                        pe.wait_ge(s["gate_lo_ready"], q - 1)
                    for k in range(4):
                        dst = ps_t if q % 2 == 0 else ps_r
                        mm = nc.tensor.transpose(dst[0:E, P * k:P * k + P], gate[:, 4 * q + k, :], ident)
                    mm.then_inc(s["gateT_ps_ready"], 1)
                pe.wait_ge(s["spread_ready"], 1)
                pe.wait_ge(s["act_ready"], NB * NF)

                def spread_gate(b, f):
                    n = NR * b + f
                    pe.wait_ge(s["gate_lo_ready"], b + 1)
                    if n >= 2:
                        pe.wait_ge(s["hc_ready"], n - 1)
                    rows = spread[:, P * f:P * f + P]
                    nc.tensor.matmul(ps_c[:, n % 2, :], rows, gate_hi[:, b, :], start=True, stop=False)
                    nc.tensor.matmul(ps_c[:, n % 2, :], rows, gate_lo[:, b, :], start=False, stop=True
                                     ).then_inc(s["c_ready"], 1)

                def down(b):
                    if b >= 2:
                        pe.wait_ge(s["x_ready"], b - 1)
                    pe.wait_ge(s["h_ready"], NF * b + NF)
                    pe.wait_ge(s["hc_ready"], NR * b + NR)
                    for k in range(4):
                        for f in range(NF):
                            lo = 2 * NF * P + f * P
                            mm = nc.tensor.matmul(ps_y[:, b % 2, P * k:P * k + P], h[:, NF * b + f, P * k:P * k + P],
                                                  weights[:, lo:lo + P], start=f == 0, stop=f == NF - 1)
                        if b + 1 < NB:
                            spread_gate(b + 1, k)
                    mm.then_inc(s["y_ready"], 1)
                for f in range(NR):
                    spread_gate(0, f)
                for b in range(NB):
                    down(b)


def mlstm(nc, g, a, experts_of_l1, weights_free_arena, pe_rows, pe_rows_ready, gate_w, gate_row, ln_w, ln_b):
    NH, C = 8, 16
    XR = 4
    HOP_FROM = 11
    HOPS_AHEAD = 4
    HOPS = ([(j, 0, 8) for j in range(HOPS_AHEAD)] + [(j, 0, NT) for j in range(HOPS_AHEAD, 16)]
            + [(j, 8, 8) for j in range(HOPS_AHEAD)])
    FLOOR_AT = HOPS_AHEAD + 5
    SPLIT = 9
    with stage(nc) as (stack, sems):
        sb, ps, sem = alloc(nc, stack, sems)
        x, ctxT, c, ident = g["x"], g["ctxT"], g["c"], g["c"]("ident")
        arena = weights_free_arena
        expert_rows, gates_l1, slots_l1 = experts_of_l1
        mv = sb("l2a_mv", [P, NT, 2])
        rstd = sb("l2a_rstd", [P, NT])
        qz = arena[:, 0:16384].rearrange("p (b h s) -> p b h s", b=2 * NT, h=NH)
        work = arena[:, 16384:20480].rearrange("p (k u n) -> p k u n", k=4, u=2)
        mb, dt, sc, cw = (work[:, k] for k in range(4))
        small = work[:, 3].rearrange("p u (k n) -> p (u k) n", k=4)
        khop = sb("l2a_khop", [P, NT, NH, S])
        back = [khop[:, 8 + 4 * k:12 + 4 * k].rearrange("p t h s -> p (t h s)").rearrange("p (t d) -> p t d", t=NT)
                for k in range(2)]
        xn = sb("l2a_xn", [P, XR, D])
        xT = sb("l2a_xT", [P, XR, P])
        pe_T = pe_rows[:].rearrange("p j d -> p (j d)")
        sums = pe_T[:, 0:NT * NH * (C + 1)].rearrange("p (t n) -> p t n", t=NT)
        gw_ctx = sb("l2a_gw_ctx", [P, 16])
        cum = sb("l2a_cum", [P, P])
        key_gate = sb("l2a_key_gate", [P, NT, NH])
        maxT = sb("l2a_maxT", [P, P])
        floor_ = sb("l2a_floor", [P, NT, NH])
        vb = sb("l2a_vb", [P, 2, NH, C + 1])
        norm = sb("l2a_norm", [P, NT, NH])
        var = sb("l2a_var", [P, NT, NH])
        rs = sb("l2a_rs", [P, NT, NH])
        sq = sb("l2a_sq", [P, 2, D])

        ps_a = ps("l2a_ps_a", [P, 2, 512])
        ps_k = ps("l2a_ps_k", [P, 2, 512])
        ps_g = ps("l2a_ps_g", [P, 512])
        ps_c = ps("l2a_ps_c", [P, 512])
        ps_x = ps("l2a_ps_x", [P, 2, 512])

        names = ("cleared", "x_added", "stats_ready", "mv_ready", "std_in", "std_ready", "rstd_ready", "w_ready", "xn_ready", "xT_ps_ready", "q0_ready", "q1_ready",  "xT_ready", "step", "act_in", "act_out",
                 "logf_ready", "cum_ready", "a_ready", "aT_ready", "maxT_ready", "max_ps_ready", "max_stored",
                 "peT_ps_ready", "peT_ready", "khop_ps_ready", "khop_ready", "shift_ready",
                 "s_ready", "m1_ready", "exp_ready", "sc_ready", "cw_ready", "o_ready", "sums_ready",
                 "chain", "cen_ready", "sq_ready", "var_ready", "root_ready", "rs_ready", "gained", "scaled0", "scaled1", "gates_done", "gate_mm")
        s = {n: sem(f"l2a_{n}") for n in names}
        fetched = [sem(f"l2a_fetched{q}") for q in range(4)]
        tile_in = [sem(f"l2a_tile_in{k}") for k in range(2)]
        v_in = [sem(f"l2a_v_in{k}") for k in range(2)]
        scratch = nc.dram_tensor("max_scratch", (2, NT, NH, S), F32).ap()

        def spread_q(ops, t):
            return ops.tensor_tensor(
                qz[:, 2 * t:2 * t + 2],
                xT[:, t % XR, :].rearrange("p (b s) -> p b s", b=2).unsqueeze(2).broadcast_to([P, 2, NH, S]),
                c("mask16").unsqueeze(1).unsqueeze(3).broadcast_to([P, 2, NH, S]), ALU.mult)

        def heads(tiles):
            return sums[:, tiles, :].rearrange("p t (h c) -> p t h c", h=NH)[:, :, :, 0:C]

        def add_heads(eng, ops, tiles, scaled):
            eng.wait_ge(s["rs_ready"], 1)
            n = tiles.stop - tiles.start
            y = heads(tiles)
            ops.tensor_tensor(y, y, rs[:, tiles, :].unsqueeze(3).broadcast_to([P, n, NH, C]), ALU.mult
                              ).then_inc(scaled, 1)
            eng.wait_ge(scaled, 1)
            xt = x[:, tiles, :].rearrange("p t (h c) -> p t h c", h=NH)
            ops.tensor_tensor(xt, xt, y, ALU.add).then_inc(scaled, 1)

        with nc.Block() as block:
            @block.sync
            def _(sp):
                def load_v(t, u):
                    sp.dma_start(vb[:, u].rearrange("p h c -> p (h c)"),
                                 a["ctx_one"][:, bass.ds(t, 1), :].rearrange("p a d -> p (a d)")
                                 ).then_inc(v_in[u], 16)
                for u in range(2):
                    load_v(u, u)
                sp.wait_ge(s["maxT_ready"], 2)
                sp.dma_start(scratch.rearrange("b t h s -> (t h) b s"),
                             maxT[:].rearrange("p (b s) -> p b s", b=2)).then_inc(s["max_stored"], 16)
                sp.wait_ge(s["max_stored"], 16)

                def body(t, u, edge):
                    if edge is None or t >= 2:
                        sp.wait_ge(s["m1_ready"], t - 1)
                    for b in range(2):
                        src = scratch[b, bass.ds(t, 1)].rearrange("a h s -> a (h s)").broadcast_to([S, NH * S])
                        sp.dma_start(mb[S * b:S * b + S, u, :], src).then_inc(tile_in[u], 16)
                    if edge is None or t >= 2:
                        sp.wait_ge(s["o_ready"], t - 1)
                        load_v(t, u)
                pipeline(sp, body, 0, NT)

            @block.gpsimd
            def _(pool):
                for t in range(NT):
                    pool.wait_ge(s["cleared"], t // 4 + 1)
                    for k in range(2):
                        nc.gpsimd.indirect_dma_start(
                            out=back[k][:, t, :], out_offset=None, in_=expert_rows,
                            in_offset=bass.IndirectOffsetOnAxis(ap=slots_l1[k][:, t:t + 1], axis=0),
                            bounds_check=8 * L1_CAP - 1, oob_is_err=False).then_inc(fetched[t // 4], 16)
                pool.wait_ge(s["xT_ready"], NT - 3)
                spread_q(nc.gpsimd, NT - 4).then_inc(s["q0_ready"], 1)
                pool.wait_ge(s["xn_ready"], NT)
                nc.gpsimd.tensor_tensor(x[:], x[:], ln_b.unsqueeze(1).broadcast_to([P, NT, D]), ALU.add
                                        ).then_inc(s["shift_ready"], 1)
                pool.wait_ge(s["shift_ready"], 1)
                pool.wait_ge(s["gates_done"], 1)

                def weights(t, u, edge):
                    pool.wait_ge(s["exp_ready"], t + 1)
                    pool.wait_ge(s["sc_ready"], t + 1)
                    if edge is None or t >= 2:
                        pool.wait_ge(s["o_ready"], t - 1)
                    nc.gpsimd.tensor_tensor(cw[:, u], sc[:, u], dt[:, u], ALU.mult).then_inc(s["cw_ready"], 1)

                def gain(t):
                    pool.wait_ge(s["var_ready"], t + 2)
                    y = heads(bass.ds(t, 2))
                    w = ln_w.rearrange("p (h c) -> p h c", h=NH).unsqueeze(1).broadcast_to([P, 2, NH, C])
                    nc.gpsimd.tensor_tensor(y, y, w, ALU.mult).then_inc(s["gained"], 2)

                def body(i, u, edge):
                    if edge is None or 1 <= i < NT + 1:
                        weights(i - 1, 1 - u, edge)
                    if u == 1 and (edge is None or i >= 5):
                        gain(i - 5)
                pipeline(pool, body, 0, NT + 4)
                pool.wait_ge(s["gained"], NT)
                add_heads(pool, nc.gpsimd, slice(SPLIT, NT), s["scaled1"])

            @block.vector
            def _(dve):
                step = Steps(dve, s["step"])
                nc.vector.tensor_tensor(gw_ctx[:], gate_w[:, 1, :], gate_w[:, 2, :], ALU.add).then_inc(s["w_ready"], 1)
                cleared = khop[:, 8:16].rearrange("p (k n) h s -> p k (n h s)", k=2)
                for q in range(4):
                    nc.vector.memset(cleared[:, :, 512 * q:512 * q + 512], 0.0).then_inc(s["cleared"], 1)
                for q in range(4):
                    if True:
                        tiles = range(4 * q, 4 * q + 4)
                        dve.wait_ge(fetched[q], 16 * 8)
                        for k in range(2):
                            if k:
                                dve.wait_ge(s["x_added"], 8 * q + 4)
                            for t in tiles:
                                nc.vector.scalar_tensor_tensor(
                                    out=x[:, t, :], in0=back[k][:, t, :], scalar=gates_l1[k][:, t:t + 1],
                                    in1=x[:, t, :], op0=ALU.mult, op1=ALU.add).then_inc(s["x_added"], 1)
                        dve.wait_ge(s["x_added"], 8 * q + 8)
                        for t in tiles:
                            nc.vector.bn_stats(g["stats"][:, t, :], x[:, t, :]).then_inc(s["stats_ready"], 1)
                        for t in tiles:
                            dve.wait_ge(s["stats_ready"], t + 1)
                            nc.vector.bn_aggr(mv[:, t, :], g["stats"][:, t, :]).then_inc(s["mv_ready"], 1)
                        four = slice(4 * q, 4 * q + 4)
                        dve.wait_ge(s["mv_ready"], 4 * q + 4)
                        nc.vector.tensor_scalar(rstd[:, four], mv[:, four, 1], 1e-5, None, ALU.add
                                                ).then_inc(s["std_in"], 1)
                    if True:
                        dve.wait_ge(s["std_ready"], q + 1)
                        nc.vector.reciprocal(rstd[:, four], rstd[:, four]).then_inc(s["rstd_ready"], 1)
                        dve.wait_ge(s["rstd_ready"], q + 1)
                        for t in tiles:
                            if t >= XR:
                                dve.wait_ge(s["xT_ps_ready"], t - XR + 1)
                            nc.vector.tensor_scalar(xn[:, t % XR, :], x[:, t, :], mv[:, t, 0:1], rstd[:, t:t + 1],
                                                    ALU.subtract, ALU.mult).then_inc(s["xn_ready"], 1)
                        for t in tiles[1::2]:
                            dve.wait_ge(s["xT_ready"], t + 1)
                            spread_q(nc.vector, t).then_inc(s["q1_ready"], 1)
                dve.wait_ge(s["gate_mm"], NT)
                gates = ps_g[:, 0:256].rearrange("p (t e) -> p t e", e=16)
                ig, fg, nab, ex, lf = (small[:, k].rearrange("p (t h) -> p t h", h=NH) for k in range(5))
                row = gate_row.unsqueeze(1)
                step.then(nc.vector.tensor_tensor(ig, gates[:, :, 0:8], row[:, :, 0:8].broadcast_to([P, NT, NH]), ALU.add))
                step.then(nc.vector.tensor_tensor(fg, gates[:, :, 8:16], row[:, :, 8:16].broadcast_to([P, NT, NH]),
                                                  ALU.add))
                nc.vector.scalar_tensor_tensor(out=nab, in0=fg, scalar=-1.0, in1=fg, op0=ALU.mult, op1=ALU.min
                                               ).then_inc(s["act_in"], 1)
                dve.wait_ge(s["act_out"], 2)
                nc.vector.scalar_tensor_tensor(out=lf, in0=fg, scalar=0.0, in1=ex, op0=ALU.min, op1=ALU.subtract
                                               ).then_inc(s["logf_ready"], 1)
                dve.wait_ge(s["cum_ready"], 1)
                step.then(nc.vector.tensor_copy(cum[:], ps_c[:, 0:P]))
                nc.vector.tensor_tensor(key_gate[:], ig, cum[:].rearrange("p (t h) -> p t h", h=NH), ALU.subtract
                                        ).then_inc(s["a_ready"], 1)
                dve.wait_ge(s["aT_ready"], 1)
                for b in range(2):
                    nc.vector.tensor_tensor_scan(maxT[:, S * b:S * b + S], c("ones")[:, 0:S],
                                                 ps_c[:, P + S * b:P + S * b + S], -3.0e38, ALU.mult, ALU.max
                                                 ).then_inc(s["maxT_ready"], 1)
                dve.wait_ge(s["max_ps_ready"], 1)
                nc.vector.tensor_tensor(floor_[:], ps_c[:, 2 * P:3 * P].rearrange("p (t h) -> p t h", h=NH),
                                        cum[:].rearrange("p (t h) -> p t h", h=NH), ALU.add).then_inc(s["act_in"], 1)
                dve.wait_ge(s["act_out"], 3)
                nc.vector.tensor_scalar(floor_[:], floor_[:], 1e-6, None, ALU.add).then_inc(s["gates_done"], 1)
                dve.wait_ge(s["gates_done"], 1)

                def mask_max(t, u, edge):
                    dve.wait_ge(tile_in[u], 16 * (t - u) + 32)
                    if edge is None or t >= 2:
                        dve.wait_ge(s["cw_ready"], t - 1)
                    nc.vector.tensor_tensor(dt[:, u].rearrange("p (h s) -> p h s", h=NH),
                                            mb[:, u].rearrange("p (h s) -> p h s", h=NH),
                                            c("later").unsqueeze(1).broadcast_to([P, NH, S]), ALU.add
                                            ).then_inc(s["m1_ready"], 1)

                def scores(t, u, edge):
                    dve.wait_ge(s["s_ready"], t + 1)
                    if edge is not None and t == 0:
                        dve.wait_ge(s["khop_ready"], len(HOPS))
                    kh = khop[:, bass.ds(t, 1)].rearrange("p a h s -> p (a h s)")
                    nc.vector.scalar_tensor_tensor(out=sc[:, u], in0=ps_a[:, u, :], scalar=0.25, in1=kh,
                                                   op0=ALU.mult, op1=ALU.add).then_inc(s["sc_ready"], 1)

                def divide(t):
                    n = [0]

                    def then(ins):
                        n[0] += 1
                        ins.then_inc(s["chain"], 2)
                        dve.wait_ge(s["chain"], 5 * t + 2 * n[0])
                    dve.wait_ge(s["sums_ready"], t + 2)
                    pair = bass.ds(t, 2)
                    total = sums[:, pair, :].rearrange("p t (h c) -> p t h c", h=NH)[:, :, :, C]
                    nr, h4 = norm[:, pair, :], heads(pair)
                    then(nc.vector.scalar_tensor_tensor(out=nr, in0=total, scalar=-1.0, in1=total,
                                                        op0=ALU.mult, op1=ALU.max))
                    then(nc.vector.scalar_tensor_tensor(out=nr, in0=nr, scalar=1e-6, in1=floor_[:, pair, :],
                                                        op0=ALU.add, op1=ALU.max))
                    then(nc.vector.reciprocal(nr, nr))
                    then(nc.vector.tensor_tensor(h4, h4, nr.unsqueeze(3).broadcast_to([P, 2, NH, C]), ALU.mult))
                    then(nc.vector.tensor_reduce(nr, h4, AX.X, ALU.add))

                def variance(t):
                    pair = bass.ds(t, 2)
                    nr, h4, q4 = norm[:, pair, :], heads(pair), sq[:].rearrange("p t (h c) -> p t h c", h=NH)
                    nc.vector.scalar_tensor_tensor(out=h4, in0=nr.unsqueeze(3).broadcast_to([P, 2, NH, C]),
                                                   scalar=-1.0 / C, in1=h4, op0=ALU.mult, op1=ALU.add
                                                   ).then_inc(s["cen_ready"], 2)
                    dve.wait_ge(s["cen_ready"], t + 2)
                    nc.vector.tensor_tensor(q4, h4, h4, ALU.mult).then_inc(s["sq_ready"], 2)
                    dve.wait_ge(s["sq_ready"], 2 * t + 2)
                    nc.vector.tensor_reduce(var[:, pair, :], q4, AX.X, ALU.add).then_inc(s["sq_ready"], 2)
                    dve.wait_ge(s["sq_ready"], 2 * t + 4)
                    nc.vector.tensor_scalar(var[:, pair, :], var[:, pair, :], 1.0 / C, 1e-5, ALU.mult, ALU.add
                                            ).then_inc(s["var_ready"], 2)

                def body(i, u, edge):
                    if edge is None or i < NT:
                        mask_max(i, u, edge)
                    if u == 0 and (edge is None or i >= 4):
                        variance(i - 4)
                    if edge is None or i < NT:
                        scores(i, u, edge)
                    if u == 1 and (edge is None or i >= 3):
                        divide(i - 3)
                pipeline(dve, body, 0, NT + 3)
                dve.wait_ge(s["root_ready"], 1)
                nc.vector.reciprocal(rs[:], rs[:]).then_inc(s["rs_ready"], 1)
                dve.wait_ge(s["gained"], NT)
                dve.wait_ge(s["shift_ready"], 1)
                add_heads(dve, nc.vector, slice(0, SPLIT), s["scaled0"])
                dve.wait_ge(s["scaled0"], 2)
                for t in range(NT):
                    if t == SPLIT:
                        dve.wait_ge(s["scaled1"], 2)
                    nc.vector.bn_stats(g["stats"][:, t, :], x[:, t, :])

            @block.scalar
            def _(act):
                def copy_peT(j):
                    act.wait_ge(s["peT_ps_ready"], j + 1)
                    nc.scalar.copy(pe_T[:, 256 * j:256 * j + 256], ps_a[:, j % 2, 0:4 * S]).then_inc(s["peT_ready"], 1)
                def copy_hop(n):
                    j, first, count = HOPS[n]
                    act.wait_ge(s["khop_ps_ready"], n + 1)
                    if n == HOPS_AHEAD:
                        act.wait_ge(s["x_added"], 2 * NT)
                    tiles = khop[:, first:first + count]
                    nc.scalar.copy(tiles.rearrange("p t h v -> p v (t h)")[:, 4 * j:4 * j + 4, :],
                                   ps_k[:, n % 2, 0:32 * count].rearrange("p (v n) -> p v n", v=4)
                                   ).then_inc(s["khop_ready"], 1)

                for j in range(16):
                    copy_peT(j)
                for t in range(NT):
                    if t % 4 == 0:
                        four = slice(t, t + 4)
                        act.wait_ge(s["std_in"], t // 4 + 1)
                        nc.scalar.activation(rstd[:, four], rstd[:, four], ACT.Sqrt).then_inc(s["std_ready"], 1)
                    act.wait_ge(s["xT_ps_ready"], t + 1)
                    if t >= XR:
                        act.wait_ge(s["gate_mm"], t - XR + 1)
                        if t % 2:
                            act.wait_ge(s["q1_ready"], (t - XR) // 2 + 1)
                        else:
                            act.wait_ge(s["q0_ready"], (t - XR) // 2 + 1)
                    nc.scalar.copy(xT[:, t % XR, :], ps_x[:, t % 2, 0:P]).then_inc(s["xT_ready"], 1)
                    if t % 4 == 3:
                        for k in (t - 3, t - 1):
                            if k == NT - 4:
                                continue
                            act.wait_ge(s["xT_ready"], k + 1)
                            for h in range(NH):
                                e = nc.scalar.activation(qz[:, 2 * k:2 * k + 2, h, :],
                                                         xT[:, k % XR, :].rearrange("p (b s) -> p b s", b=2),
                                                         ACT.Copy, scale=c("mask16")[:, h:h + 1])
                            e.then_inc(s["q0_ready"], 1)
                            if t == HOP_FROM:
                                for n in range(HOPS_AHEAD // 2):
                                    copy_hop(n + (HOPS_AHEAD // 2 if k == t - 1 else 0))
                nab, ex = small[:, 2], small[:, 3]
                act.wait_ge(s["act_in"], 1)
                nc.scalar.activation(ex, nab, ACT.Exp).then_inc(s["act_out"], 1)
                act.wait_ge(s["act_out"], 1)
                nc.scalar.activation(ex, ex, ACT.Ln, bias=1.0).then_inc(s["act_out"], 1)
                for n in range(HOPS_AHEAD, len(HOPS)):
                    if n == FLOOR_AT:
                        act.wait_ge(s["act_in"], 2)
                        nc.scalar.activation(floor_[:], floor_[:], ACT.Exp, scale=-1.0).then_inc(s["act_out"], 1)
                    copy_hop(n)

                def body(i, u, edge):
                    if edge is None or i < NT:
                        act.wait_ge(s["m1_ready"], i + 1)
                        for h in range(NH):
                            r = slice(S * h, S * h + S)
                            e = nc.scalar.activation(dt[:, u, r], dt[:, u, r], ACT.Exp, scale=-1.0,
                                                     bias=key_gate[:, bass.ds(i, 1), h:h + 1].rearrange("p a h -> p (a h)"))
                        e.then_inc(s["exp_ready"], 1)
                    if edge is None or 2 <= i < NT + 2:
                        act.wait_ge(s["o_ready"], i - 1)
                        nc.scalar.copy(sums[:, bass.ds(i - 2, 1), :].rearrange("p a n -> p (a n)"),
                                       ps_k[:, u, 0:NH * (C + 1)]).then_inc(s["sums_ready"], 1)
                pipeline(act, body, 0, NT + 2)
                act.wait_ge(s["var_ready"], NT)
                nc.scalar.activation(rs[:], var[:], ACT.Sqrt).then_inc(s["root_ready"], 1)

            @block.tensor
            def _(pe):
                pe.wait_ge(pe_rows_ready, 16 * 32)

                def turn_positions(j):
                    if j >= 2:
                        pe.wait_ge(s["peT_ready"], j - 1)
                    for k in range(2):
                        mm = nc.tensor.transpose(ps_a[:, j % 2, P * k:P * k + P], pe_rows[:, 2 * j + k, :], ident)
                    mm.then_inc(s["peT_ps_ready"], 1)
                for j in range(16):
                    turn_positions(j)
                pe.wait_ge(s["w_ready"], 1)

                def hop(n):
                    j, first, count = HOPS[n]
                    pe.wait_ge(s["peT_ready"], j + 1)
                    pe.wait_ge(s["q0_ready"], (first + count) // 2)
                    pe.wait_ge(s["q1_ready"], (first + count) // 2)
                    if n >= 2:
                        pe.wait_ge(s["khop_ready"], n - 1)
                    for v in range(4):
                        for b in range(2):
                            q = qz[:, 2 * first + b:2 * (first + count):2, :, 4 * j + v]
                            c0 = NH * count * v
                            mm = nc.tensor.matmul(
                                ps_k[S * b:S * b + S, n % 2, c0:c0 + NH * count].rearrange("p (t h) -> p t h", h=NH),
                                pe_T[:, 4 * S * j + S * v:4 * S * j + S * v + S], q, start=True, stop=True)
                    mm.then_inc(s["khop_ps_ready"], 1)

                def gate_mm(t):
                    pe.wait_ge(s["xT_ready"], t + 1)
                    dst = ps_g[:, 16 * t:16 * t + 16]
                    nc.tensor.matmul(dst, xT[:, t % XR, :], gate_w[:, 0, :], start=True, stop=False)
                    nc.tensor.matmul(dst, ctxT[:, P * t:P * t + P], gw_ctx[:], start=False, stop=True
                                     ).then_inc(s["gate_mm"], 1)
                for t in range(NT):
                    pe.wait_ge(s["xn_ready"], t + 1)
                    if t >= 2:
                        pe.wait_ge(s["xT_ready"], t - 1)
                    nc.tensor.transpose(ps_x[:, t % 2, 0:P], xn[:, t % XR, :], ident).then_inc(s["xT_ps_ready"], 1)
                    if t >= 1:
                        gate_mm(t - 1)
                    if t == HOP_FROM:
                        for n in range(HOPS_AHEAD):
                            hop(n)
                gate_mm(NT - 1)

                for n in range(HOPS_AHEAD, len(HOPS)):
                    j = n - HOPS_AHEAD
                    if j == 2:
                        pe.wait_ge(s["logf_ready"], 1)
                        nc.tensor.matmul(ps_c[:, 0:P], c("tri_seq"), small[:, 4], start=True, stop=True
                                         ).then_inc(s["cum_ready"], 1)
                    if j == 3:
                        pe.wait_ge(s["a_ready"], 1)
                        nc.tensor.transpose(ps_c[:, P:2 * P], key_gate[:].rearrange("p t h -> p (t h)"), ident
                                            ).then_inc(s["aT_ready"], 1)
                    if j == 4:
                        pe.wait_ge(s["maxT_ready"], 2)
                        nc.tensor.transpose(ps_c[:, 2 * P:3 * P], maxT[:], ident).then_inc(s["max_ps_ready"], 1)
                    hop(n)

                for t in range(NT + 1):
                    if t < NT:
                        if t >= 2:
                            pe.wait_ge(s["sc_ready"], t - 1)
                        for b in range(2):
                            mm = nc.tensor.matmul(ps_a[S * b:S * b + S, t % 2, :].rearrange("p (h s) -> p h s", h=NH),
                                                  ctxT[:, P * t + S * b:P * t + S * b + S], qz[:, 2 * t + b],
                                                  start=True, stop=True)
                        mm.then_inc(s["s_ready"], 1)
                    if t >= 1:
                        k = t - 1
                        pe.wait_ge(s["cw_ready"], k + 1)
                        pe.wait_ge(v_in[k % 2], 16 * (k // 2 + 1))
                        if k >= 2:
                            pe.wait_ge(s["sums_ready"], k - 1)
                        else:
                            pe.wait_ge(s["khop_ready"], len(HOPS))
                        for b in range(2):
                            r = slice(S * b, S * b + S)
                            for h in range(NH):
                                mm = nc.tensor.matmul(ps_k[r, k % 2, (C + 1) * h:(C + 1) * (h + 1)],
                                                      cw[r, k % 2, S * h:S * h + S], vb[r, k % 2, h, :],
                                                      start=True, stop=True)
                        mm.then_inc(s["o_ready"], 1)


ATT = ["L0_q", "L0_q_turned", "L0_k", "L0_k_turned", "L0_v", "L0_o", "L1_q", "L1_k", "L1_v", "L1_o",
       "L3_q", "L3_k", "L3_v", "L3_o"]
ROWS = ["L0_o", "L1_o", "L3_o"]
STOP = 8
L0_W, L1_W, L2_W, L3_W = 8192, 12288, 6144, 2304


def build(nc, a, out):
    with ExitStack() as stack:
        sb, ps, sem = alloc(nc, stack)
        g = {}
        x = g["x"] = sb("x", [P, NT, D])
        stats = g["stats"] = sb("x_stats", [P, NT, 6])
        ctxT = g["ctxT"] = sb("ctxT", [P, NT * P])
        consts = sb("consts", [P, CONSTS.shape[1]])
        att_w = sb("att_w", [P, len(ATT), D])
        att_col = sb("att_col", [P, 19])
        rows = sb("rows", [1, len(ROWS), D])
        ident_bf = sb("ident_bf", [P, P], BF16)
        causal_bf = sb("causal_bf", [P, S], BF16)
        g["ident_bf"], g["causal_bf"] = ident_bf[:], causal_bf[:]
        loaded, x_loaded = sem("loaded"), sem("x_loaded")
        casts = sem("casts")
        stored = sem("stored")

        def c(name):
            lo, hi = CONST_COLS[name]
            return consts[:, lo:hi]
        g["c"] = c
        late_w = sb("late_w", [P, L2_W + L3_W])
        routers = sb("routers", [P, 8 + 8 + 8 + 16])
        gate_w = sb("gate_w", [P, 3, 16])
        gate_row = sb("gate_row", [P, 17, 16])
        expert_col = sb("expert_col", [P, 2 + 16])
        ffn_loaded = {n: sem(f"ffn_loaded_{n}") for n in ("L0", "L1", "L2", "L3")}

        slots_cleared = {n: sem(f"slots_cleared_{n}") for n in ("L0", "L1")}
        zeros_ready = sem("zeros_ready")
        l0_in, l0_out = (nc.dram_tensor(f"l0_slots_{n}", (8 * L0_CAP, D), F32).ap() for n in ("in", "out"))
        l1_in, l1_out = (nc.dram_tensor(f"l1_slots_{n}", (8 * L1_CAP, D), F32).ap() for n in ("in", "out"))
        hops = sb("hops", [P, 32], mybir.dt.int32)
        l1_gates = [sb(f"l1_gates{k}", [P, NT])[:] for k in range(2)]
        l1_slots = [sb(f"l1_slots{k}", [P, NT], mybir.dt.int32)[:] for k in range(2)]
        early = stack.enter_context(ExitStack())
        arena = early.enter_context(nc.sbuf_tensor("arena", [P, L0_W + L1_W], F32))
        pe_rows = early.enter_context(nc.sbuf_tensor("pe_rows", [P, 32, D], F32))
        zeros = pe_rows[:, 0:4, :].rearrange("p a d -> p (a d)")
        hops_ready, pe_rows_ready = sem("hops_ready"), sem("pe_rows_ready")

        with nc.Block() as block:
            @block.gpsimd
            def _(pool):
                nc.gpsimd.memset(zeros, 0.0).then_inc(zeros_ready, 1)

            @block.scalar
            def _(act):
                act.wait_ge(zeros_ready, 1)
                act.wait_ge(loaded, 16 * 9)
                for n, dst, cap in (("L0", l0_in, L0_CAP), ("L1", l1_in, L1_CAP)):
                    blocks = 8 * cap * D // (P * 512)
                    act.dma_start(dst.rearrange("(p a r) d -> p a (r d)", p=P, a=blocks),
                                  zeros.unsqueeze(1).broadcast_to([P, blocks, 512])).then_inc(slots_cleared[n], 16)

            @block.sync
            def _(sp):
                sp.dma_start(x[:], a["x"]).then_inc(x_loaded, 16)
                for dst, src in ((consts, "consts"), (ctxT, "ctxT"), (att_w, "att_w"),
                                 (att_col, "att_col"), (rows, "rows")):
                    sp.dma_start(dst[:], a[src]).then_inc(loaded, 16)
                sp.dma_start(routers[:], a["routers"]).then_inc(loaded, 16)
                sp.dma_start(expert_col[:], a["expert_col"]).then_inc(loaded, 16)
                sp.dma_start(gate_w[:], a["gate_w"]).then_inc(loaded, 16)
                sp.dma_start(gate_row[:], a["gate_row"]).then_inc(loaded, 16)
                sp.dma_start(hops[:], a["hops"]).then_inc(hops_ready, 16)
                sp.wait_ge(loaded, 16 * 9)
                for n, dst in (("L0", arena[:, 0:L0_W]), ("L1", arena[:, L0_W:L0_W + L1_W]),
                               ("L2", late_w[:, 0:L2_W]), ("L3", late_w[:, L2_W:L2_W + L3_W])):
                    sp.dma_start(dst, a[f"{n}_experts"]).then_inc(ffn_loaded[n], 16)

            @block.vector
            def _(dve):
                dve.wait_ge(x_loaded, 16)
                for t in range(NT):
                    nc.vector.bn_stats(stats[:, t, :], x[:, t, :])
                dve.wait_ge(loaded, 16 * 9)
                nc.vector.tensor_scalar(gate_row[:, 1:9, :], gate_row[:, 1:9, :], 1.0, None, ALU.add
                                        ).then_inc(casts, 1)
                nc.vector.tensor_copy(ident_bf[:], c("ident")).then_inc(casts, 1)
                nc.vector.tensor_copy(causal_bf[:], c("causal")).then_inc(casts, 1)
                dve.wait_ge(casts, 3)

        w = {n: att_w[:, i, :] for i, n in enumerate(ATT)}
        r = {n: rows[:, i, :] for i, n in enumerate(ROWS)}
        attention(nc, "l0a", g, (w["L0_q"], w["L0_q_turned"], w["L0_k"], w["L0_k_turned"], w["L0_v"], w["L0_o"]),
                  att_col[:, 0:8], att_col[:, 16:17], r["L0_o"], rope=True)

        def gather_positions(pool, blocks):
            pool.wait_ge(hops_ready, 16)
            for n in ("L0", "L1"):
                pool.wait_ge(slots_cleared[n], 16)
            for j in blocks:
                nc.gpsimd.indirect_dma_start(
                    out=pe_rows[:, j, :], out_offset=None, in_=a["rpe"],
                    in_offset=bass.IndirectOffsetOnAxis(ap=hops[:, j:j + 1], axis=0)
                    ).then_inc(pe_rows_ready, 16)

        l0w, l1w = arena[:, 0:L0_W], arena[:, L0_W:L0_W + L1_W]
        l2w, l3w = late_w[:, 0:L2_W], late_w[:, L2_W:L2_W + L3_W]

        if STOP >= 2:
            routed_experts(nc, "l0f", g, 1, L0_CAP, routers[:, 0:8],
                           lambda e, f: l0w[:, e * 512 + f * P:e * 512 + f * P + P], None,
                           lambda e, f: l0w[:, 4096 + (e * 4 + f) * P:4096 + (e * 4 + f) * P + P],
                           ffn_loaded["L0"], l0_in, l0_out, slots_cleared["L0"],
                           pe_rows[:, 16:32, :].rearrange("p a d -> p (a d)"),
                           prefetch=lambda pool: gather_positions(pool, range(16)))
        if STOP >= 3:
            attention(nc, "l1a", g, (w["L1_q"], None, w["L1_k"], None, w["L1_v"], w["L1_o"]),
                      att_col[:, 8:12], att_col[:, 17:18], r["L1_o"], rope=False)
        if STOP >= 4:
            routed_experts(nc, "l1f", g, 2, L1_CAP, routers[:, 8:16],
                           lambda e, f: l1w[:, e * 1024 + f * P:e * 1024 + f * P + P],
                           lambda e, f: l1w[:, e * 1024 + 512 + f * P:e * 1024 + 512 + f * P + P],
                           lambda e, f: l1w[:, 8192 + (e * 4 + f) * P:8192 + (e * 4 + f) * P + P],
                           ffn_loaded["L1"], l1_in, l1_out, slots_cleared["L1"],
                           None, norm_gain=expert_col[:, 0:1], norm_shift=expert_col[:, 1:2],
                           prefetch=lambda pool: gather_positions(pool, range(16, 32)),
                           handed_over=(l1_gates, l1_slots))
        if STOP >= 5:
            mlstm(nc, g, a, (l1_out, l1_gates, l1_slots), arena, pe_rows, pe_rows_ready, gate_w, gate_row[:, 0, :], gate_row[:, 1:9, :].rearrange("p a b -> p (a b)"),
                  gate_row[:, 9:17, :].rearrange("p a b -> p (a b)"))
        early.close()
        if STOP >= 6:
            top2_experts(nc, "l2f", g, routers[:, 16:24], l2w, ffn_loaded["L2"])
        if STOP >= 7:
            attention(nc, "l3a", g, (w["L3_q"], None, w["L3_k"], None, w["L3_v"], w["L3_o"]),
                      att_col[:, 12:16], att_col[:, 18:19], r["L3_o"], rope=False)
        if STOP >= 8:
            grouped_experts(nc, "l3f", g, routers[:, 24:40], l3w, ffn_loaded["L3"], expert_col[:, 2:18])

        with nc.Block() as block:
            @block.sync
            def _(sp):
                sp.dma_start(out, x[:]).then_inc(stored, 16)
                sp.wait_ge(stored, 16)


def kernel(**inputs):
    import concourse.bacc as bacc
    from concourse.bass_utils import run_bass_kernel_spmd

    def two_halves(v):
        return np.concatenate([v.reshape(G, S).T] * 2, 0)

    v = {k: np.asarray(w) for k, w in inputs.items()}
    turn = (np.arange(D) // DH) * DH + (np.arange(D) + DH // 2) % DH
    att = {"L0_q": v["L0_xattn_q_w"].T, "L0_q_turned": v["L0_xattn_q_w"][turn].T,
           "L0_k": v["L0_xattn_k_w"].T, "L0_k_turned": v["L0_xattn_k_w"][turn].T,
           "L0_v": v["L0_xattn_v_w"].T, "L0_o": v["L0_xattn_o_w"].T,
           "L1_q": v["L1_xattn_w_q"].T, "L1_k": v["L1_xattn_w_k"].T, "L1_v": v["L1_xattn_w_v"].T,
           "L1_o": v["L1_xattn_w_o"].T, "L3_q": v["L3_xattn_Wq"], "L3_k": v["L3_xattn_Wk"],
           "L3_v": v["L3_xattn_Wv"], "L3_o": v["L3_xattn_Wo"]}
    arrays = {
        "consts": CONSTS,
        "x": v["x"].reshape(NT, P, D).transpose(1, 0, 2),
        "ctxT": v["ctx_1024"].reshape(NT * P, D).T,
        "att_w": np.stack([att[n] for n in ATT], 1),
        "att_col": np.concatenate([two_halves(w) for w in (
            v["L0_xattn_q_b"], v["L0_xattn_q_b"][turn], v["L0_xattn_k_b"], v["L0_xattn_k_b"][turn],
            v["L1_xattn_b_q"], v["L1_xattn_b_k"], v["L3_xattn_bq"], v["L3_xattn_bk"])]
            + [v[n][:, None] for n in ("L0_xattn_v_b", "L1_xattn_b_v", "L3_xattn_bv")], 1),
        "rows": np.stack([v["L0_xattn_o_b"], v["L1_xattn_b_o"], v["L3_xattn_bo"]])[None],
    }

    def wide(w):
        return w.transpose(1, 0, 2).reshape(w.shape[1], -1)

    def tall(w):
        e, f, d = w.shape
        return w.reshape(e, f // P, P, d).transpose(2, 0, 1, 3).reshape(P, -1)

    arrays["L0_experts"] = np.concatenate([wide(v["L0_ffn_W1"]), tall(v["L0_ffn_W2"])], 1)
    arrays["L1_experts"] = np.concatenate([wide(v["L1_ffn_W12"].transpose(0, 2, 1)),
                                           tall(v["L1_ffn_W3"].transpose(0, 2, 1))], 1)
    arrays["L2_experts"] = np.concatenate([wide(v["L2_ffn_w1"]), wide(v["L2_ffn_w3"]), tall(v["L2_ffn_w2"])], 1)
    arrays["L3_experts"] = np.concatenate([
        wide(v["L3_ffn_gate_w"]), v["L3_ffn_shared_gate_w"].T, wide(v["L3_ffn_up_w"]), v["L3_ffn_shared_up_w"].T,
        tall(v["L3_ffn_down_w"].reshape(1, 512, D)), tall(v["L3_ffn_shared_down_w"].T[None])], 1)
    arrays["routers"] = np.concatenate([v["L0_ffn_Wr"], v["L1_ffn_Wr"].T, v["L2_ffn_w_gate"],
                                        v["L3_ffn_router_w"].T], 1)
    arrays["ctx_one"] = np.concatenate([v["ctx_1024"].reshape(NT, P, 8, 16), np.ones((NT, P, 8, 1), np.float32)],
                                       3).transpose(1, 0, 2, 3).reshape(P, NT, 8 * 17)
    arrays["rpe"] = v["L2_xattn_rpe"]
    arrays["hops"] = v["itok_SxS2_0_2016"].reshape(32, P).T
    arrays["gate_w"] = np.concatenate([v["L2_xattn_igate_w"], v["L2_xattn_fgate_w"]]).reshape(16, 3, P).transpose(2, 1, 0)
    arrays["gate_row"] = np.broadcast_to(np.concatenate([
        v["L2_xattn_igate_b"], v["L2_xattn_fgate_b"], v["L2_xattn_ln_w"], v["L2_xattn_ln_b"]]
        ).reshape(17, 16), (P, 17, 16))
    arrays["expert_col"] = np.concatenate([
        v["L1_ffn_ln_gamma"][:, None], v["L1_ffn_ln_beta"][:, None],
        np.broadcast_to(v["L3_ffn_correction_bias"], (P, 16))], 1)
    nc = bacc.Bacc("TRN2", target_bir_lowering=False, num_devices=1)
    dram = {}
    for name, arr in list(arrays.items()):
        arrays[f"in_{name}"] = arr = np.ascontiguousarray(arrays.pop(name))
        dram[name] = nc.dram_tensor(f"in_{name}", arr.shape, mybir.dt.from_np(arr.dtype), kind="ExternalInput").ap()
    out = nc.dram_tensor("out", (P, NT, D), F32, kind="ExternalOutput").ap()
    build(nc, dram, out)
    result = run_bass_kernel_spmd(nc, [arrays], core_ids=[0]).results[0]["out"]
    return np.ascontiguousarray(result.transpose(1, 0, 2)).reshape(2 * NT, S, D)
```
